# Optimizing a Trainium2 kernel written in Bass

```python
import numpy as np
import jax
import jax.numpy as jnp

def _softmax(x, axis=-1):
    return jax.nn.softmax(x, axis=axis)

def _gelu(x):
    return jax.nn.gelu(x, approximate=True)

def _silu(x):
    return jax.nn.silu(x)

def _sigmoid(x):
    return jax.nn.sigmoid(x)

def _layernorm(x, axis=-1, eps=1e-05):
    m = jnp.mean(x, axis=axis, keepdims=True)
    v = jnp.var(x, axis=axis, keepdims=True)
    return (x - m) / jnp.sqrt(v + eps)

def _scatter_add(tgt, idx, src, axis=0):
    return tgt.at[idx].add(src)

def _segment_sum(src, seg, n):
    return jax.ops.segment_sum(src, seg, n)
kernel_name = 'mk_gnn_resnorm_d1_gnn_r8_331a59'

def setup_inputs(seed: int=0):
    np.random.seed(seed)
    _w = jnp.asarray

    def _rec_inputs():
        import jax
        import jax.numpy as jnp
        _gk = jax.random.key(seed)
        x = -0.0002949 + 1 * jax.random.normal(jax.random.fold_in(_gk, 1), (1250, 512), jnp.float32)
        src = jax.random.randint(jax.random.fold_in(_gk, 2), (40000,), 0, 1250, jnp.int32)
        dst = jax.random.randint(jax.random.fold_in(_gk, 3), (40000,), 0, 1250, jnp.int32)
        _o = jnp.argsort(dst, stable=True)
        src = src[_o]
        dst = dst[_o]
        node_vec1 = jax.random.uniform(jax.random.fold_in(_gk, 12), (1250, 1), jnp.float32, 0.0, 0.999957)
        return (x, src, dst, node_vec1)
    x, src, dst, node_vec1 = _rec_inputs()

    def _L0_gnn_setup():
        import jax, jax.numpy as jnp
        import numpy as np
        N_NODES = 40962
        LATENT_DIM = 512
        N_EDGES = 81924
        NUM_BLOCKS = 4
        NUM_HEADS = 4
        NUM_FREQ = 32
        BASE_PERIOD = 16
        NOISE_EMB_DIM = 16
        EPS = 1e-05

        def _cond_layer_norm(x, cond, sw, sb, bw, bb):
            mu = jnp.mean(x, axis=-1, keepdims=True)
            var = jnp.var(x, axis=-1, keepdims=True)
            xn = (x - mu) * jax.lax.rsqrt(var + EPS)
            scale = cond @ sw + sb
            bias = cond @ bw + bb
            return xn * (1.0 + scale) + bias

        def _sparse_attention(x, src, dst, wq, bq, wk, bk, wv, bv, wo, bo):
            N, D = x.shape
            H, Dh = (NUM_HEADS, D // NUM_HEADS)
            q = (x @ wq + bq).reshape(N, H, Dh) * Dh ** (-0.5)
            k = (x @ wk + bk).reshape(N, H, Dh)
            v = (x @ wv + bv).reshape(N, H, Dh)
            scores = jnp.einsum('ehd,ehd->eh', q[src], k[dst])
            smax = jax.ops.segment_max(scores, src, num_segments=N)
            ex = jnp.exp(scores - smax[src])
            denom = jax.ops.segment_sum(ex, src, num_segments=N)
            attn = ex / denom[src]
            out = jax.ops.segment_sum(attn[:, :, None] * v[dst], src, num_segments=N)
            return out.reshape(N, D) @ wo + bo

        def _forward(x, edge_index, noise_levels, f_w1, f_b1, f_w2, f_b2, s1_w, s1_b, b1_w, b1_b, wq, bq, wk, bk, wv, bv, wo, bo, s2_w, s2_b, b2_w, b2_b, m_w1, m_b1, m_w2, m_b2):
            src, dst = (edge_index[0], edge_index[1])
            freqs = jnp.arange(1, NUM_FREQ + 1, dtype=x.dtype) * (2.0 * np.pi / BASE_PERIOD)
            ph = noise_levels * freqs
            emb = jnp.concatenate([jnp.sin(ph), jnp.cos(ph)], axis=-1)
            cond = jax.nn.silu(emb @ f_w1 + f_b1) @ f_w2 + f_b2
            for i in range(NUM_BLOCKS):
                y = _cond_layer_norm(x, cond, s1_w[i], s1_b[i], b1_w[i], b1_b[i])
                y = _sparse_attention(y, src, dst, wq[i], bq[i], wk[i], bk[i], wv[i], bv[i], wo[i], bo[i])
                x = x + y
                y = _cond_layer_norm(x, cond, s2_w[i], s2_b[i], b2_w[i], b2_b[i])
                y = jax.nn.relu(y @ m_w1[i] + m_b1[i]) @ m_w2[i] + m_b2[i]
                x = x + y
            return x
        key = jax.random.key(seed)
        ks = jax.random.split(key, 20)

        def w(k, shape, s=0.02):
            return jax.random.normal(k, shape, dtype=jnp.float32) * s
        D, B, C = (LATENT_DIM, NUM_BLOCKS, NOISE_EMB_DIM)
        z = lambda *s: jnp.zeros(s, jnp.float32)
        return {'latent_mesh_nodes': jax.random.normal(ks[0], (N_NODES, D), dtype=jnp.float32), 'edge_index': jax.random.randint(ks[1], (2, N_EDGES), 0, N_NODES, dtype=jnp.int32), 'noise_levels': jax.random.uniform(ks[2], (N_NODES, 1), dtype=jnp.float32), 'f_w1': w(ks[3], (2 * NUM_FREQ, C)), 'f_b1': z(C), 'f_w2': w(ks[4], (C, C)), 'f_b2': z(C), 's1_w': w(ks[5], (B, C, D)), 's1_b': z(B, D), 'b1_w': w(ks[6], (B, C, D)), 'b1_b': z(B, D), 'wq': w(ks[7], (B, D, D)), 'bq': z(B, D), 'wk': w(ks[8], (B, D, D)), 'bk': z(B, D), 'wv': w(ks[9], (B, D, D)), 'bv': z(B, D), 'wo': w(ks[10], (B, D, D)), 'bo': z(B, D), 's2_w': w(ks[11], (B, C, D)), 's2_b': z(B, D), 'b2_w': w(ks[12], (B, C, D)), 'b2_b': z(B, D), 'm_w1': w(ks[13], (B, D, D)), 'm_b1': z(B, D), 'm_w2': w(ks[14], (B, D, D)), 'm_b2': z(B, D)}
    _L0_gnn_all = _L0_gnn_setup()
    _L0_gnn_in = {k: v for k, v in _L0_gnn_all.items() if k in ('f_w1', 'f_b1', 'f_w2', 'f_b2', 's1_w', 's1_b', 'b1_w', 'b1_b', 'wq', 'bq', 'wk', 'bk', 'wv', 'bv', 'wo', 'bo', 's2_w', 's2_b', 'b2_w', 'b2_b', 'm_w1', 'm_b1', 'm_w2', 'm_b2')}
    del _L0_gnn_all
    return {'x': x, 'src': src, 'dst': dst, 'node_vec1': node_vec1, 'L0_gnn_f_w1': _L0_gnn_in['f_w1'], 'L0_gnn_f_b1': _L0_gnn_in['f_b1'], 'L0_gnn_f_w2': _L0_gnn_in['f_w2'], 'L0_gnn_f_b2': _L0_gnn_in['f_b2'], 'L0_gnn_s1_w': _L0_gnn_in['s1_w'], 'L0_gnn_s1_b': _L0_gnn_in['s1_b'], 'L0_gnn_b1_w': _L0_gnn_in['b1_w'], 'L0_gnn_b1_b': _L0_gnn_in['b1_b'], 'L0_gnn_wq': _L0_gnn_in['wq'], 'L0_gnn_bq': _L0_gnn_in['bq'], 'L0_gnn_wk': _L0_gnn_in['wk'], 'L0_gnn_bk': _L0_gnn_in['bk'], 'L0_gnn_wv': _L0_gnn_in['wv'], 'L0_gnn_bv': _L0_gnn_in['bv'], 'L0_gnn_wo': _L0_gnn_in['wo'], 'L0_gnn_bo': _L0_gnn_in['bo'], 'L0_gnn_s2_w': _L0_gnn_in['s2_w'], 'L0_gnn_s2_b': _L0_gnn_in['s2_b'], 'L0_gnn_b2_w': _L0_gnn_in['b2_w'], 'L0_gnn_b2_b': _L0_gnn_in['b2_b'], 'L0_gnn_m_w1': _L0_gnn_in['m_w1'], 'L0_gnn_m_b1': _L0_gnn_in['m_b1'], 'L0_gnn_m_w2': _L0_gnn_in['m_w2'], 'L0_gnn_m_b2': _L0_gnn_in['m_b2']}

def reference(x, src, dst, node_vec1, L0_gnn_f_w1, L0_gnn_f_b1, L0_gnn_f_w2, L0_gnn_f_b2, L0_gnn_s1_w, L0_gnn_s1_b, L0_gnn_b1_w, L0_gnn_b1_b, L0_gnn_wq, L0_gnn_bq, L0_gnn_wk, L0_gnn_bk, L0_gnn_wv, L0_gnn_bv, L0_gnn_wo, L0_gnn_bo, L0_gnn_s2_w, L0_gnn_s2_b, L0_gnn_b2_w, L0_gnn_b2_b, L0_gnn_m_w1, L0_gnn_m_b1, L0_gnn_m_w2, L0_gnn_m_b2):
    import jax
    import jax.numpy as jnp

    def _L0_gnn_ref(latent_mesh_nodes, edge_index, noise_levels, f_w1, f_b1, f_w2, f_b2, s1_w, s1_b, b1_w, b1_b, wq, bq, wk, bk, wv, bv, wo, bo, s2_w, s2_b, b2_w, b2_b, m_w1, m_b1, m_w2, m_b2):
        import jax, jax.numpy as jnp
        import numpy as np
        N_NODES = 40962
        LATENT_DIM = 512
        N_EDGES = 81924
        NUM_BLOCKS = 4
        NUM_HEADS = 4
        NUM_FREQ = 32
        BASE_PERIOD = 16
        NOISE_EMB_DIM = 16
        EPS = 1e-05

        def _cond_layer_norm(x, cond, sw, sb, bw, bb):
            mu = jnp.mean(x, axis=-1, keepdims=True)
            var = jnp.var(x, axis=-1, keepdims=True)
            xn = (x - mu) * jax.lax.rsqrt(var + EPS)
            scale = cond @ sw + sb
            bias = cond @ bw + bb
            return xn * (1.0 + scale) + bias

        def _sparse_attention(x, src, dst, wq, bq, wk, bk, wv, bv, wo, bo):
            N, D = x.shape
            H, Dh = (NUM_HEADS, D // NUM_HEADS)
            q = (x @ wq + bq).reshape(N, H, Dh) * Dh ** (-0.5)
            k = (x @ wk + bk).reshape(N, H, Dh)
            v = (x @ wv + bv).reshape(N, H, Dh)
            scores = jnp.einsum('ehd,ehd->eh', q[src], k[dst])
            smax = jax.ops.segment_max(scores, src, num_segments=N)
            ex = jnp.exp(scores - smax[src])
            denom = jax.ops.segment_sum(ex, src, num_segments=N)
            attn = ex / denom[src]
            out = jax.ops.segment_sum(attn[:, :, None] * v[dst], src, num_segments=N)
            return out.reshape(N, D) @ wo + bo

        def _forward(x, edge_index, noise_levels, f_w1, f_b1, f_w2, f_b2, s1_w, s1_b, b1_w, b1_b, wq, bq, wk, bk, wv, bv, wo, bo, s2_w, s2_b, b2_w, b2_b, m_w1, m_b1, m_w2, m_b2):
            src, dst = (edge_index[0], edge_index[1])
            freqs = jnp.arange(1, NUM_FREQ + 1, dtype=x.dtype) * (2.0 * np.pi / BASE_PERIOD)
            ph = noise_levels * freqs
            emb = jnp.concatenate([jnp.sin(ph), jnp.cos(ph)], axis=-1)
            cond = jax.nn.silu(emb @ f_w1 + f_b1) @ f_w2 + f_b2
            for i in range(NUM_BLOCKS):
                y = _cond_layer_norm(x, cond, s1_w[i], s1_b[i], b1_w[i], b1_b[i])
                y = _sparse_attention(y, src, dst, wq[i], bq[i], wk[i], bk[i], wv[i], bv[i], wo[i], bo[i])
                x = x + y
                y = _cond_layer_norm(x, cond, s2_w[i], s2_b[i], b2_w[i], b2_b[i])
                y = jax.nn.relu(y @ m_w1[i] + m_b1[i]) @ m_w2[i] + m_b2[i]
                x = x + y
            return x
        return _forward(latent_mesh_nodes, edge_index, noise_levels, f_w1, f_b1, f_w2, f_b2, s1_w, s1_b, b1_w, b1_b, wq, bq, wk, bk, wv, bv, wo, bo, s2_w, s2_b, b2_w, b2_b, m_w1, m_b1, m_w2, m_b2)
    edge_index = jnp.stack([src, dst])
    x = _layernorm(x + _L0_gnn_ref(x, edge_index, node_vec1, L0_gnn_f_w1, L0_gnn_f_b1, L0_gnn_f_w2, L0_gnn_f_b2, L0_gnn_s1_w, L0_gnn_s1_b, L0_gnn_b1_w, L0_gnn_b1_b, L0_gnn_wq, L0_gnn_bq, L0_gnn_wk, L0_gnn_bk, L0_gnn_wv, L0_gnn_bv, L0_gnn_wo, L0_gnn_bo, L0_gnn_s2_w, L0_gnn_s2_b, L0_gnn_b2_w, L0_gnn_b2_b, L0_gnn_m_w1, L0_gnn_m_b1, L0_gnn_m_w2, L0_gnn_m_b2), axis=-1)
    return x

_drawn_inputs = setup_inputs


def setup_inputs(seed=0):
    import zlib

    import numpy as np

    out = dict(_drawn_inputs(seed))
    spreads = {'L0_gnn_f_b1': (0.0, 0.8),
     'L0_gnn_f_b2': (0.0, 0.8),
     'L0_gnn_s1_b': (0.0, 0.8),
     'L0_gnn_b1_b': (0.0, 0.389),
     'L0_gnn_bq': (0.0, 0.8),
     'L0_gnn_bk': (0.0, 0.8),
     'L0_gnn_bv': (0.0, 0.1),
     'L0_gnn_bo': (0.0, 0.1),
     'L0_gnn_s2_b': (0.0, 0.57),
     'L0_gnn_b2_b': (0.0, 0.565),
     'L0_gnn_m_b1': (0.0, 0.1),
     'L0_gnn_m_b2': (0.0, 0.1)}
    factors = {'node_vec1': 8.0,
     'L0_gnn_f_w1': 8.0,
     'L0_gnn_f_w2': 8.0,
     'L0_gnn_s1_w': 8.0,
     'L0_gnn_b1_w': 8.0,
     'L0_gnn_wq': 7.493,
     'L0_gnn_wk': 7.297,
     'L0_gnn_s2_w': 8.0,
     'L0_gnn_b2_w': 8.0}
    for name, (base, spread) in spreads.items():
        noise = np.random.default_rng([zlib.crc32(name.encode()), seed]).standard_normal(out[name].shape)
        drawn = base * np.exp(spread * noise) if base else spread * noise
        out[name] = jnp.asarray(drawn.astype(out[name].dtype))
    for name, factor in factors.items():
        out[name] = (out[name] * factor).astype(out[name].dtype)
    return out
```

```python
from contextlib import ExitStack

import concourse.bass as bass
from concourse import mybir

F32 = mybir.dt.float32
F32R = mybir.dt.float32r
F16 = mybir.dt.float16
BF16 = mybir.dt.bfloat16
I32 = mybir.dt.int32
ALU = mybir.AluOpType
ACT = mybir.ActivationFunctionType
AX_X = mybir.AxisListType.X

NODES = 1250
DIM = 512
EDGES = 40000
BLOCKS = 4
HEADS = 4
FREQS = 32
CONDS = 16
EPS = 1e-5
TILE = 125
TILES = NODES // TILE
PAIR = 2 * TILE
GROUPS = NODES // PAIR
KC = DIM // 128
HALF = 125
EPAIRS = EDGES // (2 * HALF)
EPART = EPAIRS // 2
MATS = 6
NEXT = 4
STACK = 96
BANK = 512
COLS = [(0, 512), (512, 1024), (1024, NODES)]
QSCALE = float(DIM // HEADS) ** -0.5
BIG = 1e30
TWO_PI = 6.283185307179586
PI_HI = 6.28125
PI_MID = 0.0019350051879882812
PI_LO = TWO_PI - PI_HI - PI_MID
ROUND = 12582912.0
SIN_MAX = 3.1415925
START = 1
PSLOTS = 4
TSLOTS = 4
DPAIRS = TILES // 2


def split_products(h, l, h2, l2):
    return [(h, h2), (h, l2), (l, h2)]


def gnn_kernel(nc, x, src, dst, node_vec, weights, stacks, bias_cols, f_w1, f_b1, f_w2, f_b2, consts, iota_row, out):
    ctx = ExitStack()
    with ctx:
        top = [1152]

        def at(name, shape, dt, offset=None):
            size = (2 if dt in (F16, BF16) else 4)
            for n in shape[1:]:
                size *= n
            size = (size + 31) // 32 * 32
            if offset is None:
                offset, top[0] = top[0], top[0] + size
            return nc.alloc_sbuf_tensor_at(name, shape, dt, offset=offset)

        def sem(name):
            return ctx.enter_context(nc.semaphore(name))

        x_sb = at("x_sb", [TILE, TILES, DIM], F32)
        cond_stack = at("cond_stack", [STACK, NODES], F32R)
        q_raw = at("q_raw", [128, HEADS, NODES], F32)
        ident = at("ident", [128, 128], F32)
        bcol = at("bcol", [128, 3, BLOCKS, KC], F32)
        bq_scaled = at("bq_scaled", [128, BLOCKS, KC], F32)
        cond_group = at("cond_group", [STACK, PAIR], F32R)
        ones_stack = at("ones_stack", [64, TILE], F32R)
        stats = at("stats", [TILE, 2, 6], F32)
        mean_var = at("mean_var", [TILE, 2, 2], F32)
        var_eps = at("var_eps", [TILE, 2], F32)
        rstd = at("rstd", [TILE, 2], F32)
        minus_half = at("minus_half", [TILE, 2], F32)
        row_max = at("row_max", [TILE, 8], F32)
        neg_max = at("neg_max", [TILE, 8], F32)
        den = at("den", [TILE, 8], F32)
        den_safe = at("den_safe", [TILE, 8], F32)
        rden = at("rden", [TILE, 8], F32)
        diag = at("diag", [TILE, 2, TILE], F32)
        ones_f = at("ones_f", [TILE, 128], F32)
        rbc = at("rbc", [128, PAIR], F32)
        o_f = at("o_f", [128, PAIR], F32)
        stk_a = at("stk_a", [STACK, 3, DIM], F32R)
        stk_b = at("stk_b", [STACK, DIM], F32R)
        p3 = at("p3", [TILE, NODES], F32)

        kv = top[0]
        k_hi = at("k_hi", [128, HEADS, NODES], F32R)
        k_lo = at("k_lo", [128, HEADS, NODES], F32R)
        v_hi = at("v_hi", [TILE, TILES, DIM], F32R)
        v_lo = at("v_lo", [TILE, TILES, DIM], F32R)
        kv_end = top[0]
        x0_sb = at("x0_sb", [TILE, TILES, DIM], F32, kv_end - 4 * TILES * DIM)
        m_hi = at("m_hi", [128, 2, KC, DIM], F32R, kv)
        m_lo = at("m_lo", [128, 2, KC, DIM], F32R, kv + 16384)
        stage = [at(f"stage{i}", [128, KC, DIM], F32, kv + 32768 + 8192 * i) for i in range(2)]
        h_raw = at("h_raw", [128, KC, PAIR], F32, kv + 49152)
        h_hi = at("h_hi", [128, KC, PAIR], F32R, kv + 53152)
        h_lo = at("h_lo", [128, KC, PAIR], F32R, kv + 57152)
        stk_c = at("stk_c", [STACK, 3, DIM], F32R, kv + 61152)

        wh_at = top[0]
        w_hi = at("w_hi", [128, NEXT, KC, DIM], F32R)
        wl_at = top[0]
        w_lo = at("w_lo", [128, NEXT, KC, DIM], F32R)
        pt = at("pt", [TILE, TSLOTS, 2, 2, PAIR], F32R, wh_at)
        probs = [at("p0", [TILE, NODES], F32, wh_at + 16000),
                 at("p1", [TILE, NODES], F32, wl_at), at("p2", [TILE, NODES], F32, wl_at + 5024), p3]
        lnc_sb = at("lnc_sb", [TILE, 2, NODES], F32, wl_at + 10048)

        y_at = top[0]
        y_hi = at("y_hi", [128, KC, PAIR], F32R)
        y_lo = at("y_lo", [128, KC, PAIR], F32R)
        y_sb = at("y_sb", [TILE, 2, DIM], F32)
        q_hi = at("q_hi", [128, HEADS, PAIR], F32R, y_at)
        q_lo = at("q_lo", [128, HEADS, PAIR], F32R, y_at + 4000)
        o_hi = at("o_hi", [128, HEADS, PAIR], F32R, y_at + 8000)
        o_lo = at("o_lo", [128, HEADS, PAIR], F32R, y_at + 12000)
        assert max(y_at + 16000, top[0]) <= 229344, top[0]

        spare = [kv]

        def setup(name, shape, dt):
            size = 2 if dt in (F16, BF16) else 4
            for n in shape[1:]:
                size *= n
            size = (size + 31) // 32 * 32
            if spare[0] + size > kv + 32768 and spare[0] < kv + 49152:
                spare[0] = kv + 49152
            t = at(name, shape, dt, spare[0])
            spare[0] += size
            assert spare[0] <= kv_end, name
            return t

        onehot_src = setup("onehot_src", [HALF, 2, NODES], BF16)
        onehot_dst = setup("onehot_dst", [HALF, 2, TILE], BF16)
        iota = setup("iota", [HALF, NODES], F16)
        zeros = setup("zeros", [HALF, 512], BF16)
        ct_sb = setup("ct_sb", [TILE, NODES], F32)
        ln_c = setup("ln_c", [TILE, TILES, TILE], F32)
        no_edge = setup("no_edge", [TILE, TILES, TILE], F32)
        lnc_w = setup("lnc_w", [TILE, TILES, TILE], F32)
        edge_int = setup("edge_int", [EPART, 2, 2, 2 * HALF], I32)
        edge_f = setup("edge_f", [EPART, 2, 2, 2 * HALF], F32)
        edge_t = setup("edge_t", [HALF, 2, 2, EPAIRS], F32)
        cst = setup("cst", [128, 512], F32)
        pair_stats = setup("pair_stats", [EPART, 4], F32)
        pair_wide = setup("pair_wide", [EPART, 4, TILES], F32)
        zero10 = setup("zero10", [EPART, TILES], F32)
        win_a = setup("win_a", [TILES, EPAIRS], F32)
        win_rel = setup("win_rel", [TILES, EPAIRS], F32)
        win_first = setup("win_first", [TILES, EPAIRS], F32)
        win_last = setup("win_last", [TILES, EPAIRS], F32)
        win = setup("win", [TILES, 8], F32)
        win_row = setup("win_row", [1, TILES, 2], F32)
        win_scan = setup("win_scan", [1, 3, TILES], F32)
        win_int = setup("win_int", [1, 3, TILES], I32)
        qat = [0]

        def in_q(name, shape, dt):
            size = 4
            for n in shape[1:]:
                size *= n
            t = nc.alloc_sbuf_tensor_at(name, shape, dt, offset=q_off + qat[0])
            qat[0] += (size + 31) // 32 * 32
            assert qat[0] <= 4 * HEADS * NODES, name
            return t

        q_off = 1152 + 4 * TILES * DIM + 5024
        nv = in_q("nv", [TILE, TILES], F32)
        phase = in_q("phase", [TILE, TILES, FREQS], F32)
        turns = in_q("turns", [TILE, TILES, FREQS], F32)
        emb = in_q("emb", [TILE, TILES, 2 * FREQS], F32)
        emb_t = in_q("emb_t", [2 * FREQS, NODES], F32)
        gate_z = in_q("gate_z", [CONDS, NODES], F32)
        cond_f = nc.alloc_sbuf_tensor_at("cond_f", [STACK, NODES], F32, offset=wh_at + 3 * 8192)
        gate_e = nc.alloc_sbuf_tensor_at("gate_e", [CONDS, NODES], F32, offset=y_at)
        gate_r = nc.alloc_sbuf_tensor_at("gate_r", [CONDS, NODES], F32, offset=y_at + 5024)
        small = in_q("small", [128, 2], F32)
        w1_sb = in_q("w1_sb", [2 * FREQS, CONDS], F32)
        w2_sb = in_q("w2_sb", [CONDS, STACK], F32)
        stack_raw = nc.alloc_sbuf_tensor_at("stack_raw", [STACK, BLOCKS, DIM], F32, offset=0 + wh_at)
        stack_r = nc.alloc_sbuf_tensor_at("stack_r", [STACK, BLOCKS, DIM], F32R, offset=8192 + wh_at)

        ps = ctx.enter_context(nc.psum_tensor("ps", [128, 8 * BANK], F32))

        def bank(n, parts=128, cols=BANK, start=0):
            return ps[0:parts, n * BANK + start:n * BANK + start + cols]

        score_at = [0, 3 * BANK]
        T_BANK, O_BANK = 6, 7

        lnc_dram = nc.dram_tensor("lnc_dram", [TILES, TILE, NODES], F32, kind="Internal").ap()
        stk_dram = nc.dram_tensor("stk_dram", [7, BLOCKS, STACK, DIM], F32, kind="Internal").ap()
        win_dram = nc.dram_tensor("win_dram", [TILES, 2], F32, kind="Internal").ap()

        s = {name: sem(name) for name in (
            "consts_in nv_in edges_in w1_in x_in stack_in stack_f stack_split stack_out "
            "phase_done reduced emb_ready emb_ps emb_t_ready z_ps z_ready e_ready e1_ready r_ready "
            "s_ready c_ps c_ready cond_ready bq_ready edge_float edge_ps edge_t_ready pair_stat pair_wide_ready bound_ps "
            "win_step win_out win_row_in scan_step win_ready one_ready zero_ready "
            "ct_ps ct_copied cn_ps ln_ready noedge_ready lnc_ready lnc_out "
            "w_hi_done w_lo_done stk_a_in stk_b_in stk_c_in "
            "cg_ready group_done stat_done mv_done vareps_done rstd_done mod_ps z_done y_done yt_ps yh_done yl_done "
            "qk_ps q_done kh_done kl_done v_ps vh_done vl_done "
            "qh_done ql_done lnc_in s_ps ttr_done negm_done exp_done tp_ps pth_done ptl_done pv_done "
            "densafe_done rden_done diag_done bc_ps bc_done of_done oh_done ol_done wo_ps xb_done "
            "h_ps hraw_done hh_done hl_done m2_ps xc_done "
            "apart x0_in f_sum f_stat f_mv f_var f_rstd f_out stored").split()}
        onehot_ready = [sem(f"onehot_ready{i}") for i in range(2)]
        stage_in = [sem(f"stage{i}_in") for i in range(2)]
        onehot_used = [sem(f"onehot_used{i}") for i in range(2)]
        block = ctx.enter_context(nc.Block())

        freqs = cst[0:TILE, 130:130 + FREQS]
        arange_p = cst[0:TILES, 164:164 + EPAIRS]
        win_lo, win_hi = cst[0:TILES, 128:129], cst[0:TILES, 129:130]
        bias_unit = cst[0:STACK, 162:163]

        def tile_of(buffer, t):
            return buffer[:, bass.ds(t, 1), :].rearrange("p a d -> p (a d)")

        def wait_apart(engine, semaphore, value):
            engine.wait_ge(semaphore, value)
            engine.sem_inc(s["apart"], 1)

        @block.sync
        def _(sp):
            sp.sem_inc(s["lnc_out"], 16 * START)
            sp.dma_start(cst[:], consts).then_inc(s["consts_in"], 16)
            sp.dma_start(iota[:], iota_row).then_inc(s["consts_in"], 16)
            sp.dma_start(nv[:], node_vec).then_inc(s["nv_in"], 16)
            sp.dma_start(edge_int[:, 0], src.rearrange("(q p j) -> p q j", q=2, p=EPART)).then_inc(s["edges_in"], 16)
            sp.dma_start(edge_int[:, 1], dst.rearrange("(q p j) -> p q j", q=2, p=EPART)).then_inc(s["edges_in"], 16)
            sp.dma_start(w1_sb[:], f_w1).then_inc(s["w1_in"], 16)
            sp.dma_start(w2_sb[:], f_w2).then_inc(s["w1_in"], 16)
            sp.dma_start(small[0:CONDS, 0:1], f_b1).then_inc(s["w1_in"], 16)
            sp.dma_start(small[0:STACK, 1:2], f_b2).then_inc(s["w1_in"], 16)
            sp.dma_start(bcol[:].rearrange("p a b c -> p (a b c)"), bias_cols).then_inc(s["w1_in"], 16)
            for kind in range(7):
                if kind:
                    sp.wait_ge(s["stack_split"], 4 * kind)
                for b in range(3):
                    sp.dma_start(stack_raw[32 * b:32 * b + 32, :, :],
                                 stacks[kind].rearrange("b r d -> r b d")).then_inc(s["stack_in"], 16)
                sp.wait_ge(s["stack_split"], 4 * kind + 4)
                sp.dma_start(stk_dram[kind].rearrange("b r d -> r b d"), stack_r[:].bitcast(F32)).then_inc(s["stack_out"], 16)
            sp.dma_start(x_sb[:], x.rearrange("(t p) d -> p t d", p=TILE)).then_inc(s["x_in"], 16)
            sp.wait_ge(s["stack_out"], 16 * 7)
            for n in range(NEXT):
                if n >= 2:
                    sp.wait_ge(s["w_lo_done"], n - 1)
                sp.dma_start(stage[n % 2][:].rearrange("p c d -> p (c d)"), weights[n]).then_inc(stage_in[n % 2], 16)
            sp.wait_ge(s["win_step"], 7)
            sp.dma_start(win_dram, win[:, 4:6]).then_inc(s["win_out"], 16)
            sp.wait_ge(s["win_out"], 16)
            sp.dma_start(win_row[:].rearrange("o t c -> o (t c)"),
                         win_dram.rearrange("t c -> (t c)").rearrange("(o n) -> o n", o=1)).then_inc(s["win_row_in"], 16)
            with sp.Fori(0, TILES) as t:
                sp.wait_ge(s["lnc_ready"], START + t + 1)
                sp.dma_start(lnc_dram[:, :, bass.ds(t * TILE, TILE)].rearrange("a p d -> p a d"),
                             lnc_w[:]).then_inc(s["lnc_out"], 16)
            sp.wait_ge(s["lnc_out"], 16 * START + 16 * TILES)

            def next_weight(blk, n, index):
                load = NEXT + MATS * blk + n
                sp.wait_ge(s["w_lo_done"], load - 1)
                sp.dma_start(stage[n % 2][:].rearrange("p c d -> p (c d)"),
                             weights[bass.ds(index, 1)].rearrange("a p n -> (a p) n")).then_inc(stage_in[n % 2], 16)

            with sp.Fori(0, BLOCKS) as blk:
                sp.wait_ge(s["group_done"], START + 2 * GROUPS * blk)
                sp.dma_start(stk_a[:].bitcast(F32), stk_dram[0:3, bass.ds(blk, 1)].rearrange("k a r d -> (a r) k d")).then_inc(s["stk_a_in"], 16)
                sp.dma_start(stk_b[:].bitcast(F32), stk_dram[3, bass.ds(blk, 1)].rearrange("a r d -> (a r) d")).then_inc(s["stk_b_in"], 16)
                wait_apart(sp, s["group_done"], START + GROUPS * (2 * blk + 1))
                with sp.Fori(0, GROUPS) as g:
                    sp.wait_ge(s["ttr_done"], START + 8 * (blk * GROUPS + g))
                    sp.dma_start(lnc_sb[:], lnc_dram[bass.ds(2 * g, 2)].rearrange("a p d -> p a d")).then_inc(s["lnc_in"], 16)
                sp.wait_ge(s["wo_ps"], START + 2 * GROUPS * (blk + 1))
                sp.dma_start(stk_c[:].bitcast(F32), stk_dram[4:7, bass.ds(blk, 1)].rearrange("k a r d -> (a r) k d")).then_inc(s["stk_c_in"], 16)
                for n in range(MATS):
                    next_weight(blk, n, MATS * blk + NEXT + n)
            sp.wait_ge(s["xc_done"], START + 2 * GROUPS * BLOCKS)
            sp.wait_ge(s["w_lo_done"], NEXT + MATS * BLOCKS)
            sp.dma_start(x0_sb[:], x.rearrange("(t p) d -> p t d", p=TILE)).then_inc(s["x0_in"], 16)
            for t in range(TILES):
                sp.wait_ge(s["f_out"], t + 1)
                sp.dma_start(out[t * TILE:(t + 1) * TILE, :], x_sb[:, t, :]).then_inc(s["stored"], 16)
            sp.wait_ge(s["stored"], 16 * TILES)

        @block.tensor
        def _(pe):
            for name in ("group_done", "yt_ps", "s_ps", "tp_ps", "pv_done", "wo_ps", "bc_ps"):
                pe.sem_inc(s[name], START)
            for half in range(2):
                pe.sem_inc(onehot_used[half], START)
            pe.wait_ge(s["consts_in"], 32)
            idn = cst[:, 384:512]
            pe.wait_ge(s["emb_ready"], 2)
            for t in range(TILES):
                mm = pe.transpose(ps[0:2 * FREQS, BANK * (t // 4) + TILE * (t % 4):BANK * (t // 4) + TILE * (t % 4) + TILE],
                                  emb[:, t, :], idn[0:TILE, 0:TILE])
            mm.then_inc(s["emb_ps"], 1)
            pe.wait_ge(s["w1_in"], 80)
            pe.wait_ge(s["emb_t_ready"], 3)
            for a, b in COLS:
                mm = pe.matmul(ps[0:CONDS, score_at[1] + a:score_at[1] + b], w1_sb[:], emb_t[:, a:b], start=True, stop=True)
            mm.then_inc(s["z_ps"], 1)
            pe.wait_ge(s["s_ready"], 1)
            for a, b in COLS:
                mm = pe.matmul(ps[0:STACK, a:b], w2_sb[:], gate_r[:, a:b], start=True, stop=True)
            mm.then_inc(s["c_ps"], 1)
            pe.wait_ge(s["edge_float"], 2)
            for e in range(2):
                for half in range(2):
                    for q in range(2):
                        at_ = score_at[1] + BANK * e + 2 * EPART * half + EPART * q
                        if e == 0 and half == 0 and q == 0:
                            pe.wait_ge(s["z_ready"], 1)
                        mm = pe.transpose(ps[0:HALF, at_:at_ + EPART],
                                          edge_f[:, e, q, HALF * half:HALF * half + HALF], idn[0:EPART, 0:EPART])
            mm.then_inc(s["edge_ps"], 1)
            pe.wait_ge(s["pair_wide_ready"], 4)
            for c in range(4):
                mm = pe.matmul(bank(T_BANK, TILES, EPART, EPART * c), pair_wide[:, c, :], idn[0:EPART, 0:EPART],
                               start=True, stop=True)
            mm.then_inc(s["bound_ps"], 1)
            pe.wait_ge(s["zero_ready"], 1)
            pe.wait_ge(s["win_ready"], 3)
            pe.wait_ge(s["c_ready"], 1)
            pe.wait_ge(s["edge_t_ready"], 2)
            with pe.Fori(0, TILES) as t:
                length = pe.value_load(win_int[0:1, 1, bass.ds(t, 1)], min_val=1, max_val=EPAIRS)
                base = pe.value_load(win_int[0:1, 2, bass.ds(t, 1)], min_val=0, max_val=EPAIRS * TILES)
                pe.wait_ge(s["ct_copied"], START + t)
                for a, b in COLS:
                    pe.matmul(ps[0:TILE, a:b], zeros[:, 0:TILE], zeros[:, 0:b - a], start=True, stop=False)
                with pe.Fori(0, length) as k:
                    for half in range(2):
                        pe.wait_ge(onehot_ready[half], base + k + 1)
                        for a, b in COLS:
                            mm = pe.matmul(ps[0:TILE, a:b], onehot_dst[:, half, :], onehot_src[:, half, a:b],
                                           start=False, stop=False)
                        mm.then_inc(onehot_used[half], 1)
                for a, b in COLS:
                    mm = pe.matmul(ps[0:TILE, a:b], zeros[:, 0:TILE], zeros[:, 0:b - a], start=False, stop=True)
                mm.then_inc(s["ct_ps"], 1)
                pe.wait_ge(s["ct_copied"], START + t + 1)
                pe.wait_ge(s["noedge_ready"], START + t)
                for i in range(TILES):
                    at_ = score_at[1] + BANK * (i // 4) + TILE * (i % 4)
                    mm = pe.transpose(ps[0:TILE, at_:at_ + TILE], ct_sb[:, TILE * i:TILE * i + TILE], idn[0:TILE, 0:TILE])
                mm.then_inc(s["cn_ps"], 1)

            pe.wait_ge(s["cond_ready"], 2)

            def norm(n, stk):
                pe.wait_ge(s["cg_ready"], n + 1)
                for j in range(2):
                    pe.wait_ge(s["y_done"], START + 2 * n + j)
                    pe.matmul(bank(0, TILE), cond_group[:, TILE * j:TILE * j + TILE], stk[:, 0, :], start=True, stop=True)
                    pe.matmul(bank(1, TILE), cond_group[:, TILE * j:TILE * j + TILE], stk[:, 1, :],
                              start=True, stop=True).then_inc(s["mod_ps"], 1)
                for j in range(2):
                    pe.wait_ge(s["y_done"], START + 2 * n + j + 1)
                    pe.wait_ge(s["yl_done"], START + 2 * n)
                    for c in range(KC):
                        mm = pe.transpose(bank(2 + j, 128, TILE, TILE * c), y_sb[:, j, 128 * c:128 * c + 128], ident[0:TILE, 0:TILE])
                    mm.then_inc(s["yt_ps"], 1)
                pe.wait_ge(s["yh_done"], 2 * n + 2)
                pe.wait_ge(s["yl_done"], START + 2 * n + 2)

            def features(out_bank, col, wh, wl, f):
                steps = [(a[:, c, 128 * f:128 * f + 128], b[:, c, :]) for a, b in split_products(wh, wl, y_hi, y_lo) for c in range(KC)]
                for i, (a, b) in enumerate(steps):
                    mm = pe.matmul(bank(out_bank, 128, PAIR, col), a, b, start=i == 0, stop=i == len(steps) - 1)
                return mm

            def rows(out_bank, h, l, j, wh, wl, bias):
                pe.matmul(bank(out_bank, TILE), ones_stack[:], bias, start=True, stop=False)
                steps = [(a[:, c, TILE * j:TILE * j + TILE], b[:, c, :]) for a, b in split_products(h, l, wh, wl) for c in range(KC)]
                for i, (a, b) in enumerate(steps):
                    mm = pe.matmul(bank(out_bank, TILE), a, b, start=False, stop=i == len(steps) - 1)
                return mm

            with pe.Fori(0, BLOCKS) as blk:
                pe.wait_ge(s["stk_a_in"], 16 * (blk + 1))
                pe.wait_ge(s["w_hi_done"], NEXT + MATS * blk)
                wait_apart(pe, s["w_lo_done"], NEXT + MATS * blk)
                with pe.Fori(0, GROUPS) as g:
                    it = blk * GROUPS + g
                    norm(2 * GROUPS * blk + g, stk_a)
                    pe.wait_ge(s["vl_done"], START + 2 * it)
                    for m in range(2):
                        pe.wait_ge(s["kl_done"], START + 2 * it)
                        for i in range(2):
                            for f in (2 * i, 2 * i + 1):
                                mm = features(4 + 2 * m + i, PAIR * (f % 2), w_hi[:, m], w_lo[:, m], f)
                            mm.then_inc(s["qk_ps"], 1)
                    for j in range(2):
                        pe.wait_ge(s["q_done"], 2 * it + j + 1)
                        mm = rows(4 + j, y_hi, y_lo, j, w_hi[:, 2], w_lo[:, 2], stk_a[0:64, 2, :])
                        mm.then_inc(s["v_ps"], 1)
                    pe.drain().then_inc(s["group_done"], 1)

                for name in ("kh_done", "kl_done", "vh_done", "vl_done"):
                    pe.wait_ge(s[name], (START if name in ("kl_done", "vl_done") else 0) + 2 * GROUPS * (blk + 1))
                wait_apart(pe, s["stk_b_in"], 16 * (blk + 1))
                with pe.Fori(0, GROUPS) as g:
                    it = blk * GROUPS + g
                    pe.wait_ge(s["qh_done"], it + 1)
                    pe.wait_ge(s["ql_done"], it + 1)

                    def scores(h, j, part):
                        if part == 0:
                            pe.wait_ge(s["ttr_done"], START + 8 * it + max(2 * h + j - 1, 0))
                        a, b = split_products(q_hi, q_lo, k_hi, k_lo)[part]
                        for lo, hi in COLS:
                            mm = pe.matmul(ps[0:TILE, score_at[j] + lo:score_at[j] + hi], a[:, h, TILE * j:TILE * j + TILE],
                                           b[:, h, lo:hi], start=part == 0, stop=part == 2)
                        if part == 2:
                            mm.then_inc(s["s_ps"], 1)

                    def turn(h, dp):
                        if dp == 0:
                            pe.wait_ge(s["exp_done"], 8 * it + 2 * h + 2)
                            if h == 0:
                                pe.wait_ge(s["xb_done"], START + 2 * it)
                        pe.wait_ge(s["ptl_done"], START + 5 * HEADS * it + 5 * h + dp)
                        for d in (2 * dp, 2 * dp + 1):
                            for j in range(2):
                                mm = pe.transpose(bank(T_BANK, TILE, TILE, PAIR * (d % 2) + TILE * j),
                                                  probs[(2 * h + j) % PSLOTS][:, TILE * d:TILE * d + TILE], ident[0:TILE, 0:TILE])
                        mm.then_inc(s["tp_ps"], 1)

                    def weigh(h, dp):
                        n = 5 * h + dp
                        if dp == 0:
                            pe.wait_ge(s["of_done"], START + HEADS * it + h)
                        pe.wait_ge(s["ptl_done"], START + 5 * HEADS * it + n + 1)
                        steps = [(a[:, 2 * dp + e, 128 * h:128 * h + 128], pt[:, n % TSLOTS, w, e, :])
                                 for e in range(2) for a, w in ((v_hi, 0), (v_hi, 1), (v_lo, 0))]
                        for i, (a, b) in enumerate(steps):
                            mm = pe.matmul(bank(O_BANK, 128, PAIR), a, b, start=dp == 0 and i == 0,
                                           stop=dp == DPAIRS - 1 and i == len(steps) - 1)
                        mm.then_inc(s["pv_done"], 1)

                    for j in range(2):
                        for part in range(3):
                            scores(0, j, part)
                    for h in range(HEADS):
                        todo = [(h + 1, j, part) for j in range(2) for part in range(3)] if h + 1 < HEADS else []
                        for dp in range(DPAIRS):
                            turn(h, dp)
                            for _ in range((2, 1, 2, 1, 0)[dp]):
                                if todo:
                                    scores(*todo.pop(0))
                            if dp:
                                weigh(h, dp - 1)
                        weigh(h, DPAIRS - 1)
                        pe.wait_ge(s["diag_done"], HEADS * it + h + 1)
                        for j in range(2):
                            mm = pe.matmul(bank(O_BANK, 128, TILE, PAIR + TILE * j), ones_f[:], diag[:, j, :], start=True, stop=True)
                        mm.then_inc(s["bc_ps"], 1)
                    pe.wait_ge(s["oh_done"], HEADS * (it + 1))
                    pe.wait_ge(s["ol_done"], START + HEADS * (it + 1))
                    pe.wait_ge(s["ptl_done"], START + 5 * HEADS * (it + 1))
                    for j in range(2):
                        mm = rows(T_BANK + j, o_hi, o_lo, j, w_hi[:, 3], w_lo[:, 3], stk_b[0:64, :])
                        mm.then_inc(s["wo_ps"], 1)

                wait_apart(pe, s["stk_c_in"], 16 * (blk + 1))
                with pe.Fori(0, GROUPS) as g:
                    it = blk * GROUPS + g
                    norm(2 * GROUPS * blk + GROUPS + g, stk_c)
                    pe.wait_ge(s["w_hi_done"], NEXT + MATS * blk + 2)
                    pe.wait_ge(s["w_lo_done"], NEXT + MATS * blk + 2)
                    pe.wait_ge(s["hraw_done"], START + 2 * it)
                    for i in range(2):
                        for f in (2 * i, 2 * i + 1):
                            mm = features(4 + i, PAIR * (f % 2), m_hi[:, 0], m_lo[:, 0], f)
                        mm.then_inc(s["h_ps"], 1)
                    pe.wait_ge(s["hh_done"], it + 1)
                    pe.wait_ge(s["hl_done"], START + it + 1)
                    pe.wait_ge(s["xb_done"], START + 2 * GROUPS * (blk + 1))
                    for j in range(2):
                        pe.wait_ge(s["xc_done"], START + 2 * it)
                        mm = rows(6 + j, h_hi, h_lo, j, m_hi[:, 1], m_lo[:, 1], stk_c[0:64, 2, :])
                        mm.then_inc(s["m2_ps"], 1)
                    pe.drain().then_inc(s["group_done"], 1)

        @block.vector
        def _(dve):
            for name in ("y_done", "yl_done", "vl_done", "kl_done", "ttr_done", "xb_done", "ptl_done", "of_done", "xc_done", "rden_done"):
                dve.sem_inc(s[name], START)
            dve.wait_ge(s["consts_in"], 32)
            dve.tensor_copy(ident[:], cst[:, 384:512]).then_inc(s["one_ready"], 1)
            dve.memset(ones_f[:], 1.0).then_inc(s["one_ready"], 1)
            dve.memset(zeros[:], 0.0).then_inc(s["zero_ready"], 1)
            dve.memset(zero10[:], 0.0).then_inc(s["one_ready"], 1)
            dve.memset(minus_half[:], -0.5).then_inc(s["one_ready"], 1)
            dve.wait_ge(s["one_ready"], 4)
            dve.tensor_scalar(ones_stack[:], ones_f[0:64, 0:TILE], 1.0, None, ALU.mult).then_inc(s["one_ready"], 1)
            dve.wait_ge(s["nv_in"], 16)
            for t in range(TILES):
                mm = dve.tensor_scalar(phase[:, t, :], freqs, nv[:, t:t + 1], None, ALU.mult)
            mm.then_inc(s["phase_done"], 1)
            step = 0
            dve.wait_ge(s["phase_done"], 1)
            for shift in range(2):
                part = emb[:, :, FREQS * shift:FREQS * shift + FREQS]

                def then(instruction):
                    nonlocal step
                    step += 1
                    instruction.then_inc(s["reduced"], 1)
                    dve.wait_ge(s["reduced"], step)

                then(dve.tensor_scalar(turns[:], phase[:], 1.0 / TWO_PI, 0.25 * shift, ALU.mult, ALU.add))
                then(dve.tensor_scalar(turns[:], turns[:], ROUND, None, ALU.add))
                then(dve.tensor_scalar(turns[:], turns[:], -ROUND, None, ALU.add))
                then(dve.scalar_tensor_tensor(out=part, in0=turns[:], scalar=-PI_HI, in1=phase[:], op0=ALU.mult, op1=ALU.add))
                then(dve.scalar_tensor_tensor(out=part, in0=turns[:], scalar=-PI_MID, in1=part, op0=ALU.mult, op1=ALU.add))
                then(dve.scalar_tensor_tensor(out=part, in0=turns[:], scalar=-PI_LO, in1=part, op0=ALU.mult, op1=ALU.add))
                if shift:
                    then(dve.tensor_scalar(part, part, TWO_PI / 4, None, ALU.add))
                then(dve.tensor_scalar(part, part, SIN_MAX, -SIN_MAX, ALU.min, ALU.max))
                
            for kind in range(7):
                unit = kind in (0, 4)
                dve.wait_ge(s["stack_in"], 48 * (kind + 1))
                if kind:
                    dve.wait_ge(s["stack_out"], 16 * kind)
                if unit:
                    dve.tensor_scalar(stack_raw[:], stack_raw[:], bias_unit, None, ALU.add).then_inc(s["stack_f"], 1)
                    dve.wait_ge(s["stack_f"], (0, 4).index(kind) + 1)
                dve.tensor_copy(stack_r[:], stack_raw[:]).then_inc(s["stack_split"], 1)
                dve.wait_ge(s["stack_split"], 4 * kind + 1)
                dve.tensor_tensor(stack_r[32:64], stack_raw[32:64], stack_r[32:64].bitcast(F32), ALU.subtract).then_inc(s["stack_split"], 3)
            dve.wait_ge(s["z_ps"], 1)
            dve.wait_ge(s["w1_in"], 80)
            dve.tensor_scalar(gate_z[:], ps[0:CONDS, score_at[1]:score_at[1] + NODES], small[0:CONDS, 0:1], None, ALU.add).then_inc(s["z_ready"], 1)
            dve.wait_ge(s["e_ready"], 1)
            dve.tensor_scalar(gate_e[:], gate_e[:], 1.0, None, ALU.add).then_inc(s["e1_ready"], 1)
            dve.wait_ge(s["e1_ready"], 1)
            dve.reciprocal(gate_r[:], gate_e[:]).then_inc(s["r_ready"], 1)
            dve.wait_ge(s["r_ready"], 1)
            dve.tensor_tensor(gate_r[:], gate_r[:], gate_z[:], ALU.mult).then_inc(s["s_ready"], 1)
            dve.wait_ge(s["c_ps"], 1)
            dve.tensor_scalar(cond_f[:], ps[0:STACK, 0:NODES], small[0:STACK, 1:2], None, ALU.add).then_inc(s["c_ready"], 1)
            dve.wait_ge(s["c_ready"], 1)
            dve.tensor_copy(cond_stack[:], cond_f[:]).then_inc(s["cond_ready"], 1)
            dve.wait_ge(s["cond_ready"], 1)
            dve.tensor_tensor(cond_stack[64:96], cond_f[64:96], cond_stack[64:96].bitcast(F32), ALU.subtract).then_inc(s["cond_ready"], 1)
            dve.tensor_scalar(bq_scaled[:], bcol[:, 0], QSCALE, None, ALU.mult).then_inc(s["bq_ready"], 1)
            dve.wait_ge(s["edges_in"], 32)
            for e in range(2):
                dve.tensor_copy(edge_f[:, e], edge_int[:, e]).then_inc(s["edge_float"], 1)
            dve.wait_ge(s["edge_float"], 2)
            for q in range(2):
                dve.tensor_reduce(pair_stats[:, q:q + 1], edge_f[:, 1, q, :], AX_X, ALU.min).then_inc(s["pair_stat"], 1)
                dve.tensor_reduce(pair_stats[:, 2 + q:3 + q], edge_f[:, 1, q, :], AX_X, ALU.max).then_inc(s["pair_stat"], 1)
            dve.wait_ge(s["pair_stat"], 4)
            for c in range(4):
                dve.tensor_scalar(pair_wide[:, c, :], zero10[:], pair_stats[:, c:c + 1], None, ALU.add).then_inc(s["pair_wide_ready"], 1)
            dve.wait_ge(s["edge_ps"], 1)
            for e in range(2):
                dve.tensor_copy(edge_t[:, e], ps[0:HALF, score_at[1] + BANK * e:score_at[1] + BANK * e + 2 * EPAIRS].rearrange(
                    "p (h n) -> p h n", h=2)).then_inc(s["edge_t_ready"], 1)
            dve.wait_ge(s["bound_ps"], 1)
            least, most = bank(T_BANK, TILES, EPAIRS), bank(T_BANK, TILES, EPAIRS, EPAIRS)
            wstep = 0

            def wthen(instruction):
                nonlocal wstep
                wstep += 1
                instruction.then_inc(s["win_step"], 1)
                dve.wait_ge(s["win_step"], wstep)

            dve.tensor_scalar(win_a[:], least, win_hi, None, ALU.is_le).then_inc(s["scan_step"], 1)
            dve.wait_ge(s["scan_step"], 1)
            wthen(dve.scalar_tensor_tensor(out=win_rel[:], in0=most, scalar=win_lo, in1=win_a[:], op0=ALU.is_ge, op1=ALU.mult))
            dve.scalar_tensor_tensor(out=win_first[:], in0=win_rel[:], scalar=-1000.0, in1=arange_p, op0=ALU.mult, op1=ALU.add).then_inc(s["scan_step"], 1)
            dve.scalar_tensor_tensor(out=win_last[:], in0=arange_p, scalar=-999.0, in1=win_rel[:], op0=ALU.add, op1=ALU.mult).then_inc(s["scan_step"], 1)
            dve.wait_ge(s["scan_step"], 3)
            wthen(dve.tensor_reduce(win[:, 0:1], win_first[:], AX_X, ALU.min))
            wthen(dve.tensor_reduce(win[:, 1:2], win_last[:], AX_X, ALU.max))
            wthen(dve.tensor_scalar(win[:, 4:5], win[:, 0:1], float(EPAIRS - 1), None, ALU.min))
            wthen(dve.tensor_scalar(win[:, 2:3], win[:, 4:5], 1.0, None, ALU.add))
            wthen(dve.tensor_tensor(win[:, 3:4], win[:, 1:2], win[:, 2:3], ALU.max))
            wthen(dve.tensor_tensor(win[:, 5:6], win[:, 3:4], win[:, 4:5], ALU.subtract))
            dve.wait_ge(s["win_row_in"], 16)
            dve.tensor_copy(win_scan[:, 2, :], win_row[:, :, 1]).then_inc(s["scan_step"], 1)
            dve.wait_ge(s["scan_step"], 4)
            dve.tensor_tensor_scan(win_scan[:, 0, :], ones_f[0:1, 0:TILES], win_scan[:, 2, :], 0.0, ALU.mult, ALU.add).then_inc(s["scan_step"], 1)
            dve.wait_ge(s["scan_step"], 5)
            dve.tensor_tensor(win_scan[:, 1, :], win_scan[:, 0, :], win_scan[:, 2, :], ALU.subtract).then_inc(s["scan_step"], 1)
            dve.wait_ge(s["scan_step"], 6)
            dve.tensor_copy(win_int[:, 0, :], win_row[:, :, 0]).then_inc(s["win_ready"], 1)
            dve.tensor_copy(win_int[:, 1, :], win_row[:, :, 1]).then_inc(s["win_ready"], 1)
            dve.tensor_copy(win_int[:, 2, :], win_scan[:, 1, :]).then_inc(s["win_ready"], 1)
            dve.wait_ge(s["win_ready"], 3)
            dve.wait_ge(s["edge_t_ready"], 2)
            with dve.Fori(0, TILES) as t:
                first = dve.value_load(win_int[0:1, 0, bass.ds(t, 1)], min_val=0, max_val=EPAIRS - 1)
                length = dve.value_load(win_int[0:1, 1, bass.ds(t, 1)], min_val=1, max_val=EPAIRS)
                base = dve.value_load(win_int[0:1, 2, bass.ds(t, 1)], min_val=0, max_val=EPAIRS * TILES)
                with dve.Fori(0, length) as k:
                    pair = nc.s_assert_within(first + k, 0, EPAIRS - 1, skip_runtime_bounds_check_because="a window ends at the last pair")
                    for half in range(2):
                        dve.wait_ge(onehot_used[half], START + base + k)
                        dve.tensor_scalar(onehot_dst[:, half, :], iota[:, bass.ds(t * TILE, TILE)],
                                          edge_t[:, 1, half, bass.ds(pair, 1)], None, ALU.is_equal)
                        dve.tensor_scalar(onehot_src[:, half, :], iota[:],
                                          edge_t[:, 0, half, bass.ds(pair, 1)], None, ALU.is_equal).then_inc(onehot_ready[half], 1)

            dve.wait_ge(s["x_in"], 16)
            dve.wait_ge(s["lnc_out"], 16 * START + 16 * TILES)

            def norm(n):
                for j in range(2):
                    t = 2 * group + j
                    dve.bn_stats(stats[:, j, :], tile_of(x_sb, t)).then_inc(s["stat_done"], 1)
                    wait_apart(dve, s["stat_done"], 2 * n + j + 1)
                    dve.bn_aggr(mean_var[:, j, :], stats[:, j, :]).then_inc(s["mv_done"], 1)
                dve.wait_ge(s["mv_done"], 2 * n + 2)
                dve.wait_ge(s["yt_ps"], START + 2 * n)
                for j in range(2):
                    dve.wait_ge(s["mod_ps"], 2 * n + j + 1)
                    dve.scalar_tensor_tensor(out=y_sb[:, j, :], in0=tile_of(x_sb, 2 * group + j), scalar=mean_var[:, j, 0:1],
                                             in1=bank(0, TILE), op0=ALU.subtract, op1=ALU.mult).then_inc(s["z_done"], 1)
                    dve.wait_ge(s["z_done"], 2 * n + j + 1)
                    if j == 0:
                        dve.wait_ge(s["rstd_done"], n + 1)
                    dve.scalar_tensor_tensor(out=y_sb[:, j, :], in0=y_sb[:, j, :], scalar=rstd[:, j:j + 1],
                                             in1=bank(1, TILE), op0=ALU.mult, op1=ALU.add).then_inc(s["y_done"], 1)
                for j in range(2):
                    dve.wait_ge(s["yh_done"], 2 * n + j + 1)
                    part = slice(TILE * j, TILE * j + TILE)
                    dve.tensor_tensor(y_lo[:, :, part], bank(2 + j, 128, 4 * TILE).rearrange("p (c n) -> p c n", c=KC),
                                      y_hi[:, :, part].bitcast(F32), ALU.subtract).then_inc(s["yl_done"], 1)

            with dve.Fori(0, BLOCKS) as blk:
                wait_apart(dve, s["xc_done"], START + 2 * GROUPS * blk)
                with dve.Fori(0, GROUPS) as group:
                    it = blk * GROUPS + group
                    norm(2 * GROUPS * blk + group)
                    for i in range(2):
                        dve.wait_ge(s["kh_done"], 2 * it + i + 1)
                        for f in (2 * i, 2 * i + 1):
                            out_ = k_lo[:, f, bass.ds(group * PAIR, PAIR)]
                            mm = dve.scalar_tensor_tensor(out=out_, in0=bank(6 + i, 128, PAIR, PAIR * (f % 2)),
                                                          scalar=bcol[:, 1, bass.ds(blk, 1), f], in1=k_hi[:, f, bass.ds(group * PAIR, PAIR)].bitcast(F32),
                                                          op0=ALU.add, op1=ALU.subtract)
                        mm.then_inc(s["kl_done"], 1)
                    for j in range(2):
                        dve.wait_ge(s["vh_done"], 2 * it + j + 1)
                        dve.tensor_tensor(tile_of(v_lo, 2 * group + j), bank(4 + j, TILE), tile_of(v_hi, 2 * group + j).bitcast(F32),
                                          ALU.subtract).then_inc(s["vl_done"], 1)
                wait_apart(dve, s["group_done"], START + GROUPS * (2 * blk + 1))
                with dve.Fori(0, GROUPS) as group:
                    it = blk * GROUPS + group
                    dve.wait_ge(s["q_done"], 2 * GROUPS * (blk + 1))
                    dve.wait_ge(s["s_ps"], START + 8 * it)
                    dve.tensor_copy(q_hi[:], q_raw[:, :, bass.ds(group * PAIR, PAIR)]).then_inc(s["qh_done"], 1)

                    def masked_max(h, j):
                        n = 2 * h + j
                        if n == 0:
                            dve.wait_ge(s["lnc_in"], 16 * (it + 1))
                        dve.wait_ge(s["s_ps"], START + 8 * it + n + 1)
                        wait_apart(dve, s["tp_ps"], START + 5 * HEADS * it + max(5 * (h - 1), 0))
                        dve.tensor_tensor_reduce(probs[n % PSLOTS][:], ps[0:TILE, score_at[j]:score_at[j] + NODES], lnc_sb[:, j, :],
                                                 1.0, -BIG / 10, ALU.add, ALU.max, row_max[:, n:n + 1]).then_inc(s["ttr_done"], 1)
                        dve.wait_ge(s["ttr_done"], START + 8 * it + n + 1)
                        dve.tensor_scalar(neg_max[:, n:n + 1], row_max[:, n:n + 1], -1.0, None, ALU.mult).then_inc(s["negm_done"], 1)

                    for j in range(2):
                        masked_max(0, j)
                    for h in range(HEADS):
                        for dp in range(DPAIRS):
                            n = 5 * h + dp
                            if dp == 2:
                                dve.wait_ge(s["exp_done"], 8 * it + 2 * h + 2)
                                dve.tensor_scalar(den_safe[:, 2 * h:2 * h + 2], den[:, 2 * h:2 * h + 2], 1e-30, None, ALU.max).then_inc(s["densafe_done"], 1)
                                dve.wait_ge(s["densafe_done"], HEADS * it + h + 1)
                                dve.reciprocal(rden[:, 2 * h:2 * h + 2], den_safe[:, 2 * h:2 * h + 2]).then_inc(s["rden_done"], 1)
                            dve.wait_ge(s["pth_done"], 5 * HEADS * it + n + 1)
                            dve.tensor_tensor(pt[:, n % TSLOTS, 1], bank(T_BANK, TILE, 2 * PAIR).rearrange("p (e n) -> p e n", e=2),
                                              pt[:, n % TSLOTS, 0].bitcast(F32), ALU.subtract).then_inc(s["ptl_done"], 1)
                            if h + 1 < HEADS and dp == 2:
                                masked_max(h + 1, 0)
                            if h + 1 < HEADS and dp == 4:
                                masked_max(h + 1, 1)
                        dve.wait_ge(s["bc_done"], HEADS * it + h + 1)
                        dve.wait_ge(s["ol_done"], START + HEADS * it + h)
                        dve.tensor_tensor(o_f[:], bank(O_BANK, 128, PAIR), rbc[:], ALU.mult).then_inc(s["of_done"], 1)
                    for j in range(2):
                        dve.wait_ge(s["wo_ps"], START + 2 * it + j + 1)
                        dve.tensor_tensor(tile_of(x_sb, 2 * group + j), bank(T_BANK + j, TILE), tile_of(x_sb, 2 * group + j),
                                          ALU.add).then_inc(s["xb_done"], 1)
                wait_apart(dve, s["xb_done"], START + 2 * GROUPS * (blk + 1))
                with dve.Fori(0, GROUPS) as group:
                    it = blk * GROUPS + group
                    norm(2 * GROUPS * blk + GROUPS + group)
                    dve.wait_ge(s["hraw_done"], START + 2 * it + 2)
                    dve.wait_ge(s["group_done"], START + 2 * GROUPS * blk + GROUPS + group)
                    dve.tensor_copy(h_hi[:], h_raw[:]).then_inc(s["hh_done"], 1)
                    for j in range(2):
                        dve.wait_ge(s["m2_ps"], 2 * it + j + 1)
                        dve.tensor_tensor(tile_of(x_sb, 2 * group + j), bank(6 + j, TILE), tile_of(x_sb, 2 * group + j),
                                          ALU.add).then_inc(s["xc_done"], 1)
            dve.wait_ge(s["x0_in"], 16)
            dve.wait_ge(s["xc_done"], START + 2 * GROUPS * BLOCKS)
            for t in range(TILES):
                dve.tensor_tensor(x_sb[:, t, :], x_sb[:, t, :], x0_sb[:, t, :], ALU.add).then_inc(s["f_sum"], 1)
                dve.wait_ge(s["f_sum"], t + 1)
                dve.bn_stats(stats[:, t % 2, :], x_sb[:, t, :]).then_inc(s["f_stat"], 1)
                dve.wait_ge(s["f_stat"], t + 1)
                dve.bn_aggr(mean_var[:, t % 2, :], stats[:, t % 2, :]).then_inc(s["f_mv"], 1)
                dve.wait_ge(s["f_rstd"], t + 1)
                dve.tensor_scalar(x_sb[:, t, :], x_sb[:, t, :], mean_var[:, t % 2, 0:1], rstd[:, t % 2:t % 2 + 1],
                                  ALU.subtract, ALU.mult).then_inc(s["f_out"], 1)

        @block.scalar
        def _(act):
            for name in ("hraw_done", "ct_copied", "noedge_ready"):
                act.sem_inc(s[name], START)
            for shift in range(2):
                act.wait_ge(s["reduced"], (7, 15)[shift])
                part = emb[:, :, FREQS * shift:FREQS * shift + FREQS]
                act.activation(part, part, ACT.Sin).then_inc(s["emb_ready"], 1)
            act.wait_ge(s["emb_ps"], 1)
            for i, n in enumerate((4, 4, 2)):
                act.activation(emb_t[:, 4 * TILE * i:4 * TILE * i + n * TILE], ps[0:2 * FREQS, BANK * i:BANK * i + n * TILE],
                               ACT.Copy).then_inc(s["emb_t_ready"], 1)
            act.wait_ge(s["z_ready"], 1)
            act.activation(gate_e[:], gate_z[:], ACT.Exp, scale=-1.0).then_inc(s["e_ready"], 1)

            def split_hi(turn, stage_n, dst):
                act.wait_ge(stage_in[stage_n], 16 * (turn + 1))
                act.activation(dst, stage[stage_n][:], ACT.Copy).then_inc(s["w_hi_done"], 1)

            act.wait_ge(s["cond_ready"], 2)
            for n in range(NEXT):
                split_hi(n // 2, n % 2, w_hi[:, n])
            with act.Fori(0, TILES) as t:
                act.wait_ge(s["ct_ps"], t + 1)
                act.activation(ct_sb[:], ps[0:TILE, 0:NODES], ACT.Copy).then_inc(s["ct_copied"], 1)
                act.wait_ge(s["cn_ps"], t + 1)
                act.wait_ge(s["lnc_ready"], START + t)
                for i, n in enumerate((4, 4, 2)):
                    counts = ps[0:TILE, score_at[1] + BANK * i:score_at[1] + BANK * i + n * TILE].rearrange("p (a b) -> p a b", a=n)
                    mm = act.activation(ln_c[:, 4 * i:4 * i + n, :], counts, ACT.Ln, bias=float(2.0 ** -60))
                mm.then_inc(s["ln_ready"], 1)
                for i, n in enumerate((4, 4, 2)):
                    counts = ps[0:TILE, score_at[1] + BANK * i:score_at[1] + BANK * i + n * TILE].rearrange("p (a b) -> p a b", a=n)
                    mm = act.activation(no_edge[:, 4 * i:4 * i + n, :], counts, ACT.Relu, bias=BIG, scale=-BIG)
                mm.then_inc(s["noedge_ready"], 1)

            act.wait_ge(s["lnc_out"], 16 * START + 16 * TILES)
            act.wait_ge(s["bq_ready"], 1)

            def norm(n):
                for j in range(2):
                    act.wait_ge(s["yt_ps"], START + 2 * n + j + 1)
                    act.wait_ge(s["group_done"], START + n)
                    act.activation(y_hi[:, :, TILE * j:TILE * j + TILE], bank(2 + j, 128, 4 * TILE).rearrange("p (c n) -> p c n", c=KC),
                                   ACT.Copy).then_inc(s["yh_done"], 1)

            with act.Fori(0, BLOCKS) as blk:
                with act.Fori(0, GROUPS) as g:
                    it = blk * GROUPS + g
                    norm(2 * GROUPS * blk + g)
                    for m in range(2):
                        for i in range(2):
                            wait_apart(act, s["qk_ps"], 4 * it + 2 * m + i + 1)
                            for f in (2 * i, 2 * i + 1):
                                dst_ = (q_raw, k_hi)[m][:, f, bass.ds(g * PAIR, PAIR)]
                                bias = (bq_scaled[:, bass.ds(blk, 1), f], bcol[:, 1, bass.ds(blk, 1), f])[m]
                                mm = act.activation(dst_, bank(4 + 2 * m + i, 128, PAIR, PAIR * (f % 2)), ACT.Identity,
                                                    bias=bias, scale=(QSCALE, 1.0)[m])
                            mm.then_inc(s[("q_done", "kh_done")[m]], 1)
                    for j in range(2):
                        wait_apart(act, s["v_ps"], 2 * it + j + 1)
                        act.activation(tile_of(v_hi, 2 * g + j), bank(4 + j, TILE), ACT.Copy).then_inc(s["vh_done"], 1)
                with act.Fori(0, GROUPS) as g:
                    it = blk * GROUPS + g

                    def exponent(h, j):
                        n = 2 * h + j
                        act.wait_ge(s["negm_done"], 8 * it + n + 1)
                        act.activation(probs[n % PSLOTS][:], probs[n % PSLOTS][:], ACT.Exp, bias=neg_max[:, n:n + 1],
                                       accum_out=den[:, n:n + 1]).then_inc(s["exp_done"], 1)

                    act.wait_ge(s["rden_done"], START + HEADS * it)
                    for j in range(2):
                        exponent(0, j)
                    for h in range(HEADS):
                        for dp in range(DPAIRS):
                            n = 5 * h + dp
                            act.wait_ge(s["tp_ps"], START + 5 * HEADS * it + n + 1)
                            act.wait_ge(s["pv_done"], START + 5 * HEADS * it + max(n - TSLOTS + 1, 0))
                            act.activation(pt[:, n % TSLOTS, 0], bank(T_BANK, TILE, 2 * PAIR).rearrange("p (e n) -> p e n", e=2),
                                           ACT.Copy).then_inc(s["pth_done"], 1)
                            if h + 1 < HEADS and dp == 3:
                                exponent(h + 1, 0)
                            if h + 1 < HEADS and dp == 4:
                                exponent(h + 1, 1)
                        act.wait_ge(s["bc_ps"], START + HEADS * it + h + 1)
                        act.wait_ge(s["of_done"], START + HEADS * it + h)
                        act.activation(rbc[:], bank(O_BANK, 128, PAIR, PAIR), ACT.Copy).then_inc(s["bc_done"], 1)
                        act.wait_ge(s["of_done"], START + HEADS * it + h + 1)
                        act.wait_ge(s["wo_ps"], START + 2 * it)
                        act.activation(o_hi[:, h, :], o_f[:], ACT.Copy).then_inc(s["oh_done"], 1)
                act.wait_ge(s["wo_ps"], START + 2 * GROUPS * (blk + 1))
                for n in range(2):
                    split_hi(NEXT // 2 + MATS // 2 * blk, n, m_hi[:, n])

                def mlp_group(g):
                    it = blk * GROUPS + g
                    norm(2 * GROUPS * blk + GROUPS + g)
                    act.wait_ge(s["hl_done"], START + it)
                    for i in range(2):
                        wait_apart(act, s["h_ps"], 2 * it + i + 1)
                        for f in (2 * i, 2 * i + 1):
                            mm = act.activation(h_raw[:, f, :], bank(4 + i, 128, PAIR, PAIR * (f % 2)), ACT.Relu,
                                                bias=bcol[:, 2, bass.ds(blk, 1), f])
                        mm.then_inc(s["hraw_done"], 1)

                for g in range(NEXT):
                    mlp_group(g)
                    split_hi(NEXT // 2 + MATS // 2 * blk + 1 + g // 2, g % 2, w_hi[:, g])
                mlp_group(NEXT)

        @block.gpsimd
        def _(pool):
            for name in ("ol_done", "hl_done", "lnc_ready"):
                pool.sem_inc(s[name], START)
            def split_lo(load, stage_n, dst, hi):
                pool.wait_ge(s["w_hi_done"], load + 1)
                pool.tensor_tensor(dst, stage[stage_n][:], hi.bitcast(F32), ALU.subtract).then_inc(s["w_lo_done"], 1)

            for n in range(NEXT):
                split_lo(n, n % 2, w_lo[:, n], w_hi[:, n])
            with pool.Fori(0, TILES) as t:
                pool.wait_ge(s["ln_ready"], t + 1)
                pool.wait_ge(s["noedge_ready"], START + t + 1)
                pool.wait_ge(s["lnc_out"], 16 * START + 16 * t)
                pool.tensor_tensor(lnc_w[:], ln_c[:], no_edge[:], ALU.subtract).then_inc(s["lnc_ready"], 1)
            pool.wait_ge(s["cond_ready"], 2)
            pool.wait_ge(s["one_ready"], 5)

            def norm(n, g):
                wait_apart(pool, s["group_done"], START + n)
                pool.tensor_copy(cond_group[:], cond_stack[:, bass.ds(g * PAIR, PAIR)].bitcast(F32)).then_inc(s["cg_ready"], 1)
                wait_apart(pool, s["mv_done"], 2 * n + 2)
                pool.tensor_scalar(var_eps[:], mean_var[:, :, 1], EPS, None, ALU.add).then_inc(s["vareps_done"], 1)
                pool.wait_ge(s["vareps_done"], n + 1)
                pool.wait_ge(s["y_done"], START + 2 * n)
                pool.tensor_tensor(rstd[:], var_eps[:], minus_half[:], ALU.pow).then_inc(s["rstd_done"], 1)

            with pool.Fori(0, BLOCKS) as blk:
                with pool.Fori(0, GROUPS) as g:
                    norm(2 * GROUPS * blk + g, g)
                wait_apart(pool, s["group_done"], START + GROUPS * (2 * blk + 1))
                with pool.Fori(0, GROUPS) as g:
                    it = blk * GROUPS + g
                    pool.wait_ge(s["qh_done"], it + 1)
                    pool.tensor_tensor(q_lo[:], q_raw[:, :, bass.ds(g * PAIR, PAIR)], q_hi[:].bitcast(F32), ALU.subtract).then_inc(s["ql_done"], 1)
                    for h in range(HEADS):
                        pool.wait_ge(s["rden_done"], START + HEADS * it + h + 1)
                        wait_apart(pool, s["bc_ps"], START + HEADS * it + h)
                        for j in range(2):
                            mm = pool.tensor_scalar(diag[:, j, :], ident[0:TILE, 0:TILE], rden[:, 2 * h + j:2 * h + j + 1], None, ALU.mult)
                        mm.then_inc(s["diag_done"], 1)
                        pool.wait_ge(s["oh_done"], HEADS * it + h + 1)
                        pool.wait_ge(s["wo_ps"], START + 2 * it)
                        pool.tensor_tensor(o_lo[:, h, :], o_f[:], o_hi[:, h, :].bitcast(F32), ALU.subtract).then_inc(s["ol_done"], 1)
                for n in range(2):
                    split_lo(NEXT + MATS * blk + n, n, m_lo[:, n], m_hi[:, n])

                def mlp_group(g):
                    it = blk * GROUPS + g
                    norm(2 * GROUPS * blk + GROUPS + g, g)
                    pool.wait_ge(s["hh_done"], it + 1)
                    pool.tensor_tensor(h_lo[:], h_raw[:], h_hi[:].bitcast(F32), ALU.subtract).then_inc(s["hl_done"], 1)

                for g in range(NEXT):
                    mlp_group(g)
                    split_lo(NEXT + MATS * blk + 2 + g, g % 2, w_lo[:, g], w_hi[:, g])
                mlp_group(NEXT)
            for t in range(TILES):
                pool.wait_ge(s["f_mv"], t + 1)
                pool.tensor_scalar(var_eps[:, 0:1], mean_var[:, t % 2, 1:2], EPS, None, ALU.add).then_inc(s["f_var"], 1)
                pool.wait_ge(s["f_var"], t + 1)
                pool.tensor_tensor(rstd[:, t % 2:t % 2 + 1], var_eps[:, 0:1], minus_half[:, 0:1], ALU.pow).then_inc(s["f_rstd"], 1)


def kernel(**inputs):
    import numpy as np
    import concourse.bacc as bacc
    from concourse.bass_utils import run_bass_kernel_spmd

    a = {k.replace("L0_gnn_", ""): np.ascontiguousarray(v) for k, v in inputs.items()}
    f32 = np.float32

    def chunked(w):
        return w.reshape(KC, 128, DIM).transpose(1, 0, 2).reshape(128, KC * DIM)

    mats = [chunked(a[name][b]) for b in range(BLOCKS) for name in ("wq", "wk", "wv", "wo", "m_w1", "m_w2")]
    mats += mats[:NEXT]
    stacks = np.zeros((7, BLOCKS, 32, DIM), f32)
    for kind, (w, b) in enumerate((("s1_w", "s1_b"), ("b1_w", "b1_b"), (None, "bv"), (None, "bo"),
                                   ("s2_w", "s2_b"), ("b2_w", "b2_b"), (None, "m_b2"))):
        if w:
            stacks[kind, :, 0:CONDS] = a[w]
        stacks[kind, :, CONDS] = a[b]
    bias_cols = np.stack([a[n].reshape(BLOCKS, KC, 128) for n in ("bq", "bk", "m_b1")]).transpose(3, 0, 1, 2).reshape(128, -1)
    w2 = np.zeros((CONDS, STACK), f32)
    b2 = np.zeros((STACK, 1), f32)
    for i in range(3):
        w2[:, 32 * i:32 * i + CONDS] = a["f_w2"]
        b2[32 * i:32 * i + CONDS, 0] = a["f_b2"]
    b2[CONDS] = b2[32 + CONDS] = 1.0
    consts = np.zeros((128, 512), f32)
    consts[0:TILES, 128] = TILE * np.arange(TILES)
    consts[0:TILES, 129] = TILE * np.arange(TILES) + TILE - 1
    consts[:, 130:130 + FREQS] = np.arange(1, FREQS + 1, dtype=f32) * f32(2.0 * np.pi / 16)
    consts[[CONDS, 32 + CONDS, 64 + CONDS], 162] = 1.0
    consts[:, 164:164 + EPAIRS] = 1000.0 + np.arange(EPAIRS)
    consts[:, 384:512] = np.eye(128)
    arrays = {
        "x": a["x"], "src": a["src"], "dst": a["dst"], "node_vec": np.ascontiguousarray(a["node_vec1"].reshape(TILES, TILE).T),
        "weights": np.ascontiguousarray(np.stack(mats)), "stacks": stacks, "bias_cols": np.ascontiguousarray(bias_cols),
        "f_w1": a["f_w1"], "f_b1": a["f_b1"].reshape(CONDS, 1), "f_w2": w2, "f_b2": b2,
        "consts": consts, "iota_row": np.tile(np.arange(NODES, dtype=np.float16), (HALF, 1)),
    }
    arrays = {f"in_{k}": v for k, v in arrays.items()}
    nc = bacc.Bacc("TRN2", target_bir_lowering=False, num_devices=1, dynamic_dma_scratch_size=1024)
    args = [nc.dram_tensor(k, v.shape, mybir.dt.from_np(v.dtype), kind="ExternalInput").ap() for k, v in arrays.items()]
    args.append(nc.dram_tensor("out", (NODES, DIM), F32, kind="ExternalOutput").ap())
    gnn_kernel(nc, *args)
    r = run_bass_kernel_spmd(nc, [arrays], core_ids=[0])
    return r.results[0]["out"]
```

```python
from contextlib import ExitStack

import concourse.bass as bass
from concourse import mybir

F32 = mybir.dt.float32
F32R = mybir.dt.float32r
F16 = mybir.dt.float16
BF16 = mybir.dt.bfloat16
I32 = mybir.dt.int32
ALU = mybir.AluOpType
ACT = mybir.ActivationFunctionType
AX_X = mybir.AxisListType.X

NODES = 1250
DIM = 512
EDGES = 40000
BLOCKS = 4
HEADS = 4
FREQS = 32
CONDS = 16
EPS = 1e-5
TILE = 125
TILES = NODES // TILE
PAIR = 2 * TILE
GROUPS = NODES // PAIR
KC = DIM // 128
HALF = 125
PARTS = 4
STEPS = EDGES // (PARTS * HALF)
MATS = 6
NEXT = 4
STACK = 96
BANK = 512
COLS = [(0, 512), (512, 1024), (1024, NODES)]
QSCALE = float(DIM // HEADS) ** -0.5
BIG = 1e30
TWO_PI = 6.283185307179586
PI_HI = 6.28125
PI_MID = 0.0019350051879882812
PI_LO = TWO_PI - PI_HI - PI_MID
ROUND = 12582912.0
SIN_MAX = 3.1415925
START = 4
PSLOTS = 4
TSLOTS = 4
DPAIRS = TILES // 2


def split_products(h, l, h2, l2):
    return [(h, h2), (h, l2), (l, h2)]


def gnn_kernel(nc, x, src, dst, node_vec, weights, stacks, bias_cols, f_w1, f_b1, f_w2, f_b2, consts, iota_row, out):
    ctx = ExitStack()
    with ctx:
        top = [1152]

        def size_of(shape, dt):
            size = 2 if dt in (F16, BF16) else 4
            for n in shape[1:]:
                size *= n
            return (size + 31) // 32 * 32

        def at(name, shape, dt, offset=None):
            if offset is None:
                offset, top[0] = top[0], top[0] + size_of(shape, dt)
            return nc.alloc_sbuf_tensor_at(name, shape, dt, offset=offset)

        def sem(name):
            return ctx.enter_context(nc.semaphore(name))

        x_sb = at("x_sb", [TILE, TILES, DIM], F32)
        cond_stack = at("cond_stack", [STACK, NODES], F32R)
        ident = at("ident", [128, 128], F32)
        bcol = at("bcol", [128, 3, BLOCKS, KC], F32)
        bq_scaled = at("bq_scaled", [128, BLOCKS, KC], F32)
        cond_group = at("cond_group", [STACK, PAIR], F32R)
        ones_stack = at("ones_stack", [64, TILE], F32R)
        stats = at("stats", [TILE, 2, 6], F32)
        mean_var = at("mean_var", [TILE, 2, 2], F32)
        var_eps = at("var_eps", [TILE, 2], F32)
        rstd = at("rstd", [TILE, 2], F32)
        minus_half = at("minus_half", [TILE, TILES], F32)
        row_max = at("row_max", [TILE, 8], F32)
        neg_max = at("neg_max", [TILE, 8], F32)
        den = at("den", [TILE, 8], F32)
        den_safe = at("den_safe", [TILE, 8], F32)
        rden = at("rden", [TILE, 8], F32)
        diag = at("diag", [TILE, 2, TILE], F32)
        ones_f = at("ones_f", [TILE, 128], F32)
        rbc = at("rbc", [128, PAIR], F32)
        o_f = at("o_f", [128, PAIR], F32)
        stk_a = at("stk_a", [STACK, 3, DIM], F32R)
        stk_b = at("stk_b", [STACK, DIM], F32R)

        q_at = top[0]
        q_raw = at("q_raw", [128, HEADS, NODES], F32)
        stage = [at(f"stage{i}", [128, KC, DIM], F32, q_at + 8192 * i) for i in range(2)]

        kv = top[0]
        k_hi = at("k_hi", [128, HEADS, NODES], F32R)
        kl_at = top[0]
        k_lo = at("k_lo", [128, HEADS, NODES], F32R)
        vh_at = top[0]
        v_hi = at("v_hi", [TILE, TILES, DIM], F32R)
        vl_at = top[0]
        v_lo = at("v_lo", [TILE, TILES, DIM], F32R)
        kv_end = top[0]
        m_hi = at("m_hi", [128, 2, KC, DIM], F32R, kv)
        m_lo = at("m_lo", [128, 2, KC, DIM], F32R, kl_at)
        stk_c = [at("stk_c0", [STACK, DIM], F32R, kv + 16384), at("stk_c1", [STACK, DIM], F32R, kl_at + 16384),
                 at("stk_c2", [STACK, DIM], F32R, vh_at)]
        h_raw = at("h_raw", [128, KC, PAIR], F32, vh_at + 2048)
        h_hi = at("h_hi", [128, KC, PAIR], F32R, vh_at + 6048)
        h_lo = at("h_lo", [128, KC, PAIR], F32R, vh_at + 10048)
        f_stats = at("f_stats", [TILE, TILES, 6], F32, vh_at + 14048)
        f_mean_var = at("f_mean_var", [TILE, TILES, 2], F32, vh_at + 14304)
        f_var = at("f_var", [TILE, TILES], F32, vh_at + 14400)
        f_rstd = at("f_rstd", [TILE, TILES], F32, vh_at + 14464)
        x0_sb = at("x0_sb", [TILE, TILES, DIM], F32, vl_at)

        wh_at = top[0]
        w_hi = at("w_hi", [128, NEXT, KC, DIM], F32R)
        wl_at = top[0]
        w_lo = at("w_lo", [128, NEXT, KC, DIM], F32R)
        pt = [at(f"pt{i}", [TILE, 2, 2, PAIR], F32R, wh_at + offset) for i, offset in enumerate((0, 4000, 13216, 17216))]
        lnc_sb = [at("lnc0_sb", [TILE, NODES], F32, wl_at + 10048), at("lnc1_sb", [TILE, NODES], F32, wh_at + 8192)]

        y_at = top[0]
        y_a = [at(name, [128, KC, PAIR], F32R) for name in ("ya_hi", "ya_lo")]
        y_sb = at("y_sb", [TILE, 2, DIM], F32)
        o_hi = at("o_hi", [128, HEADS, PAIR], F32R, y_at)
        o_lo = at("o_lo", [128, HEADS, PAIR], F32R, y_at + 4000)
        probs = [at("p0", [TILE, NODES], F32, y_at + 8000), at("p1", [TILE, NODES], F32, wl_at),
                 at("p2", [TILE, NODES], F32, wl_at + 5024), at("p3", [TILE, NODES], F32, wl_at + 15072)]
        q_hi = at("q_hi", [128, HEADS, PAIR], F32R, y_at + 13024)
        q_lo = at("q_lo", [128, HEADS, PAIR], F32R, y_at + 17024)
        y_c = [at("yc_hi", [128, KC, PAIR], F32R, y_at + 13024), at("yc_lo", [128, KC, PAIR], F32R, y_at + 17024)]
        assert y_at + 21024 <= 229344, y_at

        spare = [kv]

        def setup(name, shape, dt):
            spare[0] += size_of(shape, dt)
            assert spare[0] <= kv_end, name
            return at(name, shape, dt, spare[0] - size_of(shape, dt))

        onehot_src = setup("onehot_src", [HALF, PARTS, NODES], BF16)
        onehot_dst = setup("onehot_dst", [HALF, PARTS, TILE], BF16)
        iota = setup("iota", [HALF, NODES], F16)
        zeros = setup("zeros", [HALF, 512], BF16)
        ct_sb = setup("ct_sb", [TILE, NODES], F32)
        ln_c = setup("ln_c", [TILE, TILES, TILE], F32)
        no_edge = setup("no_edge", [TILE, TILES, TILE], F32)
        lnc_w = setup("lnc_w", [TILE, TILES, TILE], F32)
        edge_int = setup("edge_int", [STEPS, 2, PARTS * HALF], I32)
        edge_f = setup("edge_f", [STEPS, 2, PARTS * HALF], F32)
        src_t = setup("src_t", [HALF, PARTS, STEPS], F32)
        dst_t = setup("dst_t", [HALF, PARTS, STEPS], F32)
        cst = setup("cst", [128, 512], F32)
        step_stats = setup("step_stats", [STEPS, 2], F32)
        step_wide = setup("step_wide", [STEPS, 2, TILES], F32)
        zero10 = setup("zero10", [STEPS, TILES], F32)
        win_a = setup("win_a", [TILES, STEPS], F32)
        win_rel = setup("win_rel", [TILES, STEPS], F32)
        win_first = setup("win_first", [TILES, STEPS], F32)
        win_last = setup("win_last", [TILES, STEPS], F32)
        win = setup("win", [TILES, 8], F32)
        win_row = setup("win_row", [1, TILES, 2], F32)
        win_scan = setup("win_scan", [1, 3, TILES], F32)
        win_int = setup("win_int", [1, 3, TILES], I32)
        nv = setup("nv", [TILE, TILES], F32)
        phase = setup("phase", [TILE, TILES, FREQS], F32)
        turns = setup("turns", [TILE, TILES, FREQS], F32)
        emb = setup("emb", [TILE, TILES, 2 * FREQS], F32)
        emb_t = setup("emb_t", [2 * FREQS, NODES], F32)
        gate_z = setup("gate_z", [CONDS, NODES], F32)
        small = setup("small", [128, 2], F32)
        w1_sb = setup("w1_sb", [2 * FREQS, CONDS], F32)
        w2_sb = setup("w2_sb", [CONDS, STACK], F32)
        cond_f = at("cond_f", [STACK, NODES], F32, wh_at + 3 * 8192)
        gate_e = at("gate_e", [CONDS, NODES], F32, wl_at + 3 * 8192)
        gate_r = at("gate_r", [CONDS, NODES], F32, wl_at + 2 * 8192)
        stack_raw = at("stack_raw", [STACK, BLOCKS, DIM], F32, y_at)
        stack_r = at("stack_r", [STACK, BLOCKS, DIM], F32R, y_at + 8192)

        ps = ctx.enter_context(nc.psum_tensor("ps", [128, 8 * BANK], F32))
        T_BANK, O_BANK = 5, 7

        def bank(n, parts=128, cols=BANK, start=0):
            return ps[0:parts, n * BANK + start:n * BANK + start + cols]

        def tiles_of(n):
            return bank(n, 128, KC * TILE).rearrange("p (c n) -> p c n", c=KC)

        def chunks(start):
            cuts = [0] + [b * BANK - start for b in range(1, 9) if 0 < b * BANK - start < NODES] + [NODES]
            return list(zip(cuts, cuts[1:]))

        lnc_dram = nc.dram_tensor("lnc_dram", [TILES, TILE, NODES], F32, kind="Internal").ap()
        stk_dram = nc.dram_tensor("stk_dram", [7, BLOCKS + 1, STACK, DIM], F32, kind="Internal").ap()
        win_dram = nc.dram_tensor("win_dram", [TILES, 2], F32, kind="Internal").ap()

        by_pe = "mod_ps yt_ps h_ps s_ps pv_done wo_ps bc_ps m2_ps v_ps".split()
        by_dve = "y_done yl_done vl_done kl_done ttr_done xb_done ptl_done of_done xc_done hl_done rden_done".split()
        by_act = "hraw_done ct_copied noedge_ready".split()
        by_pool = "ol_done lnc_ready".split()
        s = {name: sem(name) for name in by_pe + by_dve + by_act + by_pool + (
            "consts_in nv_in edges_in w1_in x_in stack_in stack_hi stack_split stack_out "
            "phase_done reduced emb_ready emb_ps emb_t_ready z_ps z_ready e_ready e1_ready r_ready "
            "s_ready c_ps c_ready cond_ready bq_ready edge_float edge_ps edge_t_ready step_stat step_wide_ready bound_ps "
            "win_step win_out win_row_in scan_step win_ready const_ready zero_ready "
            "ct_ps cn_ps ln_ready lnc_out "
            "w_hi_done w_lo_done m_hi0_done m_hi1_done m_lo0_done m_lo1_done stk_a_in stk_b_in stk_c_in stk_d_in "
            "cg_ready stat_done mv_done vareps_done rstd_done z_done yh_done "
            "q_ps k_ps q_done kh_done vh_done "
            "qh_done ql_done negm_done exp_done tp_ps pth_done "
            "densafe_done diag_done bc_done oh_done "
            "hh_done apart x0_in f_sum f_stat f_mv f_var f_rstd f_out stored").split()}
        onehot_ready = [sem(f"onehot_ready{i}") for i in range(PARTS)]
        onehot_used = [sem(f"onehot_used{i}") for i in range(PARTS)]
        stage_in = [sem(f"stage{i}_in") for i in range(2)]
        lnc_in = [sem(f"lnc{i}_in") for i in range(2)]
        block = ctx.enter_context(nc.Block())

        freqs = cst[0:TILE, 130:130 + FREQS]
        arange_p = cst[0:TILES, 164:164 + STEPS]
        win_lo, win_hi = cst[0:TILES, 128:129], cst[0:TILES, 129:130]
        idn = cst[:, 384:512]

        def tile_of(buffer, t):
            return buffer[:, bass.ds(t, 1), :].rearrange("p a d -> p (a d)")

        def tile_of_dram(buffer, t):
            return buffer[bass.ds(t, 1)].rearrange("a p d -> (a p) d")

        def wait_apart(engine, semaphore, value):
            engine.wait_ge(semaphore, value)
            engine.sem_inc(s["apart"], 1)

        def start_counts(engine, semaphores):
            for semaphore in semaphores:
                engine.sem_inc(semaphore, START)

        @block.sync
        def _(sp):
            sp.sem_inc(s["lnc_out"], 16)
            sp.sem_inc(s["stack_out"], 16)
            sp.dma_start(cst[:], consts).then_inc(s["consts_in"], 16)
            sp.dma_start(edge_int[:, 0], src.rearrange("(p j) -> p j", p=STEPS)).then_inc(s["edges_in"], 16)
            sp.dma_start(edge_int[:, 1], dst.rearrange("(p j) -> p j", p=STEPS)).then_inc(s["edges_in"], 16)
            sp.dma_start(nv[:], node_vec).then_inc(s["nv_in"], 16)
            sp.dma_start(iota[:], iota_row).then_inc(s["consts_in"], 16)
            sp.dma_start(w1_sb[:], f_w1).then_inc(s["w1_in"], 16)
            sp.dma_start(w2_sb[:], f_w2).then_inc(s["w1_in"], 16)
            sp.dma_start(small[0:CONDS, 0:1], f_b1).then_inc(s["w1_in"], 16)
            sp.dma_start(small[0:STACK, 1:2], f_b2).then_inc(s["w1_in"], 16)
            sp.dma_start(bcol[:].rearrange("p a b c -> p (a b c)"), bias_cols).then_inc(s["w1_in"], 16)
            sp.wait_ge(s["win_step"], 7)
            sp.dma_start(win_dram, win[:, 4:6]).then_inc(s["win_out"], 16)
            sp.wait_ge(s["win_out"], 16)
            sp.dma_start(win_row[:].rearrange("o t c -> o (t c)"),
                         win_dram.rearrange("t c -> (t c)").rearrange("(o n) -> o n", o=1)).then_inc(s["win_row_in"], 16)
            for n in range(NEXT):
                if n >= 2:
                    sp.wait_ge(s["w_lo_done"], n - 1)
                sp.dma_start(stage[n % 2][:].rearrange("p c d -> p (c d)"), weights[n]).then_inc(stage_in[n % 2], 16)
            sp.dma_start(x_sb[:], x.rearrange("(t p) d -> p t d", p=TILE)).then_inc(s["x_in"], 16)

            def store_counts(t):
                sp.wait_ge(s["lnc_ready"], START + t + 1)
                sp.dma_start(lnc_dram[:, :, bass.ds(t * TILE, TILE)].rearrange("a p d -> p a d"),
                             lnc_w[:]).then_inc(s["lnc_out"], 16)

            with sp.Fori(0, 7) as t:
                sp.wait_ge(s["stack_out"], 16 * (2 * t + 1))
                for b in range(3):
                    sp.dma_start(stack_raw[32 * b:32 * b + 32, :, :],
                                 stacks[bass.ds(t, 1)].rearrange("a b r d -> (a r) b d")).then_inc(s["stack_in"], 16)
                sp.wait_ge(s["stack_split"], t + 1)
                sp.dma_start(stk_dram[bass.ds(t, 1), 0:BLOCKS].rearrange("a b r d -> (a r) b d"),
                             stack_r[:].bitcast(F32)).then_inc(s["stack_out"], 16)
                sp.dma_start(stk_dram[bass.ds(t, 1), BLOCKS].rearrange("a r d -> (a r) d"),
                             stack_r[:, 0].bitcast(F32)).then_inc(s["stack_out"], 16)
                store_counts(t)
            with sp.Fori(7, TILES) as t:
                store_counts(t)
            sp.wait_ge(s["stack_out"], 16 * 15)
            sp.dma_start(stk_a[:].bitcast(F32), stk_dram[0:3, 0].rearrange("k r d -> r k d")).then_inc(s["stk_a_in"], 16)
            sp.wait_ge(s["lnc_out"], 16 * (TILES + 1))

            with sp.Fori(0, BLOCKS) as blk:
                sp.wait_ge(s["wo_ps"], START + 2 * GROUPS * blk)
                sp.dma_start(stk_b[:].bitcast(F32), stk_dram[3, bass.ds(blk, 1)].rearrange("a r d -> (a r) d")).then_inc(s["stk_b_in"], 16)
                wait_apart(sp, s["k_ps"], 2 * GROUPS * (blk + 1))
                with sp.Fori(0, GROUPS) as g:
                    for j in range(2):
                        sp.wait_ge(s["ttr_done"], START + 8 * (blk * GROUPS + g) + j - 1)
                        sp.dma_start(lnc_sb[j][:], tile_of_dram(lnc_dram, 2 * g + j)).then_inc(lnc_in[j], 16)
                wait_apart(sp, s["w_lo_done"], NEXT * (blk + 1))
                sp.wait_ge(s["ql_done"], HEADS * GROUPS * (blk + 1))
                for n in range(2):
                    sp.dma_start(stage[n][:].rearrange("p c d -> p (c d)"),
                                 weights[bass.ds(MATS * blk + NEXT + n, 1)].rearrange("a p n -> (a p) n")).then_inc(stage_in[n], 16)
                sp.wait_ge(s["s_ps"], START + 8 * GROUPS * (blk + 1))
                for k in range(2):
                    sp.dma_start(stk_c[k][:].bitcast(F32), stk_dram[4 + k, bass.ds(blk, 1)].rearrange("a r d -> (a r) d")).then_inc(s["stk_c_in"], 16)
                sp.wait_ge(s["wo_ps"], START + 2 * GROUPS * (blk + 1))
                sp.dma_start(stk_c[2][:].bitcast(F32), stk_dram[6, bass.ds(blk, 1)].rearrange("a r d -> (a r) d")).then_inc(s["stk_d_in"], 16)
                sp.dma_start(stk_a[:].bitcast(F32), stk_dram[0:3, bass.ds(blk + 1, 1)].rearrange("k a r d -> (a r) k d")).then_inc(s["stk_a_in"], 16)
                for n in range(NEXT):
                    if n == 0:
                        sp.wait_ge(s["m_lo0_done"], blk + 1)
                    elif n == 1:
                        sp.wait_ge(s["m_lo1_done"], blk + 1)
                    else:
                        wait_apart(sp, s["w_lo_done"], NEXT * (blk + 1) + n - 1)
                    sp.dma_start(stage[n % 2][:].rearrange("p c d -> p (c d)"),
                                 weights[bass.ds(MATS * (blk + 1) + n, 1)].rearrange("a p n -> (a p) n")).then_inc(stage_in[n % 2], 16)
            sp.dma_start(x0_sb[:], x.rearrange("(t p) d -> p t d", p=TILE)).then_inc(s["x0_in"], 16)
            for t in range(TILES):
                sp.wait_ge(s["f_out"], t + 1)
                sp.dma_start(out[t * TILE:(t + 1) * TILE, :], x_sb[:, t, :]).then_inc(s["stored"], 16)
            sp.wait_ge(s["stored"], 16 * TILES)

        @block.tensor
        def _(pe):
            start_counts(pe, [s[name] for name in by_pe] + onehot_used)
            pe.wait_ge(s["consts_in"], 32)
            pe.wait_ge(s["edge_float"], 2)
            for e in range(2):
                for part in range(PARTS):
                    mm = pe.transpose(bank(3 + e, HALF, STEPS, STEPS * part), edge_f[:, e, HALF * part:HALF * part + HALF],
                                      idn[0:STEPS, 0:STEPS])
            mm.then_inc(s["edge_ps"], 1)
            pe.wait_ge(s["step_wide_ready"], 2)
            for c in range(2):
                mm = pe.matmul(bank(6, TILES, STEPS, STEPS * c), step_wide[:, c, :], idn[0:STEPS, 0:STEPS], start=True, stop=True)
            mm.then_inc(s["bound_ps"], 1)
            pe.wait_ge(s["emb_ready"], 2)
            for t in range(TILES):
                mm = pe.transpose(bank(t // 4, 2 * FREQS, TILE, TILE * (t % 4)), emb[:, t, :], idn[0:TILE, 0:TILE])
            mm.then_inc(s["emb_ps"], 1)
            pe.wait_ge(s["w1_in"], 80)
            pe.wait_ge(s["emb_t_ready"], 3)
            pe.wait_ge(s["edge_t_ready"], 2)
            for a, b in chunks(0):
                mm = pe.matmul(ps[0:CONDS, 3 * BANK + a:3 * BANK + b], w1_sb[:], emb_t[:, a:b], start=True, stop=True)
            mm.then_inc(s["z_ps"], 1)
            pe.wait_ge(s["s_ready"], 1)
            for a, b in chunks(0):
                mm = pe.matmul(ps[0:STACK, a:b], w2_sb[:], gate_r[:, a:b], start=True, stop=True)
            mm.then_inc(s["c_ps"], 1)
            pe.wait_ge(s["zero_ready"], 1)
            pe.wait_ge(s["win_ready"], 3)
            pe.wait_ge(s["c_ready"], 1)
            with pe.Fori(0, TILES) as t:
                length = pe.value_load(win_int[0:1, 1, bass.ds(t, 1)], min_val=1, max_val=STEPS)
                base = pe.value_load(win_int[0:1, 2, bass.ds(t, 1)], min_val=0, max_val=STEPS * TILES)
                pe.wait_ge(s["ct_copied"], START + t)
                for a, b in chunks(0):
                    pe.matmul(ps[0:TILE, a:b], zeros[:, 0:TILE], zeros[:, 0:b - a], start=True, stop=False)
                with pe.Fori(0, length) as k:
                    for part in range(PARTS):
                        pe.wait_ge(onehot_ready[part], base + k + 1)
                        for a, b in chunks(0):
                            mm = pe.matmul(ps[0:TILE, a:b], onehot_dst[:, part, :], onehot_src[:, part, a:b],
                                           start=False, stop=False)
                        mm.then_inc(onehot_used[part], 1)
                for a, b in chunks(0):
                    mm = pe.matmul(ps[0:TILE, a:b], zeros[:, 0:TILE], zeros[:, 0:b - a], start=False, stop=True)
                mm.then_inc(s["ct_ps"], 1)
                pe.wait_ge(s["ct_copied"], START + t + 1)
                pe.wait_ge(s["noedge_ready"], START + t)
                for i in range(TILES):
                    mm = pe.transpose(bank(3 + i // 4, TILE, TILE, TILE * (i % 4)), ct_sb[:, TILE * i:TILE * i + TILE],
                                      idn[0:TILE, 0:TILE])
                mm.then_inc(s["cn_ps"], 1)

            pe.wait_ge(s["cond_ready"], 2)
            pe.wait_ge(s["noedge_ready"], START + TILES)

            def modulate(n, scale, bias):
                pe.wait_ge(s["cg_ready"], n + 1)
                for j in range(2):
                    pe.wait_ge(s["yl_done"], START + 2 * n + j - 1)
                    pe.matmul(bank(2 * j, TILE), cond_group[:, TILE * j:TILE * j + TILE], scale, start=True, stop=True)
                    pe.matmul(bank(2 * j + 1, TILE), cond_group[:, TILE * j:TILE * j + TILE], bias,
                              start=True, stop=True).then_inc(s["mod_ps"], 1)

            def turn_rows(n):
                for j in range(2):
                    pe.wait_ge(s["y_done"], START + 2 * n + j + 1)
                    for c in range(KC):
                        mm = pe.transpose(bank(2 * j, 128, TILE, TILE * c), y_sb[:, j, 128 * c:128 * c + 128], ident[0:TILE, 0:TILE])
                    mm.then_inc(s["yt_ps"], 1)

            def normalised(n):
                pe.wait_ge(s["yh_done"], 2 * n + 2)
                pe.wait_ge(s["yl_done"], START + 2 * n + 2)

            def features(out_bank, col, wh, wl, y, f):
                steps = [(a[:, c, 128 * f:128 * f + 128], b[:, c, :]) for a, b in split_products(wh, wl, *y) for c in range(KC)]
                for i, (a, b) in enumerate(steps):
                    mm = pe.matmul(bank(out_bank, 128, PAIR, col), a, b, start=i == 0, stop=i == len(steps) - 1)
                return mm

            def rows(out_bank, h, l, j, wh, wl, bias):
                pe.matmul(bank(out_bank, TILE), ones_stack[:], bias, start=True, stop=False)
                steps = [(a[:, c, TILE * j:TILE * j + TILE], b[:, c, :]) for a, b in split_products(h, l, wh, wl) for c in range(KC)]
                for i, (a, b) in enumerate(steps):
                    mm = pe.matmul(bank(out_bank, TILE), a, b, start=False, stop=i == len(steps) - 1)
                return mm

            pe.wait_ge(s["stk_a_in"], 16)
            modulate(0, stk_a[:, 0, :], stk_a[:, 1, :])
            turn_rows(0)

            with pe.Fori(0, BLOCKS) as blk:
                it0 = blk * GROUPS
                def queries():
                    for i in range(2):
                        for f in (2 * i, 2 * i + 1):
                            mm = features(4 + i, PAIR * (f % 2), w_hi[:, 0], w_lo[:, 0], y_a, f)
                        mm.then_inc(s["q_ps"], 1)

                def keys():
                    for i in range(2):
                        for f in (2 * i, 2 * i + 1):
                            mm = features(6 + i, PAIR * (f % 2), w_hi[:, 1], w_lo[:, 1], y_a, f)
                        mm.then_inc(s["k_ps"], 1)

                def values(out_bank, j):
                    mm = rows(out_bank, y_a[0], y_a[1], j, w_hi[:, 2], w_lo[:, 2], stk_a[0:64, 2, :])
                    mm.then_inc(s["v_ps"], 1)

                def project(g):
                    it = blk * GROUPS + g
                    n = 2 * GROUPS * blk + g
                    modulate(n + 1, stk_a[:, 0, :], stk_a[:, 1, :])
                    normalised(n)
                    pe.wait_ge(s["vl_done"], START + 2 * it)
                    queries()
                    pe.wait_ge(s["kl_done"], START + 2 * it)
                    pe.wait_ge(s["xc_done"], START + 2 * it0)
                    keys()
                    turn_rows(n + 1)
                    for j in range(2):
                        pe.wait_ge(s["q_done"], 2 * it + j + 1)
                        values(4 + j, j)

                pe.wait_ge(s["hraw_done"], START + 2 * it0)
                pe.wait_ge(s["w_hi_done"], NEXT * (blk + 1))
                wait_apart(pe, s["w_lo_done"], NEXT * (blk + 1))
                with pe.Fori(0, GROUPS - 1) as g:
                    project(g)

                def scores(it, h, j, i):
                    if i < 2:
                        pe.wait_ge(s["ttr_done"], START + 8 * it + 2 * h + j - 1)
                    else:
                        pe.wait_ge(s["ttr_done"], START + 8 * it + 2 * h + j)
                    lo, hi = (chunks(0), chunks(NODES)[1:] + chunks(NODES)[:1])[j][i]
                    for part, (a, b) in enumerate(split_products(q_hi, q_lo, k_hi, k_lo)):
                        mm = pe.matmul(ps[0:TILE, NODES * j + lo:NODES * j + hi], a[:, h, TILE * j:TILE * j + TILE],
                                       b[:, h, lo:hi], start=part == 0, stop=part == 2)
                    if i == 2:
                        mm.then_inc(s["s_ps"], 1)

                def turn(it, h, dp):
                    n = 5 * h + dp
                    if dp == 0:
                        pe.wait_ge(s["exp_done"], 8 * it + 2 * h + 2)
                    pe.wait_ge(s["ptl_done"], START + 5 * HEADS * it + n - 1)
                    for d in (2 * dp, 2 * dp + 1):
                        for j in range(2):
                            mm = pe.transpose(bank(T_BANK + n % 2, TILE, TILE, PAIR * (d % 2) + TILE * j),
                                              probs[(2 * h + j) % PSLOTS][:, TILE * d:TILE * d + TILE], ident[0:TILE, 0:TILE])
                    mm.then_inc(s["tp_ps"], 1)

                def weigh(it, h, dp):
                    n = 5 * h + dp
                    if dp == 0:
                        pe.wait_ge(s["of_done"], START + HEADS * it + h)
                    pe.wait_ge(s["ptl_done"], START + 5 * HEADS * it + n + 1)
                    steps = [(a[:, 2 * dp + e, 128 * h:128 * h + 128], pt[n % TSLOTS][:, w, e, :])
                             for e in range(2) for a, w in ((v_hi, 0), (v_hi, 1), (v_lo, 0))]
                    for i, (a, b) in enumerate(steps):
                        mm = pe.matmul(bank(O_BANK, 128, PAIR), a, b, start=dp == 0 and i == 0,
                                       stop=dp == DPAIRS - 1 and i == len(steps) - 1)
                    mm.then_inc(s["pv_done"], 1)

                def spread(it, h):
                    pe.wait_ge(s["diag_done"], HEADS * it + h + 1)
                    for j in range(2):
                        mm = pe.matmul(bank(O_BANK, 128, TILE, PAIR + TILE * j), ones_f[:], diag[:, j, :], start=True, stop=True)
                    mm.then_inc(s["bc_ps"], 1)

                def output(it, out_bank, j):
                    pe.wait_ge(s["oh_done"], HEADS * (it + 1))
                    pe.wait_ge(s["ol_done"], START + HEADS * (it + 1))
                    mm = rows(out_bank, o_hi, o_lo, j, w_hi[:, 3], w_lo[:, 3], stk_b[0:64, :])
                    mm.then_inc(s["wo_ps"], 1)

                def attend(g, first, last):
                    it = blk * GROUPS + g
                    for h in range(HEADS):
                        before = (it, h - 1) if h else None if first else (it - 1, HEADS - 1)
                        nxt = (it, h + 1) if h + 1 < HEADS else None if last else (it + 1, 0)
                        if nxt:
                            pe.wait_ge(s["ql_done"], HEADS * nxt[0] + nxt[1] + 1)
                            for i in range(3):
                                scores(*nxt, 0, i)
                        if before:
                            weigh(*before, 3)
                        if h == 0 and first:
                            pe.wait_ge(s["vl_done"], START + 2 * GROUPS * (blk + 1) - 1)
                        if h == 1 and not first:
                            pe.wait_ge(s["xb_done"], START + 2 * it)
                        turn(it, h, 0)
                        if before:
                            weigh(*before, 4)
                            spread(*before)
                        if nxt:
                            for i in range(2):
                                scores(*nxt, 1, i)
                        if h == 0 and first:
                            pe.wait_ge(s["vl_done"], START + 2 * GROUPS * (blk + 1))
                        turn(it, h, 1)
                        if nxt:
                            scores(*nxt, 1, 2)
                        elif last:
                            pe.wait_ge(s["stk_c_in"], 32 * (blk + 1))
                            pe.wait_ge(s["ttr_done"], START + 8 * GROUPS * (blk + 1))
                            modulate(GROUPS * (2 * blk + 1), stk_c[0][:], stk_c[1][:])
                        turn(it, h, 2)
                        weigh(it, h, 0)
                        turn(it, h, 3)
                        if h == 0 and not first:
                            pe.wait_ge(s["ptl_done"], START + 5 * HEADS * it + 3)
                            output(it - 1, T_BANK, 0)
                        weigh(it, h, 1)
                        if h == 0 and not first:
                            pe.wait_ge(s["xb_done"], START + 2 * it - 1)
                        turn(it, h, 4)
                        weigh(it, h, 2)
                        if h == 0 and not first:
                            pe.wait_ge(s["ptl_done"], START + 5 * HEADS * it + 4)
                            output(it - 1, T_BANK + 1, 1)
                    if last:
                        weigh(it, HEADS - 1, 3)
                        weigh(it, HEADS - 1, 4)
                        spread(it, HEADS - 1)

                it = it0 + GROUPS - 1
                normalised(2 * GROUPS * blk + GROUPS - 1)
                pe.wait_ge(s["kl_done"], START + 2 * it)
                keys()
                pe.wait_ge(s["vl_done"], START + 2 * it)
                queries()
                pe.wait_ge(s["kh_done"], 2 * GROUPS * (blk + 1))
                pe.wait_ge(s["kl_done"], START + 2 * GROUPS * (blk + 1))
                pe.wait_ge(s["ql_done"], HEADS * it0 + 1)
                for i in range(3):
                    scores(it0, 0, 0, i)
                pe.wait_ge(s["q_done"], 2 * GROUPS * (blk + 1))
                for i in range(3):
                    scores(it0, 0, 1, i)
                for j in range(2):
                    values(5 + j, j)
                attend(0, True, False)
                wait_apart(pe, s["stk_b_in"], 16 * (blk + 1))
                with pe.Fori(1, GROUPS - 1) as g:
                    attend(g, False, False)
                attend(GROUPS - 1, False, True)
                turn_rows(GROUPS * (2 * blk + 1))
                for j in range(2):
                    output(it0 + GROUPS - 1, 6 + j, j)

                pe.wait_ge(s["m_hi0_done"], blk + 1)
                pe.wait_ge(s["m_lo0_done"], blk + 1)

                def hidden(g):
                    it = blk * GROUPS + g
                    normalised(GROUPS * (2 * blk + 1) + g)
                    pe.wait_ge(s["hraw_done"], START + 2 * it)
                    for i in range(2):
                        for f in (2 * i, 2 * i + 1):
                            mm = features(4 + i, PAIR * (f % 2), m_hi[:, 0], m_lo[:, 0], y_c, f)
                        mm.then_inc(s["h_ps"], 1)

                def contract(g):
                    it = blk * GROUPS + g
                    pe.wait_ge(s["hh_done"], it + 1)
                    pe.wait_ge(s["hl_done"], START + it + 1)
                    for j in range(2):
                        pe.wait_ge(s["xc_done"], START + 2 * it + j - 1)
                        mm = rows(6 + j, h_hi, h_lo, j, m_hi[:, 1], m_lo[:, 1], stk_c[2][0:64, :])
                        mm.then_inc(s["m2_ps"], 1)

                def mlp(g, first, last):
                    n = GROUPS * (2 * blk + 1) + g + 1
                    if last:
                        pe.wait_ge(s["stk_a_in"], 16 * (blk + 2))
                        modulate(n, stk_a[:, 0, :], stk_a[:, 1, :])
                    else:
                        modulate(n, stk_c[0][:], stk_c[1][:])
                    hidden(g)
                    turn_rows(n)
                    if not first:
                        contract(g - 1)

                mlp(0, True, False)
                pe.wait_ge(s["xb_done"], START + 2 * GROUPS * (blk + 1))
                pe.wait_ge(s["m_hi1_done"], blk + 1)
                pe.wait_ge(s["m_lo1_done"], blk + 1)
                wait_apart(pe, s["stk_d_in"], 16 * (blk + 1))
                with pe.Fori(1, GROUPS - 1) as g:
                    mlp(g, False, False)
                mlp(GROUPS - 1, False, True)
                contract(GROUPS - 1)

        @block.vector
        def _(dve):
            start_counts(dve, [s[name] for name in by_dve])
            dve.memset(ones_f[:], 1.0).then_inc(s["const_ready"], 1)
            dve.memset(zero10[:], 0.0).then_inc(s["const_ready"], 1)
            dve.memset(minus_half[:], -0.5).then_inc(s["const_ready"], 1)
            dve.memset(zeros[:], 0.0).then_inc(s["zero_ready"], 1)
            dve.wait_ge(s["edges_in"], 32)
            for e in range(2):
                dve.tensor_copy(edge_f[:, e], edge_int[:, e]).then_inc(s["edge_float"], 1)
            dve.wait_ge(s["edge_float"], 2)
            dve.tensor_reduce(step_stats[:, 0:1], edge_f[:, 1, :], AX_X, ALU.min).then_inc(s["step_stat"], 1)
            dve.tensor_reduce(step_stats[:, 1:2], edge_f[:, 1, :], AX_X, ALU.max).then_inc(s["step_stat"], 1)
            dve.wait_ge(s["step_stat"], 2)
            dve.wait_ge(s["const_ready"], 3)
            for c in range(2):
                dve.tensor_scalar(step_wide[:, c, :], zero10[:], step_stats[:, c:c + 1], None, ALU.add).then_inc(s["step_wide_ready"], 1)
            dve.wait_ge(s["consts_in"], 32)
            dve.wait_ge(s["nv_in"], 16)
            for t in range(TILES):
                mm = dve.tensor_scalar(phase[:, t, :], freqs, nv[:, t:t + 1], None, ALU.mult)
            mm.then_inc(s["phase_done"], 1)
            dve.wait_ge(s["phase_done"], 1)
            counts = {"reduced": 0, "win_step": 0, "scan_step": 0}

            def then(name, instruction):
                counts[name] += 1
                instruction.then_inc(s[name], 1)
                dve.wait_ge(s[name], counts[name])

            for shift in range(2):
                part = emb[:, :, FREQS * shift:FREQS * shift + FREQS]
                then("reduced", dve.tensor_scalar(turns[:], phase[:], 1.0 / TWO_PI, 0.25 * shift, ALU.mult, ALU.add))
                then("reduced", dve.tensor_scalar(turns[:], turns[:], ROUND, None, ALU.add))
                then("reduced", dve.tensor_scalar(turns[:], turns[:], -ROUND, None, ALU.add))
                then("reduced", dve.scalar_tensor_tensor(out=part, in0=turns[:], scalar=-PI_HI, in1=phase[:], op0=ALU.mult, op1=ALU.add))
                then("reduced", dve.scalar_tensor_tensor(out=part, in0=turns[:], scalar=-PI_MID, in1=part, op0=ALU.mult, op1=ALU.add))
                then("reduced", dve.scalar_tensor_tensor(out=part, in0=turns[:], scalar=-PI_LO, in1=part, op0=ALU.mult, op1=ALU.add))
                if shift:
                    then("reduced", dve.tensor_scalar(part, part, TWO_PI / 4, None, ALU.add))
                then("reduced", dve.tensor_scalar(part, part, SIN_MAX, -SIN_MAX, ALU.min, ALU.max))
            dve.wait_ge(s["edge_ps"], 1)
            for e, ends in enumerate((src_t, dst_t)):
                dve.tensor_copy(ends[:], bank(3 + e, HALF, PARTS * STEPS).rearrange("p (h n) -> p h n", h=PARTS)).then_inc(s["edge_t_ready"], 1)
            dve.wait_ge(s["bound_ps"], 1)
            least, most = bank(6, TILES, STEPS), bank(6, TILES, STEPS, STEPS)
            then("scan_step", dve.tensor_scalar(win_a[:], least, win_hi, None, ALU.is_le))
            then("win_step", dve.scalar_tensor_tensor(out=win_rel[:], in0=most, scalar=win_lo, in1=win_a[:], op0=ALU.is_ge, op1=ALU.mult))
            then("scan_step", dve.scalar_tensor_tensor(out=win_first[:], in0=win_rel[:], scalar=-1000.0, in1=arange_p, op0=ALU.mult, op1=ALU.add))
            then("scan_step", dve.scalar_tensor_tensor(out=win_last[:], in0=arange_p, scalar=-999.0, in1=win_rel[:], op0=ALU.add, op1=ALU.mult))
            then("win_step", dve.tensor_reduce(win[:, 0:1], win_first[:], AX_X, ALU.min))
            then("win_step", dve.tensor_reduce(win[:, 1:2], win_last[:], AX_X, ALU.max))
            then("win_step", dve.tensor_scalar(win[:, 4:5], win[:, 0:1], float(STEPS - 1), None, ALU.min))
            then("win_step", dve.tensor_scalar(win[:, 2:3], win[:, 4:5], 1.0, None, ALU.add))
            then("win_step", dve.tensor_tensor(win[:, 3:4], win[:, 1:2], win[:, 2:3], ALU.max))
            then("win_step", dve.tensor_tensor(win[:, 5:6], win[:, 3:4], win[:, 4:5], ALU.subtract))
            dve.wait_ge(s["z_ps"], 1)
            dve.wait_ge(s["w1_in"], 80)
            dve.tensor_scalar(gate_z[:], ps[0:CONDS, 3 * BANK:3 * BANK + NODES], small[0:CONDS, 0:1], None, ALU.add).then_inc(s["z_ready"], 1)
            dve.wait_ge(s["e_ready"], 1)
            dve.tensor_scalar(gate_e[:], gate_e[:], 1.0, None, ALU.add).then_inc(s["e1_ready"], 1)
            dve.wait_ge(s["e1_ready"], 1)
            dve.reciprocal(gate_r[:], gate_e[:]).then_inc(s["r_ready"], 1)
            dve.wait_ge(s["r_ready"], 1)
            dve.tensor_tensor(gate_r[:], gate_r[:], gate_z[:], ALU.mult).then_inc(s["s_ready"], 1)
            dve.tensor_copy(ident[:], idn).then_inc(s["const_ready"], 1)
            dve.tensor_scalar(ones_stack[:], ones_f[0:64, 0:TILE], 1.0, None, ALU.mult).then_inc(s["const_ready"], 1)
            dve.tensor_scalar(bq_scaled[:], bcol[:, 0], QSCALE, None, ALU.mult).then_inc(s["bq_ready"], 1)
            dve.wait_ge(s["c_ps"], 1)
            dve.tensor_scalar(cond_f[:], ps[0:STACK, 0:NODES], small[0:STACK, 1:2], None, ALU.add).then_inc(s["c_ready"], 1)
            dve.wait_ge(s["c_ready"], 1)
            dve.tensor_copy(cond_stack[:], cond_f[:]).then_inc(s["cond_ready"], 1)
            dve.wait_ge(s["cond_ready"], 1)
            dve.tensor_tensor(cond_stack[64:96], cond_f[64:96], cond_stack[64:96].bitcast(F32), ALU.subtract).then_inc(s["cond_ready"], 1)
            dve.wait_ge(s["win_row_in"], 16)
            then("scan_step", dve.tensor_copy(win_scan[:, 2, :], win_row[:, :, 1]))
            then("scan_step", dve.tensor_tensor_scan(win_scan[:, 0, :], ones_f[0:1, 0:TILES], win_scan[:, 2, :], 0.0, ALU.mult, ALU.add))
            then("scan_step", dve.tensor_tensor(win_scan[:, 1, :], win_scan[:, 0, :], win_scan[:, 2, :], ALU.subtract))
            dve.tensor_copy(win_int[:, 0, :], win_row[:, :, 0]).then_inc(s["win_ready"], 1)
            dve.tensor_copy(win_int[:, 1, :], win_row[:, :, 1]).then_inc(s["win_ready"], 1)
            dve.tensor_copy(win_int[:, 2, :], win_scan[:, 1, :]).then_inc(s["win_ready"], 1)
            dve.wait_ge(s["win_ready"], 3)
            dve.wait_ge(s["edge_t_ready"], 2)
            with dve.Fori(0, TILES) as t:
                first = dve.value_load(win_int[0:1, 0, bass.ds(t, 1)], min_val=0, max_val=STEPS - 1)
                length = dve.value_load(win_int[0:1, 1, bass.ds(t, 1)], min_val=1, max_val=STEPS)
                base = dve.value_load(win_int[0:1, 2, bass.ds(t, 1)], min_val=0, max_val=STEPS * TILES)
                with dve.Fori(0, length) as k:
                    step = nc.s_assert_within(first + k, 0, STEPS - 1, skip_runtime_bounds_check_because="a window ends at the last step")
                    for part in range(PARTS):
                        wait_apart(dve, onehot_used[part], START + base + k)
                        dve.tensor_scalar(onehot_dst[:, part, :], iota[:, bass.ds(t * TILE, TILE)],
                                          dst_t[:, part, bass.ds(step, 1)], None, ALU.is_equal)
                        dve.tensor_scalar(onehot_src[:, part, :], iota[:],
                                          src_t[:, part, bass.ds(step, 1)], None, ALU.is_equal).then_inc(onehot_ready[part], 1)

            dve.wait_ge(s["x_in"], 16)
            dve.wait_ge(s["lnc_out"], 16 * (TILES + 1))

            def statistics(n, g):
                for j in range(2):
                    dve.bn_stats(stats[:, j, :], tile_of(x_sb, 2 * g + j)).then_inc(s["stat_done"], 1)
                for j in range(2):
                    wait_apart(dve, s["stat_done"], 2 * n + j + 1)
                    dve.bn_aggr(mean_var[:, j, :], stats[:, j, :]).then_inc(s["mv_done"], 1)

            def modulated(n, g):
                dve.wait_ge(s["mv_done"], 2 * n + 2)
                dve.wait_ge(s["yt_ps"], START + 2 * n)
                for j in range(2):
                    dve.wait_ge(s["mod_ps"], START + 2 * n + j + 1)
                    dve.scalar_tensor_tensor(out=y_sb[:, j, :], in0=tile_of(x_sb, 2 * g + j), scalar=mean_var[:, j, 0:1],
                                             in1=bank(2 * j, TILE), op0=ALU.subtract, op1=ALU.mult).then_inc(s["z_done"], 1)
                for j in range(2):
                    dve.wait_ge(s["z_done"], 2 * n + j + 1)
                    if j == 0:
                        dve.wait_ge(s["rstd_done"], n + 1)
                    dve.scalar_tensor_tensor(out=y_sb[:, j, :], in0=y_sb[:, j, :], scalar=rstd[:, j:j + 1],
                                             in1=bank(2 * j + 1, TILE), op0=ALU.mult, op1=ALU.add).then_inc(s["y_done"], 1)

            def low_rows(n, y, j):
                dve.wait_ge(s["yh_done"], 2 * n + j + 1)
                dve.tensor_tensor(y[1][:, :, TILE * j:TILE * j + TILE], tiles_of(2 * j),
                                  y[0][:, :, TILE * j:TILE * j + TILE].bitcast(F32), ALU.subtract).then_inc(s["yl_done"], 1)

            statistics(0, 0)
            modulated(0, 0)
            for j in range(2):
                low_rows(0, y_a, j)

            with dve.Fori(0, BLOCKS) as blk:
                it0 = blk * GROUPS
                def low_keys(g):
                    for i in range(2):
                        dve.wait_ge(s["kh_done"], 2 * (it0 + g) + i + 1)
                        for f in (2 * i, 2 * i + 1):
                            mm = dve.scalar_tensor_tensor(out=k_lo[:, f, bass.ds(g * PAIR, PAIR)], in0=bank(6 + i, 128, PAIR, PAIR * (f % 2)),
                                                          scalar=bcol[:, 1, bass.ds(blk, 1), f], in1=k_hi[:, f, bass.ds(g * PAIR, PAIR)].bitcast(F32),
                                                          op0=ALU.add, op1=ALU.subtract)
                        mm.then_inc(s["kl_done"], 1)

                def low_values(g, v_bank, j):
                    dve.wait_ge(s["vh_done"], 2 * (it0 + g) + j + 1)
                    dve.tensor_tensor(tile_of(v_lo, 2 * g + j), bank(v_bank, TILE), tile_of(v_hi, 2 * g + j).bitcast(F32),
                                      ALU.subtract).then_inc(s["vl_done"], 1)

                def high_queries(g, h):
                    dve.tensor_copy(q_hi[:, h, :], q_raw[:, h, bass.ds(g * PAIR, PAIR)]).then_inc(s["qh_done"], 1)

                def project(g):
                    n = 2 * GROUPS * blk + g + 1
                    statistics(n, g + 1)
                    modulated(n, g + 1)
                    low_keys(g)
                    for j in range(2):
                        low_rows(n, y_a, j)
                        low_values(g, 4 + j, j)

                wait_apart(dve, s["xc_done"], START + 2 * it0)
                with dve.Fori(0, GROUPS - 1) as g:
                    project(g)
                dve.wait_ge(s["q_done"], 2 * it0 + 2)
                for h in range(HEADS):
                    high_queries(0, h)
                low_keys(GROUPS - 1)

                def masked_max(it, h, j):
                    n = 2 * h + j
                    if h == 0:
                        dve.wait_ge(lnc_in[j], 16 * (it + 1))
                    wait_apart(dve, s["s_ps"], START + 8 * it + n + 1)
                    dve.tensor_tensor_reduce(probs[n % PSLOTS][:], ps[0:TILE, NODES * j:NODES * j + NODES], lnc_sb[j][:],
                                             1.0, -BIG / 10, ALU.add, ALU.max, row_max[:, n:n + 1]).then_inc(s["ttr_done"], 1)
                    dve.wait_ge(s["ttr_done"], START + 8 * it + n + 1)
                    dve.tensor_scalar(neg_max[:, n:n + 1], row_max[:, n:n + 1], -1.0, None, ALU.mult).then_inc(s["negm_done"], 1)

                def low_probs(it, h, dp):
                    n = 5 * h + dp
                    dve.wait_ge(s["pth_done"], 5 * HEADS * it + n + 1)
                    dve.tensor_tensor(pt[n % TSLOTS][:, 1], bank(T_BANK + n % 2, TILE, 2 * PAIR).rearrange("p (e n) -> p e n", e=2),
                                      pt[n % TSLOTS][:, 0].bitcast(F32), ALU.subtract).then_inc(s["ptl_done"], 1)

                def normalise(it, h):
                    dve.wait_ge(s["bc_done"], HEADS * it + h + 1)
                    dve.wait_ge(s["ol_done"], START + HEADS * it + h)
                    dve.tensor_tensor(o_f[:], bank(O_BANK, 128, PAIR), rbc[:], ALU.mult).then_inc(s["of_done"], 1)

                def add_output(g, out_bank, j):
                    dve.wait_ge(s["wo_ps"], START + 2 * (it0 + g) + j + 1)
                    dve.tensor_tensor(tile_of(x_sb, 2 * g + j), bank(out_bank, TILE), tile_of(x_sb, 2 * g + j),
                                      ALU.add).then_inc(s["xb_done"], 1)

                def attend(g, first, last):
                    it = blk * GROUPS + g
                    for h in range(HEADS):
                        before = (it, h - 1) if h else None if first else (it - 1, HEADS - 1)
                        nxt = (it, h + 1) if h + 1 < HEADS else None if last else (it + 1, 0)
                        low_probs(it, h, 0)
                        dve.wait_ge(s["exp_done"], 8 * it + 2 * h + 2)
                        dve.tensor_scalar(den_safe[:, 2 * h:2 * h + 2], den[:, 2 * h:2 * h + 2], 1e-30, None, ALU.max).then_inc(s["densafe_done"], 1)
                        dve.wait_ge(s["densafe_done"], HEADS * it + h + 1)
                        dve.reciprocal(rden[:, 2 * h:2 * h + 2], den_safe[:, 2 * h:2 * h + 2]).then_inc(s["rden_done"], 1)
                        if nxt:
                            masked_max(*nxt, 0)
                        elif last:
                            dve.wait_ge(s["xb_done"], START + 2 * it0 + 2)
                            statistics(GROUPS * (2 * blk + 1), 0)
                        if before:
                            normalise(*before)
                        low_probs(it, h, 1)
                        low_probs(it, h, 2)
                        if nxt:
                            masked_max(*nxt, 1)
                        elif last:
                            modulated(GROUPS * (2 * blk + 1), 0)
                        low_probs(it, h, 3)
                        if h == 0 and not first:
                            add_output(g - 1, T_BANK, 0)
                        low_probs(it, h, 4)
                        if h == 0 and not first:
                            add_output(g - 1, T_BANK + 1, 1)
                        if not last:
                            high_queries(g + 1, h)
                    if last:
                        normalise(it, HEADS - 1)

                for j in range(2):
                    masked_max(it0, 0, j)
                for j in range(2):
                    low_values(GROUPS - 1, 5 + j, j)
                attend(0, True, False)
                with dve.Fori(1, GROUPS - 1) as g:
                    attend(g, False, False)
                attend(GROUPS - 1, False, True)
                for j in range(2):
                    low_rows(GROUPS * (2 * blk + 1), y_c, j)
                dve.wait_ge(stage_in[0], 16 * (NEXT // 2 + MATS // 2 * blk + 1))
                dve.tensor_copy(m_hi[:, 0], stage[0][:]).then_inc(s["m_hi0_done"], 1)
                dve.wait_ge(s["m_hi0_done"], blk + 1)
                dve.tensor_tensor(m_lo[:, 0], stage[0][:], m_hi[:, 0].bitcast(F32), ALU.subtract).then_inc(s["m_lo0_done"], 1)
                for j in range(2):
                    add_output(GROUPS - 1, 6 + j, j)

                dve.wait_ge(s["xb_done"], START + 2 * GROUPS * (blk + 1))

                def residual(g):
                    it = blk * GROUPS + g
                    for j in range(2):
                        dve.wait_ge(s["m2_ps"], START + 2 * it + j + 1)
                        dve.tensor_tensor(tile_of(x_sb, 2 * g + j), bank(6 + j, TILE), tile_of(x_sb, 2 * g + j),
                                          ALU.add).then_inc(s["xc_done"], 1)

                def mlp(g, first, last):
                    it = blk * GROUPS + g
                    n = GROUPS * (2 * blk + 1) + g + 1
                    following, y = (0, y_a) if last else (g + 1, y_c)
                    if last:
                        dve.wait_ge(s["xc_done"], START + 2 * it0 + 2)
                    statistics(n, following)
                    modulated(n, following)
                    for j in range(2):
                        low_rows(n, y, j)
                    if not first:
                        residual(g - 1)
                    dve.wait_ge(s["hraw_done"], START + 2 * it + 2)
                    dve.tensor_copy(h_hi[:], h_raw[:]).then_inc(s["hh_done"], 1)
                    dve.wait_ge(s["hh_done"], it + 1)
                    dve.tensor_tensor(h_lo[:], h_raw[:], h_hi[:].bitcast(F32), ALU.subtract).then_inc(s["hl_done"], 1)

                mlp(0, True, False)
                with dve.Fori(1, GROUPS - 1) as g:
                    mlp(g, False, False)
                mlp(GROUPS - 1, False, True)
                residual(GROUPS - 1)

            dve.wait_ge(s["x0_in"], 16)
            dve.wait_ge(s["xc_done"], START + 2 * GROUPS * BLOCKS)
            for t in range(TILES):
                dve.tensor_tensor(x_sb[:, t, :], x_sb[:, t, :], x0_sb[:, t, :], ALU.add).then_inc(s["f_sum"], 1)
            for t in range(TILES):
                dve.wait_ge(s["f_sum"], t + 1)
                dve.bn_stats(f_stats[:, t, :], x_sb[:, t, :]).then_inc(s["f_stat"], 1)
            for t in range(TILES):
                dve.wait_ge(s["f_stat"], t + 1)
                dve.bn_aggr(f_mean_var[:, t, :], f_stats[:, t, :]).then_inc(s["f_mv"], 1)
            dve.wait_ge(s["f_rstd"], 1)
            for t in range(TILES):
                dve.tensor_scalar(x_sb[:, t, :], x_sb[:, t, :], f_mean_var[:, t, 0:1], f_rstd[:, t:t + 1],
                                  ALU.subtract, ALU.mult).then_inc(s["f_out"], 1)

        @block.scalar
        def _(act):
            start_counts(act, [s[name] for name in by_act])
            for shift in range(2):
                act.wait_ge(s["reduced"], (7, 15)[shift])
                part = emb[:, :, FREQS * shift:FREQS * shift + FREQS]
                act.activation(part, part, ACT.Sin).then_inc(s["emb_ready"], 1)
            act.wait_ge(s["emb_ps"], 1)
            for i, n in enumerate((4, 4, 2)):
                act.activation(emb_t[:, 4 * TILE * i:4 * TILE * i + n * TILE], bank(i, 2 * FREQS, n * TILE),
                               ACT.Copy).then_inc(s["emb_t_ready"], 1)
            act.wait_ge(s["z_ready"], 1)
            act.activation(gate_e[:], gate_z[:], ACT.Exp, scale=-1.0).then_inc(s["e_ready"], 1)

            def split_hi(turn, stage_n, matrix):
                act.wait_ge(stage_in[stage_n], 16 * (turn + 1))
                act.activation(matrix, stage[stage_n][:], ACT.Copy).then_inc(s["w_hi_done"], 1)

            act.wait_ge(s["cond_ready"], 2)
            for n in range(NEXT):
                split_hi(n // 2, n % 2, w_hi[:, n])

            def log_counts(t):
                act.wait_ge(s["ct_ps"], t + 1)
                act.activation(ct_sb[:], ps[0:TILE, 0:NODES], ACT.Copy).then_inc(s["ct_copied"], 1)
                act.wait_ge(s["cn_ps"], t + 1)
                act.wait_ge(s["lnc_ready"], START + t)
                for i, n in enumerate((4, 4, 2)):
                    window = bank(3 + i, TILE, n * TILE).rearrange("p (a b) -> p a b", a=n)
                    mm = act.activation(ln_c[:, 4 * i:4 * i + n, :], window, ACT.Ln, bias=float(2.0 ** -60))
                mm.then_inc(s["ln_ready"], 1)
                for i, n in enumerate((4, 4, 2)):
                    window = bank(3 + i, TILE, n * TILE).rearrange("p (a b) -> p a b", a=n)
                    mm = act.activation(no_edge[:, 4 * i:4 * i + n, :], window, ACT.Relu, bias=BIG, scale=-BIG)
                mm.then_inc(s["noedge_ready"], 1)

            with act.Fori(0, 7) as t:
                act.wait_ge(s["stack_in"], 48 * (t + 1))
                wait_apart(act, s["stack_out"], 16 * (2 * t + 1))
                act.activation(stack_raw[:], stack_raw[:], ACT.Identity, bias=cst[0:STACK, bass.ds(260 + t, 1)]).then_inc(s["stack_hi"], 1)
                wait_apart(act, s["stack_hi"], 2 * t + 1)
                act.activation(stack_r[:], stack_raw[:], ACT.Copy).then_inc(s["stack_hi"], 1)
                log_counts(t)
            with act.Fori(7, TILES) as t:
                log_counts(t)

            act.wait_ge(s["lnc_out"], 16 * (TILES + 1))
            act.wait_ge(s["stack_out"], 16 * 15)
            act.wait_ge(s["bq_ready"], 1)

            def high_rows(n, y, j):
                act.wait_ge(s["yt_ps"], START + 2 * n + j + 1)
                act.activation(y[0][:, :, TILE * j:TILE * j + TILE], tiles_of(2 * j), ACT.Copy).then_inc(s["yh_done"], 1)

            for j in range(2):
                high_rows(0, y_a, j)

            with act.Fori(0, BLOCKS) as blk:
                it0 = blk * GROUPS
                def copy_queries(g):
                    for i in range(2):
                        wait_apart(act, s["q_ps"], 2 * (it0 + g) + i + 1)
                        for f in (2 * i, 2 * i + 1):
                            mm = act.activation(q_raw[:, f, bass.ds(g * PAIR, PAIR)], bank(4 + i, 128, PAIR, PAIR * (f % 2)), ACT.Identity,
                                                bias=bq_scaled[:, bass.ds(blk, 1), f], scale=QSCALE)
                        mm.then_inc(s["q_done"], 1)

                def high_keys(g):
                    for i in range(2):
                        wait_apart(act, s["k_ps"], 2 * (it0 + g) + i + 1)
                        for f in (2 * i, 2 * i + 1):
                            mm = act.activation(k_hi[:, f, bass.ds(g * PAIR, PAIR)], bank(6 + i, 128, PAIR, PAIR * (f % 2)), ACT.Identity,
                                                bias=bcol[:, 1, bass.ds(blk, 1), f])
                        mm.then_inc(s["kh_done"], 1)

                def high_values(g, v_bank, j):
                    act.activation(tile_of(v_hi, 2 * g + j), bank(v_bank, TILE), ACT.Copy).then_inc(s["vh_done"], 1)

                with act.Fori(0, GROUPS - 1) as g:
                    copy_queries(g)
                    high_keys(g)
                    for j in range(2):
                        wait_apart(act, s["v_ps"], START + 2 * (it0 + g) + j + 1)
                        high_rows(2 * GROUPS * blk + g + 1, y_a, j)
                        high_values(g, 4 + j, j)

                def exponent(it, h, j):
                    n = 2 * h + j
                    act.wait_ge(s["negm_done"], 8 * it + n + 1)
                    act.activation(probs[n % PSLOTS][:], probs[n % PSLOTS][:], ACT.Exp, bias=neg_max[:, n:n + 1],
                                   accum_out=den[:, n:n + 1]).then_inc(s["exp_done"], 1)

                def high_probs(it, h, dp):
                    n = 5 * h + dp
                    act.wait_ge(s["tp_ps"], 5 * HEADS * it + n + 1)
                    act.wait_ge(s["pv_done"], START + 5 * HEADS * it + n - 3)
                    act.activation(pt[n % TSLOTS][:, 0], bank(T_BANK + n % 2, TILE, 2 * PAIR).rearrange("p (e n) -> p e n", e=2),
                                   ACT.Copy).then_inc(s["pth_done"], 1)

                def copy_spread(it, h):
                    act.wait_ge(s["bc_ps"], START + HEADS * it + h + 1)
                    act.wait_ge(s["of_done"], START + HEADS * it + h)
                    act.activation(rbc[:], bank(O_BANK, 128, PAIR, PAIR), ACT.Copy).then_inc(s["bc_done"], 1)

                def high_output(it, h):
                    act.wait_ge(s["of_done"], START + HEADS * it + h + 1)
                    act.wait_ge(s["wo_ps"], START + 2 * it)
                    act.activation(o_hi[:, h, :], o_f[:], ACT.Copy).then_inc(s["oh_done"], 1)

                def attend(g, first, last):
                    it = blk * GROUPS + g
                    for h in range(HEADS):
                        before = (it, h - 1) if h else None if first else (it - 1, HEADS - 1)
                        nxt = (it, h + 1) if h + 1 < HEADS else None if last else (it + 1, 0)
                        high_probs(it, h, 0)
                        if before:
                            copy_spread(*before)
                        high_probs(it, h, 1)
                        if before:
                            high_output(*before)
                        high_probs(it, h, 2)
                        if nxt:
                            exponent(*nxt, 0)
                        else:
                            act.wait_ge(stage_in[1], 16 * (NEXT // 2 + MATS // 2 * blk + 1))
                            act.activation(m_hi[:, 1], stage[1][:], ACT.Copy).then_inc(s["m_hi1_done"], 1)
                        high_probs(it, h, 3)
                        high_probs(it, h, 4)
                        if nxt:
                            exponent(*nxt, 1)

                high_keys(GROUPS - 1)
                copy_queries(GROUPS - 1)
                for j in range(2):
                    exponent(it0, 0, j)
                for j in range(2):
                    act.wait_ge(s["v_ps"], START + 2 * (it0 + GROUPS - 1) + j + 1)
                    high_values(GROUPS - 1, 5 + j, j)
                attend(0, True, False)
                with act.Fori(1, GROUPS - 1) as g:
                    attend(g, False, False)
                attend(GROUPS - 1, False, True)
                n1 = GROUPS * (2 * blk + 1)
                copy_spread(it0 + GROUPS - 1, HEADS - 1)
                high_rows(n1, y_c, 0)
                high_output(it0 + GROUPS - 1, HEADS - 1)
                high_rows(n1, y_c, 1)

                for g in range(GROUPS):
                    it = blk * GROUPS + g
                    act.wait_ge(s["hl_done"], START + it)
                    for i in range(2):
                        wait_apart(act, s["h_ps"], START + 2 * it + i + 1)
                        for f in (2 * i, 2 * i + 1):
                            mm = act.activation(h_raw[:, f, :], bank(4 + i, 128, PAIR, PAIR * (f % 2)), ACT.Relu,
                                                bias=bcol[:, 2, bass.ds(blk, 1), f])
                        mm.then_inc(s["hraw_done"], 1)
                    for j in range(2):
                        high_rows(n1 + g + 1, y_a if g == GROUPS - 1 else y_c, j)
                    if g < NEXT:
                        split_hi(NEXT // 2 + MATS // 2 * blk + 1 + g // 2, g % 2, w_hi[:, g])

        @block.gpsimd
        def _(pool):
            start_counts(pool, [s[name] for name in by_pool])

            def split_lo(count, stage_n, low, high):
                pool.wait_ge(s["w_hi_done"], count)
                pool.tensor_tensor(low, stage[stage_n][:], high.bitcast(F32), ALU.subtract).then_inc(s["w_lo_done"], 1)

            for n in range(NEXT):
                split_lo(n + 1, n % 2, w_lo[:, n], w_hi[:, n])

            def log_counts(t):
                pool.wait_ge(s["ln_ready"], t + 1)
                pool.wait_ge(s["noedge_ready"], START + t + 1)
                pool.wait_ge(s["lnc_out"], 16 * (t + 1))
                pool.tensor_tensor(lnc_w[:], ln_c[:], no_edge[:], ALU.subtract).then_inc(s["lnc_ready"], 1)

            def split_stacks(t, first):
                if first:
                    pool.wait_ge(s["w_lo_done"], NEXT)
                else:
                    wait_apart(pool, s["lnc_ready"], START + t)
                pool.wait_ge(s["stack_hi"], 2 * t + 2)
                pool.tensor_tensor(stack_r[32:64], stack_raw[32:64], stack_r[32:64].bitcast(F32), ALU.subtract).then_inc(s["stack_split"], 1)
                pool.wait_ge(s["stack_split"], t + 1)
                log_counts(t)

            split_stacks(0, True)
            with pool.Fori(1, 7) as t:
                split_stacks(t, False)
            with pool.Fori(7, TILES) as t:
                log_counts(t)
            pool.wait_ge(s["cond_ready"], 2)
            pool.wait_ge(s["const_ready"], 5)

            def condition(n, g):
                wait_apart(pool, s["mod_ps"], START + 2 * n)
                pool.tensor_copy(cond_group[:], cond_stack[:, bass.ds(g * PAIR, PAIR)].bitcast(F32)).then_inc(s["cg_ready"], 1)

            def deviation(n):
                wait_apart(pool, s["mv_done"], 2 * n + 2)
                pool.tensor_scalar(var_eps[:], mean_var[:, :, 1], EPS, None, ALU.add).then_inc(s["vareps_done"], 1)
                pool.wait_ge(s["vareps_done"], n + 1)
                pool.wait_ge(s["y_done"], START + 2 * n)
                pool.tensor_tensor(rstd[:], var_eps[:], minus_half[:, 0:2], ALU.pow).then_inc(s["rstd_done"], 1)

            condition(0, 0)
            deviation(0)
            condition(1, 1)

            with pool.Fori(0, BLOCKS) as blk:
                it0 = blk * GROUPS
                n0 = 2 * GROUPS * blk
                n1 = n0 + GROUPS
                with pool.Fori(0, GROUPS - 2) as g:
                    deviation(n0 + g + 1)
                    condition(n0 + g + 2, g + 2)
                deviation(n1 - 1)
                condition(n1, 0)

                def low_queries(g, h):
                    pool.wait_ge(s["qh_done"], HEADS * (it0 + g) + h + 1)
                    pool.tensor_tensor(q_lo[:, h, :], q_raw[:, h, bass.ds(g * PAIR, PAIR)], q_hi[:, h, :].bitcast(F32), ALU.subtract).then_inc(s["ql_done"], 1)

                def low_output(it, h):
                    pool.wait_ge(s["oh_done"], HEADS * it + h + 1)
                    pool.wait_ge(s["wo_ps"], START + 2 * it)
                    pool.tensor_tensor(o_lo[:, h, :], o_f[:], o_hi[:, h, :].bitcast(F32), ALU.subtract).then_inc(s["ol_done"], 1)

                def attend(g, first, last):
                    it = blk * GROUPS + g
                    for h in range(HEADS):
                        before = (it, h - 1) if h else None if first else (it - 1, HEADS - 1)
                        pool.wait_ge(s["bc_ps"], START + HEADS * it + h)
                        wait_apart(pool, s["rden_done"], START + HEADS * it + h + 1)
                        for j in range(2):
                            mm = pool.tensor_scalar(diag[:, j, :], ident[0:TILE, 0:TILE], rden[:, 2 * h + j:2 * h + j + 1], None, ALU.mult)
                        mm.then_inc(s["diag_done"], 1)
                        if h == HEADS - 1 and last:
                            deviation(n1)
                        if before:
                            low_output(*before)
                        if not last:
                            low_queries(g + 1, h)

                for h in range(HEADS):
                    low_queries(0, h)
                attend(0, True, False)
                with pool.Fori(1, GROUPS - 1) as g:
                    attend(g, False, False)
                attend(GROUPS - 1, False, True)
                low_output(it0 + GROUPS - 1, HEADS - 1)
                condition(n1 + 1, 1)
                pool.wait_ge(s["m_hi1_done"], blk + 1)
                pool.tensor_tensor(m_lo[:, 1], stage[1][:], m_hi[:, 1].bitcast(F32), ALU.subtract).then_inc(s["m_lo1_done"], 1)

                for g in range(GROUPS):
                    deviation(n1 + g + 1)
                    condition(n1 + g + 2, (2, 3, 4, 0, 1)[g])
                    if g < NEXT:
                        split_lo(NEXT * (blk + 1) + g + 1, g % 2, w_lo[:, g], w_hi[:, g])
            pool.wait_ge(s["f_mv"], TILES)
            pool.tensor_scalar(f_var[:], f_mean_var[:, :, 1], EPS, None, ALU.add).then_inc(s["f_var"], 1)
            pool.wait_ge(s["f_var"], 1)
            pool.tensor_tensor(f_rstd[:], f_var[:], minus_half[:], ALU.pow).then_inc(s["f_rstd"], 1)


def kernel(**inputs):
    import numpy as np
    import concourse.bacc as bacc
    from concourse.bass_utils import run_bass_kernel_spmd

    a = {k.replace("L0_gnn_", ""): np.ascontiguousarray(v) for k, v in inputs.items()}
    f32 = np.float32

    def chunked(w):
        return w.reshape(KC, 128, DIM).transpose(1, 0, 2).reshape(128, KC * DIM)

    mats = [chunked(a[name][b]) for b in range(BLOCKS) for name in ("wq", "wk", "wv", "wo", "m_w1", "m_w2")]
    mats += mats[:NEXT]
    stacks = np.zeros((7, BLOCKS, 32, DIM), f32)
    for kind, (w, b) in enumerate((("s1_w", "s1_b"), ("b1_w", "b1_b"), (None, "bv"), (None, "bo"),
                                   ("s2_w", "s2_b"), ("b2_w", "b2_b"), (None, "m_b2"))):
        if w:
            stacks[kind, :, 0:CONDS] = a[w]
        stacks[kind, :, CONDS] = a[b]
    bias_cols = np.stack([a[n].reshape(BLOCKS, KC, 128) for n in ("bq", "bk", "m_b1")]).transpose(3, 0, 1, 2).reshape(128, -1)
    w2 = np.zeros((CONDS, STACK), f32)
    b2 = np.zeros((STACK, 1), f32)
    for i in range(3):
        w2[:, 32 * i:32 * i + CONDS] = a["f_w2"]
        b2[32 * i:32 * i + CONDS, 0] = a["f_b2"]
    b2[CONDS] = b2[32 + CONDS] = 1.0
    consts = np.zeros((128, 512), f32)
    consts[0:TILES, 128] = TILE * np.arange(TILES)
    consts[0:TILES, 129] = TILE * np.arange(TILES) + TILE - 1
    consts[:, 130:130 + FREQS] = np.arange(1, FREQS + 1, dtype=f32) * f32(2.0 * np.pi / 16)
    for kind in (0, 4):
        consts[[CONDS, 32 + CONDS, 64 + CONDS], 260 + kind] = 1.0
    consts[:, 164:164 + STEPS] = 1000.0 + np.arange(STEPS)
    consts[:, 384:512] = np.eye(128)
    arrays = {
        "x": a["x"], "src": a["src"], "dst": a["dst"], "node_vec": np.ascontiguousarray(a["node_vec1"].reshape(TILES, TILE).T),
        "weights": np.ascontiguousarray(np.stack(mats)), "stacks": stacks, "bias_cols": np.ascontiguousarray(bias_cols),
        "f_w1": a["f_w1"], "f_b1": a["f_b1"].reshape(CONDS, 1), "f_w2": w2, "f_b2": b2,
        "consts": consts, "iota_row": np.tile(np.arange(NODES, dtype=np.float16), (HALF, 1)),
    }
    arrays = {f"in_{k}": v for k, v in arrays.items()}
    nc = bacc.Bacc("TRN2", target_bir_lowering=False, num_devices=1, dynamic_dma_scratch_size=1024)
    args = [nc.dram_tensor(k, v.shape, mybir.dt.from_np(v.dtype), kind="ExternalInput").ap() for k, v in arrays.items()]
    args.append(nc.dram_tensor("out", (NODES, DIM), F32, kind="ExternalOutput").ap())
    gnn_kernel(nc, *args)
    r = run_bass_kernel_spmd(nc, [arrays], core_ids=[0])
    return r.results[0]["out"]
```

```python
from contextlib import ExitStack

import concourse.bass as bass
from concourse import mybir

F32 = mybir.dt.float32
F32R = mybir.dt.float32r
F16 = mybir.dt.float16
BF16 = mybir.dt.bfloat16
I32 = mybir.dt.int32
ALU = mybir.AluOpType
ACT = mybir.ActivationFunctionType
AX_X = mybir.AxisListType.X

NODES = 1250
DIM = 512
EDGES = 40000
BLOCKS = 4
HEADS = 4
FREQS = 32
CONDS = 16
EPS = 1e-5
TILE = 125
TILES = NODES // TILE
PAIR = 2 * TILE
GROUPS = NODES // PAIR
KC = DIM // 128
HALF = 125
PARTS = 4
STEPS = EDGES // (PARTS * HALF)
MATS = 6
NEXT = 4
CUT = 7
STACK = 96
BANK = 512
QSCALE = float(DIM // HEADS) ** -0.5
BIG = 1e30
TWO_PI = 6.283185307179586
PI_HI = 6.28125
PI_MID = 0.0019350051879882812
PI_LO = TWO_PI - PI_HI - PI_MID
ROUND = 12582912.0
SIN_MAX = 3.1415925
START = 4
EARLY = range(4, 8)
PSLOTS = 4
TSLOTS = 4
DPAIRS = TILES // 2


def split_products(h, l, h2, l2):
    return [(h, h2), (h, l2), (l, h2)]


def gnn_kernel(nc, x, src, dst, node_vec, weights, stacks, bias_cols, f_w1, f_b1, f_w2, f_b2, consts, iota_row, out):
    ctx = ExitStack()
    with ctx:
        top = [1152]

        def size_of(shape, dt):
            size = 2 if dt in (F16, BF16) else 4
            for n in shape[1:]:
                size *= n
            return (size + 31) // 32 * 32

        def at(name, shape, dt, offset=None):
            if offset is None:
                offset, top[0] = top[0], top[0] + size_of(shape, dt)
            return nc.alloc_sbuf_tensor_at(name, shape, dt, offset=offset)

        def sem(name):
            return ctx.enter_context(nc.semaphore(name))

        x_sb = at("x_sb", [TILE, TILES, DIM], F32)
        cond_stack = at("cond_stack", [STACK, NODES], F32R)
        ident = at("ident", [128, 128], F32)
        bcol = at("bcol", [128, 3, BLOCKS, KC], F32)
        bq_scaled = at("bq_scaled", [128, BLOCKS, KC], F32)
        cond_group = at("cond_group", [STACK, PAIR], F32R)
        ones_stack = at("ones_stack", [64, TILE], F32R)
        stats = at("stats", [TILE, 2, 6], F32)
        mean_var = at("mean_var", [TILE, 2, 2], F32)
        var_eps = at("var_eps", [TILE, 2], F32)
        rstd = at("rstd", [TILE, 2], F32)
        minus_half = at("minus_half", [TILE, TILES], F32)
        row_max = at("row_max", [TILE, 8], F32)
        neg_max = at("neg_max", [TILE, 8], F32)
        den = at("den", [TILE, 8], F32)
        den_safe = at("den_safe", [TILE, 8], F32)
        rden = at("rden", [TILE, 8], F32)
        diag = at("diag", [TILE, 2, TILE], F32)
        ones_f = at("ones_f", [TILE, 128], F32)
        rbc = at("rbc", [128, PAIR], F32)
        o_f = at("o_f", [128, PAIR], F32)
        stk_a = at("stk_a", [STACK, 3, DIM], F32R)
        stk_b = at("stk_b", [STACK, DIM], F32R)

        q_at = top[0]
        q_raw = at("q_raw", [128, HEADS, NODES], F32)
        stage = [at(f"stage{i}", [128, KC, DIM], F32, q_at + 8192 * i) for i in range(2)]

        kv = top[0]
        k_hi = at("k_hi", [128, HEADS, NODES], F32R)
        kl_at = top[0]
        k_lo = at("k_lo", [128, HEADS, NODES], F32R)
        vh_at = top[0]
        v_hi = at("v_hi", [TILE, TILES, DIM], F32R)
        vl_at = top[0]
        v_lo = at("v_lo", [TILE, TILES, DIM], F32R)
        kv_end = top[0]
        m_hi = at("m_hi", [128, 2, KC, DIM], F32R, kv)
        m_lo = at("m_lo", [128, 2, KC, DIM], F32R, kl_at)
        stk_c = [at("stk_c0", [STACK, DIM], F32R, kv + 16384), at("stk_c1", [STACK, DIM], F32R, kl_at + 16384),
                 at("stk_c2", [STACK, DIM], F32R, vh_at)]
        h_raw = at("h_raw", [128, KC, PAIR], F32, vh_at + 2048)
        h_hi = at("h_hi", [128, KC, PAIR], F32R, vh_at + 6048)
        h_lo = at("h_lo", [128, KC, PAIR], F32R, vh_at + 10048)
        h_last = [at("h_last_hi", [128, KC, PAIR], F32R, vl_at), at("h_last_lo", [128, KC, PAIR], F32R, vl_at + 4000)]
        f_stats = at("f_stats", [TILE, TILES, 6], F32, vh_at + 14048)
        f_mean_var = at("f_mean_var", [TILE, TILES, 2], F32, vh_at + 14304)
        f_var = at("f_var", [TILE, TILES], F32, vh_at + 14400)
        f_rstd = at("f_rstd", [TILE, TILES], F32, vh_at + 14464)

        wh_at = top[0]
        w_hi = at("w_hi", [128, NEXT, KC, DIM], F32R)
        x0_sb = at("x0_sb", [TILE, TILES, DIM], F32, wh_at)
        wl_at = top[0]
        w_lo = at("w_lo", [128, NEXT, KC, DIM], F32R)
        pt = [at(f"pt{i}", [TILE, 2, 2, PAIR], F32R, wh_at + offset) for i, offset in enumerate((0, 4000, 13216, 17216))]
        lnc_sb = [at("lnc0_sb", [TILE, NODES], F32, wl_at + 10048), at("lnc1_sb", [TILE, NODES], F32, wh_at + 8192)]

        y_at = top[0]
        y_a = [at(name, [128, KC, PAIR], F32R) for name in ("ya_hi", "ya_lo")]
        y_sb = at("y_sb", [TILE, 2, DIM], F32)
        o_hi = at("o_hi", [128, HEADS, PAIR], F32R, y_at)
        o_lo = at("o_lo", [128, HEADS, PAIR], F32R, y_at + 4000)
        probs = [at("p0", [TILE, NODES], F32, y_at + 8000), at("p1", [TILE, NODES], F32, wl_at),
                 at("p2", [TILE, NODES], F32, wl_at + 5024), at("p3", [TILE, NODES], F32, wl_at + 15072)]
        q_hi = at("q_hi", [128, HEADS, PAIR], F32R, y_at + 13024)
        q_lo = at("q_lo", [128, HEADS, PAIR], F32R, y_at + 17024)
        y_c = [at("yc_hi", [128, KC, PAIR], F32R, y_at + 13024), at("yc_lo", [128, KC, PAIR], F32R, y_at + 17024)]
        Y = [y_a, y_c]
        assert y_at + 21024 <= 229344, y_at

        spare = [kv]

        def setup(name, shape, dt):
            spare[0] += size_of(shape, dt)
            assert spare[0] <= kv_end, name
            return at(name, shape, dt, spare[0] - size_of(shape, dt))

        onehot_src = setup("onehot_src", [HALF, PARTS, NODES], BF16)
        onehot_dst = setup("onehot_dst", [HALF, PARTS, TILE], BF16)
        iota = setup("iota", [HALF, NODES], F16)
        zeros = setup("zeros", [HALF, 512], BF16)
        ct_sb = setup("ct_sb", [TILE, NODES], F32)
        ln_c = setup("ln_c", [TILE, TILES, TILE], F32)
        no_edge = setup("no_edge", [TILE, TILES, TILE], F32)
        lnc_w = setup("lnc_w", [TILE, TILES, TILE], F32)
        edge_int = setup("edge_int", [STEPS, 2, PARTS * HALF], I32)
        edge_f = setup("edge_f", [STEPS, 2, PARTS * HALF], F32)
        src_t = setup("src_t", [HALF, PARTS, STEPS], F32)
        dst_t = setup("dst_t", [HALF, PARTS, STEPS], F32)
        cst = setup("cst", [128, 512], F32)
        step_stats = setup("step_stats", [STEPS, 2], F32)
        step_wide = setup("step_wide", [STEPS, 2, TILES], F32)
        zero10 = setup("zero10", [STEPS, TILES], F32)
        win_a = setup("win_a", [TILES, STEPS], F32)
        win_rel = setup("win_rel", [TILES, STEPS], F32)
        win_first = setup("win_first", [TILES, STEPS], F32)
        win_last = setup("win_last", [TILES, STEPS], F32)
        win = setup("win", [TILES, 8], F32)
        win_row = setup("win_row", [1, TILES, 2], F32)
        win_scan = setup("win_scan", [1, 3, TILES], F32)
        win_int = setup("win_int", [1, 3, TILES], I32)
        nv = setup("nv", [TILE, TILES], F32)
        phase = setup("phase", [TILE, TILES, FREQS], F32)
        turns = setup("turns", [TILE, TILES, FREQS], F32)
        emb = setup("emb", [TILE, TILES, 2 * FREQS], F32)
        emb_t = setup("emb_t", [2 * FREQS, NODES], F32)
        gate_z = setup("gate_z", [CONDS, NODES], F32)
        small = setup("small", [128, 2], F32)
        w1_sb = setup("w1_sb", [2 * FREQS, CONDS], F32)
        w2_sb = setup("w2_sb", [CONDS, STACK], F32)
        cond_f = setup("cond_f", [STACK, NODES], F32)
        gate_e = setup("gate_e", [CONDS, NODES], F32)
        gate_r = setup("gate_r", [CONDS, NODES], F32)
        stack_raw = at("stack_raw", [STACK, BLOCKS, DIM], F32, y_at)
        stack_r = at("stack_r", [STACK, BLOCKS, DIM], F32R, y_at + 8192)

        ps = ctx.enter_context(nc.psum_tensor("ps", [128, 8 * BANK], F32))
        T_BANK, O_BANK = 5, 7

        def bank(n, parts=128, cols=BANK, start=0):
            return ps[0:parts, n * BANK + start:n * BANK + start + cols]

        def tiles_of(n):
            return bank(n, 128, KC * TILE).rearrange("p (c n) -> p c n", c=KC)

        def chunks(start):
            cuts = [0] + [b * BANK - start for b in range(1, 9) if 0 < b * BANK - start < NODES] + [NODES]
            return list(zip(cuts, cuts[1:]))

        lnc_dram = nc.dram_tensor("lnc_dram", [TILES, TILE, NODES], F32, kind="Internal").ap()
        stk_dram = nc.dram_tensor("stk_dram", [CUT, BLOCKS + 1, STACK, DIM], F32, kind="Internal").ap()
        win_dram = nc.dram_tensor("win_dram", [TILES, 2], F32, kind="Internal").ap()

        by_pe = "mod_ps yt_ps h_ps s_ps pv_done wo_ps bc_ps m2_ps v_ps".split()
        by_dve = "y_done yl_done vl_done kl_done ttr_done xb_done ptl_done of_done xc_done hl_done rden_done".split()
        by_act = "hraw_done ct_copied noedge_ready".split()
        by_pool = "ol_done lnc_ready".split()
        s = {name: sem(name) for name in by_pe + by_dve + by_act + by_pool + (
            "consts_in nv_in edges_in w1_in x_in stack_in stack_hi stack_split stack_out "
            "phase_done reduced emb_ready emb_ps emb_t_ready z_ps z_ready e_ready e1_ready r_ready "
            "s_ready c_ps c_ready cond_ready bq_ready edge_float edge_ps edge_t_ready step_stat step_wide_ready bound_ps "
            "win_step win_out win_row_in scan_step win_ready const_ready zero_ready "
            "ct_ps cn_ps ln_ready lnc_out "
            "w_hi_done w_lo_done m_hi0_done m_hi1_done m_lo0_done m_lo1_done stk_a_in stk_b_in stk_c_in stk_d_in "
            "cg_ready stat_done mv_done vareps_done rstd_done z_done yh_done "
            "q_ps k_ps q_done kh_done vh_done "
            "qh_done ql_done negm_done exp_done tp_ps pth_done "
            "densafe_done diag_done bc_done oh_done "
            "hh_done apart x0_in f_sum f_early f_stat f_mv f_var f_rstd f_out stored").split()}
        onehot_ready = [sem(f"onehot_ready{i}") for i in range(PARTS)]
        onehot_used = [sem(f"onehot_used{i}") for i in range(PARTS)]
        stage_in = [sem(f"stage{i}_in") for i in range(2)]
        lnc_in = [sem(f"lnc{i}_in") for i in range(2)]
        block = ctx.enter_context(nc.Block())

        freqs = cst[0:TILE, 130:130 + FREQS]
        arange_p = cst[0:TILES, 164:164 + STEPS]
        win_lo, win_hi = cst[0:TILES, 128:129], cst[0:TILES, 129:130]
        idn = cst[:, 384:512]

        def tile_of(buffer, t):
            return buffer[:, bass.ds(t, 1), :].rearrange("p a d -> p (a d)")

        def tile_of_dram(buffer, t):
            return buffer[bass.ds(t, 1)].rearrange("a p d -> (a p) d")

        def wait_apart(engine, semaphore, value):
            engine.wait_ge(semaphore, value)
            engine.sem_inc(s["apart"], 1)

        def start_counts(engine, semaphores):
            for semaphore in semaphores:
                engine.sem_inc(semaphore, START)

        @block.sync
        def _(sp):
            sp.sem_inc(s["lnc_out"], 16)
            sp.sem_inc(s["stack_out"], 16)
            sp.dma_start(cst[:], consts).then_inc(s["consts_in"], 16)
            sp.dma_start(edge_int[:, 0], src.rearrange("(p j) -> p j", p=STEPS)).then_inc(s["edges_in"], 16)
            sp.dma_start(edge_int[:, 1], dst.rearrange("(p j) -> p j", p=STEPS)).then_inc(s["edges_in"], 16)
            sp.dma_start(nv[:], node_vec).then_inc(s["nv_in"], 16)
            sp.dma_start(iota[:], iota_row).then_inc(s["consts_in"], 16)
            sp.dma_start(w1_sb[:], f_w1).then_inc(s["w1_in"], 16)
            sp.dma_start(w2_sb[:], f_w2).then_inc(s["w1_in"], 16)
            sp.dma_start(small[0:CONDS, 0:1], f_b1).then_inc(s["w1_in"], 16)
            sp.dma_start(small[0:STACK, 1:2], f_b2).then_inc(s["w1_in"], 16)
            sp.dma_start(bcol[:].rearrange("p a b c -> p (a b c)"), bias_cols).then_inc(s["w1_in"], 16)
            sp.wait_ge(s["win_step"], 7)
            sp.dma_start(win_dram, win[:, 4:6]).then_inc(s["win_out"], 16)
            sp.wait_ge(s["win_out"], 16)
            sp.dma_start(win_row[:].rearrange("o t c -> o (t c)"),
                         win_dram.rearrange("t c -> (t c)").rearrange("(o n) -> o n", o=1)).then_inc(s["win_row_in"], 16)
            for n in range(NEXT):
                if n >= 2:
                    sp.wait_ge(s["w_lo_done"], n - 1)
                sp.dma_start(stage[n % 2][:].rearrange("p c d -> p (c d)"), weights[n]).then_inc(stage_in[n % 2], 16)
            sp.dma_start(x_sb[:], x.rearrange("(t p) d -> p t d", p=TILE)).then_inc(s["x_in"], 16)

            def store_counts(t):
                sp.wait_ge(s["lnc_ready"], START + t + 1)
                sp.dma_start(lnc_dram[:, :, bass.ds(t * TILE, TILE)].rearrange("a p d -> p a d"),
                             lnc_w[:]).then_inc(s["lnc_out"], 16)

            with sp.Fori(0, CUT) as t:
                sp.wait_ge(s["stack_out"], 16 * (2 * t + 1))
                for b in range(3):
                    sp.dma_start(stack_raw[32 * b:32 * b + 32, :, :],
                                 stacks[bass.ds(t, 1)].rearrange("a b r d -> (a r) b d")).then_inc(s["stack_in"], 16)
                sp.wait_ge(s["stack_split"], t + 1)
                sp.dma_start(stk_dram[bass.ds(t, 1), 0:BLOCKS].rearrange("a b r d -> (a r) b d"),
                             stack_r[:].bitcast(F32)).then_inc(s["stack_out"], 16)
                sp.dma_start(stk_dram[bass.ds(t, 1), BLOCKS].rearrange("a r d -> (a r) d"),
                             stack_r[:, 0].bitcast(F32)).then_inc(s["stack_out"], 16)
                store_counts(t)
            sp.wait_ge(s["stack_out"], 16 * (2 * CUT + 1))
            sp.dma_start(stk_a[:].bitcast(F32), stk_dram[0:3, 0].rearrange("k r d -> r k d")).then_inc(s["stk_a_in"], 16)
            with sp.Fori(CUT, TILES) as t:
                store_counts(t)
            sp.wait_ge(s["lnc_out"], 16 * (TILES + 1))

            with sp.Fori(0, BLOCKS) as blk:
                sp.wait_ge(s["wo_ps"], START + 2 * GROUPS * blk)
                sp.dma_start(stk_b[:].bitcast(F32), stk_dram[3, bass.ds(blk, 1)].rearrange("a r d -> (a r) d")).then_inc(s["stk_b_in"], 16)
                wait_apart(sp, s["k_ps"], 2 * GROUPS * (blk + 1))
                with sp.Fori(0, GROUPS) as g:
                    for j in range(2):
                        sp.wait_ge(s["ttr_done"], START + 8 * (blk * GROUPS + g) + j - 1)
                        sp.dma_start(lnc_sb[j][:], tile_of_dram(lnc_dram, 2 * g + j)).then_inc(lnc_in[j], 16)
                wait_apart(sp, s["w_lo_done"], NEXT * (blk + 1))
                sp.wait_ge(s["ql_done"], HEADS * GROUPS * (blk + 1))
                for n in range(2):
                    sp.dma_start(stage[n][:].rearrange("p c d -> p (c d)"),
                                 weights[bass.ds(MATS * blk + NEXT + n, 1)].rearrange("a p n -> (a p) n")).then_inc(stage_in[n], 16)
                sp.wait_ge(s["s_ps"], START + 8 * GROUPS * (blk + 1))
                for k in range(2):
                    sp.dma_start(stk_c[k][:].bitcast(F32), stk_dram[4 + k, bass.ds(blk, 1)].rearrange("a r d -> (a r) d")).then_inc(s["stk_c_in"], 16)
                sp.wait_ge(s["wo_ps"], START + 2 * GROUPS * (blk + 1))
                sp.dma_start(stk_c[2][:].bitcast(F32), stk_dram[6, bass.ds(blk, 1)].rearrange("a r d -> (a r) d")).then_inc(s["stk_d_in"], 16)
                sp.dma_start(stk_a[:].bitcast(F32), stk_dram[0:3, bass.ds(blk + 1, 1)].rearrange("k a r d -> (a r) k d")).then_inc(s["stk_a_in"], 16)
                for n in range(NEXT):
                    if n == 0:
                        sp.wait_ge(s["m_lo0_done"], blk + 1)
                    elif n == 1:
                        sp.wait_ge(s["m_lo1_done"], blk + 1)
                    else:
                        wait_apart(sp, s["w_lo_done"], NEXT * (blk + 1) + n - 1)
                    sp.dma_start(stage[n % 2][:].rearrange("p c d -> p (c d)"),
                                 weights[bass.ds(MATS * (blk + 1) + n, 1)].rearrange("a p n -> (a p) n")).then_inc(stage_in[n % 2], 16)
            sp.wait_ge(s["w_lo_done"], NEXT * (BLOCKS + 1))
            sp.dma_start(x0_sb[:], x.rearrange("(t p) d -> p t d", p=TILE)).then_inc(s["x0_in"], 16)
            for t in range(TILES):
                sp.wait_ge(s["f_out"], t + 1)
                sp.dma_start(out[t * TILE:(t + 1) * TILE, :], x_sb[:, t, :]).then_inc(s["stored"], 16)
            sp.wait_ge(s["stored"], 16 * TILES)

        @block.tensor
        def _(pe):
            start_counts(pe, [s[name] for name in by_pe] + onehot_used)
            pe.wait_ge(s["consts_in"], 32)
            pe.wait_ge(s["edge_float"], 2)
            for e in range(2):
                for part in range(PARTS):
                    mm = pe.transpose(bank(3 + e, HALF, STEPS, STEPS * part), edge_f[:, e, HALF * part:HALF * part + HALF],
                                      idn[0:STEPS, 0:STEPS])
            mm.then_inc(s["edge_ps"], 1)
            pe.wait_ge(s["step_wide_ready"], 2)
            for c in range(2):
                mm = pe.matmul(bank(6, TILES, STEPS, STEPS * c), step_wide[:, c, :], idn[0:STEPS, 0:STEPS], start=True, stop=True)
            mm.then_inc(s["bound_ps"], 1)
            pe.wait_ge(s["emb_ready"], 2)
            for t in range(TILES):
                mm = pe.transpose(bank(t // 4, 2 * FREQS, TILE, TILE * (t % 4)), emb[:, t, :], idn[0:TILE, 0:TILE])
            mm.then_inc(s["emb_ps"], 1)
            pe.wait_ge(s["w1_in"], 80)
            pe.wait_ge(s["emb_t_ready"], 3)
            pe.wait_ge(s["edge_t_ready"], 2)
            for a, b in chunks(0):
                mm = pe.matmul(ps[0:CONDS, 3 * BANK + a:3 * BANK + b], w1_sb[:], emb_t[:, a:b], start=True, stop=True)
            mm.then_inc(s["z_ps"], 1)
            pe.wait_ge(s["zero_ready"], 1)
            pe.wait_ge(s["win_ready"], 3)
            def turn_counts(t):
                pe.wait_ge(s["noedge_ready"], START + t)
                for i in range(TILES):
                    mm = pe.transpose(bank(3 + i // 4, TILE, TILE, TILE * (i % 4)), ct_sb[:, TILE * i:TILE * i + TILE],
                                      idn[0:TILE, 0:TILE])
                mm.then_inc(s["cn_ps"], 1)

            def window(t, first=False, read=False):
                length = pe.value_load(win_int[0:1, 1, bass.ds(t, 1)], min_val=1, max_val=STEPS)
                base = pe.value_load(win_int[0:1, 2, bass.ds(t, 1)], min_val=0, max_val=STEPS * TILES)
                pe.wait_ge(s["ct_copied"], START + t)
                for a, b in chunks(0):
                    pe.matmul(ps[0:TILE, a:b], zeros[:, 0:TILE], zeros[:, 0:b - a], start=True, stop=False)
                if read:
                    pe.wait_ge(s["c_ready"], 1)
                if not first:
                    turn_counts(t - 1)
                with pe.Fori(0, length) as k:
                    for part in range(PARTS):
                        pe.wait_ge(onehot_ready[part], base + k + 1)
                        for a, b in chunks(0):
                            mm = pe.matmul(ps[0:TILE, a:b], onehot_dst[:, part, :], onehot_src[:, part, a:b],
                                           start=False, stop=False)
                        mm.then_inc(onehot_used[part], 1)
                for a, b in chunks(0):
                    mm = pe.matmul(ps[0:TILE, a:b], zeros[:, 0:TILE], zeros[:, 0:b - a], start=False, stop=True)
                mm.then_inc(s["ct_ps"], 1)

            window(0, first=True)
            with pe.Fori(1, CUT) as t:
                window(t)
            pe.wait_ge(s["s_ready"], 1)
            pe.wait_ge(s["noedge_ready"], START + CUT - 1)
            for a, b in chunks(0):
                mm = pe.matmul(ps[0:STACK, 3 * BANK + a:3 * BANK + b], w2_sb[:], gate_r[:, a:b], start=True, stop=True)
            mm.then_inc(s["c_ps"], 1)
            window(CUT, read=True)
            with pe.Fori(CUT + 1, TILES) as t:
                window(t)
            pe.wait_ge(s["ct_copied"], START + TILES)
            turn_counts(TILES - 1)

            pe.wait_ge(s["cond_ready"], 2)
            pe.wait_ge(s["noedge_ready"], START + TILES)

            def modulate(n, scale, bias):
                pe.wait_ge(s["cg_ready"], n + 1)
                for j in range(2):
                    pe.wait_ge(s["yl_done"], START + 2 * n + j - 1)
                    pe.matmul(bank(2 * j, TILE), cond_group[:, TILE * j:TILE * j + TILE], scale, start=True, stop=True)
                    pe.matmul(bank(2 * j + 1, TILE), cond_group[:, TILE * j:TILE * j + TILE], bias,
                              start=True, stop=True).then_inc(s["mod_ps"], 1)

            def turn_rows(n):
                for j in range(2):
                    pe.wait_ge(s["y_done"], START + 2 * n + j + 1)
                    for c in range(KC):
                        mm = pe.transpose(bank(2 * j, 128, TILE, TILE * c), y_sb[:, j, 128 * c:128 * c + 128], ident[0:TILE, 0:TILE])
                    mm.then_inc(s["yt_ps"], 1)

            def normalised(n):
                pe.wait_ge(s["yh_done"], 2 * n + 2)
                pe.wait_ge(s["yl_done"], START + 2 * n + 2)

            def features(out_bank, col, wh, wl, y, f):
                steps = [(a[:, c, 128 * f:128 * f + 128], b[:, c, :]) for a, b in split_products(wh, wl, *y) for c in range(KC)]
                for i, (a, b) in enumerate(steps):
                    mm = pe.matmul(bank(out_bank, 128, PAIR, col), a, b, start=i == 0, stop=i == len(steps) - 1)
                return mm

            def rows(out_bank, h, l, j, wh, wl, bias):
                pe.matmul(bank(out_bank, TILE), ones_stack[:], bias, start=True, stop=False)
                steps = [(a[:, c, TILE * j:TILE * j + TILE], b[:, c, :]) for a, b in split_products(h, l, wh, wl) for c in range(KC)]
                for i, (a, b) in enumerate(steps):
                    mm = pe.matmul(bank(out_bank, TILE), a, b, start=False, stop=i == len(steps) - 1)
                return mm

            pe.wait_ge(s["stk_a_in"], 16)
            modulate(0, stk_a[:, 0, :], stk_a[:, 1, :])
            turn_rows(0)

            with pe.Fori(0, BLOCKS) as blk:
                it0 = blk * GROUPS
                def queries(y, first_bank):
                    for i in range(2):
                        for f in (2 * i, 2 * i + 1):
                            mm = features(first_bank + i, PAIR * (f % 2), w_hi[:, 0], w_lo[:, 0], y, f)
                        mm.then_inc(s["q_ps"], 1)

                def keys(y, first_bank):
                    for i in range(2):
                        for f in (2 * i, 2 * i + 1):
                            mm = features(first_bank + i, PAIR * (f % 2), w_hi[:, 1], w_lo[:, 1], y, f)
                        mm.then_inc(s["k_ps"], 1)

                def values(y, out_bank, j):
                    mm = rows(out_bank, *y, j, w_hi[:, 2], w_lo[:, 2], stk_a[0:64, 2, :])
                    mm.then_inc(s["v_ps"], 1)

                def project_even(g, y):
                    it = blk * GROUPS + g
                    n = 2 * GROUPS * blk + g
                    modulate(n + 1, stk_a[:, 0, :], stk_a[:, 1, :])
                    normalised(n)
                    queries(y, 4)
                    pe.wait_ge(s["vl_done"], START + 2 * it)
                    pe.wait_ge(s["xc_done"], START + 2 * it0)
                    keys(y, 6)
                    turn_rows(n + 1)
                    for j in range(2):
                        pe.wait_ge(s["q_done"], 2 * it + j + 1)
                        values(y, 4 + j, j)

                def project_odd(g, y):
                    it = blk * GROUPS + g
                    n = 2 * GROUPS * blk + g
                    modulate(n + 1, stk_a[:, 0, :], stk_a[:, 1, :])
                    normalised(n)
                    pe.wait_ge(s["kl_done"], START + 2 * it)
                    keys(y, 6)
                    pe.wait_ge(s["vl_done"], START + 2 * it)
                    queries(y, 4)
                    turn_rows(n + 1)
                    for j in range(2):
                        pe.wait_ge(s["kl_done"], START + 2 * it + j + 1)
                        values(y, 6 + j, j)

                pe.wait_ge(s["hraw_done"], START + 2 * it0)
                pe.wait_ge(s["w_hi_done"], NEXT * (blk + 1))
                wait_apart(pe, s["w_lo_done"], NEXT * (blk + 1))
                with pe.Fori(0, GROUPS // 2) as i:
                    project_even(2 * i, Y[0])
                    project_odd(2 * i + 1, Y[1])

                def scores(it, h, j, i):
                    if i < 2:
                        pe.wait_ge(s["ttr_done"], START + 8 * it + 2 * h + j - 1)
                    else:
                        pe.wait_ge(s["ttr_done"], START + 8 * it + 2 * h + j)
                    lo, hi = (chunks(0), chunks(NODES)[1:] + chunks(NODES)[:1])[j][i]
                    for part, (a, b) in enumerate(split_products(q_hi, q_lo, k_hi, k_lo)):
                        mm = pe.matmul(ps[0:TILE, NODES * j + lo:NODES * j + hi], a[:, h, TILE * j:TILE * j + TILE],
                                       b[:, h, lo:hi], start=part == 0, stop=part == 2)
                    if i == 2:
                        mm.then_inc(s["s_ps"], 1)

                def turn(it, h, dp):
                    n = 5 * h + dp
                    if dp == 0:
                        pe.wait_ge(s["exp_done"], 8 * it + 2 * h + 2)
                    pe.wait_ge(s["ptl_done"], START + 5 * HEADS * it + n - 1)
                    for d in (2 * dp, 2 * dp + 1):
                        for j in range(2):
                            mm = pe.transpose(bank(T_BANK + n % 2, TILE, TILE, PAIR * (d % 2) + TILE * j),
                                              probs[(2 * h + j) % PSLOTS][:, TILE * d:TILE * d + TILE], ident[0:TILE, 0:TILE])
                    mm.then_inc(s["tp_ps"], 1)

                def weigh(it, h, dp):
                    n = 5 * h + dp
                    if dp == 0:
                        pe.wait_ge(s["of_done"], START + HEADS * it + h)
                    pe.wait_ge(s["ptl_done"], START + 5 * HEADS * it + n + 1)
                    steps = [(a[:, 2 * dp + e, 128 * h:128 * h + 128], pt[n % TSLOTS][:, w, e, :])
                             for e in range(2) for a, w in ((v_hi, 0), (v_hi, 1), (v_lo, 0))]
                    for i, (a, b) in enumerate(steps):
                        mm = pe.matmul(bank(O_BANK, 128, PAIR), a, b, start=dp == 0 and i == 0,
                                       stop=dp == DPAIRS - 1 and i == len(steps) - 1)
                    mm.then_inc(s["pv_done"], 1)

                def spread(it, h):
                    pe.wait_ge(s["diag_done"], HEADS * it + h + 1)
                    for j in range(2):
                        mm = pe.matmul(bank(O_BANK, 128, TILE, PAIR + TILE * j), ones_f[:], diag[:, j, :], start=True, stop=True)
                    mm.then_inc(s["bc_ps"], 1)

                def output(it, out_bank, j):
                    pe.wait_ge(s["oh_done"], HEADS * (it + 1))
                    pe.wait_ge(s["ol_done"], START + HEADS * (it + 1))
                    mm = rows(out_bank, o_hi, o_lo, j, w_hi[:, 3], w_lo[:, 3], stk_b[0:64, :])
                    mm.then_inc(s["wo_ps"], 1)

                def attend(g, first, last):
                    it = blk * GROUPS + g
                    for h in range(HEADS):
                        before = (it, h - 1) if h else None if first else (it - 1, HEADS - 1)
                        nxt = (it, h + 1) if h + 1 < HEADS else None if last else (it + 1, 0)
                        if nxt:
                            pe.wait_ge(s["ql_done"], HEADS * nxt[0] + nxt[1] + 1)
                            for i in range(3):
                                scores(*nxt, 0, i)
                        if before:
                            weigh(*before, 3)
                        if h == 0 and first:
                            pe.wait_ge(s["vl_done"], START + 2 * GROUPS * (blk + 1) - 1)
                        if h == 1 and not first:
                            pe.wait_ge(s["xb_done"], START + 2 * it)
                        turn(it, h, 0)
                        if before:
                            weigh(*before, 4)
                            spread(*before)
                        if nxt:
                            for i in range(2):
                                scores(*nxt, 1, i)
                        if h == 0 and first:
                            pe.wait_ge(s["vl_done"], START + 2 * GROUPS * (blk + 1))
                        turn(it, h, 1)
                        if nxt:
                            scores(*nxt, 1, 2)
                        elif last:
                            pe.wait_ge(s["stk_c_in"], 32 * (blk + 1))
                            pe.wait_ge(s["ttr_done"], START + 8 * GROUPS * (blk + 1))
                            modulate(GROUPS * (2 * blk + 1), stk_c[0][:], stk_c[1][:])
                        turn(it, h, 2)
                        weigh(it, h, 0)
                        turn(it, h, 3)
                        if h == 0 and not first:
                            pe.wait_ge(s["ptl_done"], START + 5 * HEADS * it + 3)
                            output(it - 1, T_BANK, 0)
                        weigh(it, h, 1)
                        if h == 0 and not first:
                            pe.wait_ge(s["xb_done"], START + 2 * it - 1)
                        turn(it, h, 4)
                        weigh(it, h, 2)
                        if h == 0 and not first:
                            pe.wait_ge(s["ptl_done"], START + 5 * HEADS * it + 4)
                            output(it - 1, T_BANK + 1, 1)
                    if last:
                        weigh(it, HEADS - 1, 3)
                        weigh(it, HEADS - 1, 4)
                        spread(it, HEADS - 1)

                it = it0 + GROUPS - 1
                normalised(2 * GROUPS * blk + GROUPS - 1)
                pe.wait_ge(s["q_done"], 2 * it)
                keys(Y[0], 4)
                pe.wait_ge(s["vl_done"], START + 2 * it)
                queries(Y[0], 6)
                pe.wait_ge(s["kh_done"], 2 * GROUPS * (blk + 1))
                pe.wait_ge(s["kl_done"], START + 2 * GROUPS * (blk + 1))
                pe.wait_ge(s["ql_done"], HEADS * it0 + 1)
                for i in range(3):
                    scores(it0, 0, 0, i)
                for i in range(3):
                    scores(it0, 0, 1, i)
                for j in range(2):
                    pe.wait_ge(s["q_done"], 2 * GROUPS * (blk + 1))
                    values(Y[0], 5 + j, j)
                attend(0, True, False)
                wait_apart(pe, s["stk_b_in"], 16 * (blk + 1))
                with pe.Fori(1, GROUPS - 1) as g:
                    attend(g, False, False)
                attend(GROUPS - 1, False, True)
                turn_rows(GROUPS * (2 * blk + 1))
                for j in range(2):
                    output(it0 + GROUPS - 1, 6 + j, j)

                pe.wait_ge(s["m_hi0_done"], blk + 1)
                pe.wait_ge(s["m_lo0_done"], blk + 1)

                def hidden(g):
                    it = blk * GROUPS + g
                    normalised(GROUPS * (2 * blk + 1) + g)
                    pe.wait_ge(s["hraw_done"], START + 2 * it)
                    for i in range(2):
                        for f in (2 * i, 2 * i + 1):
                            mm = features(4 + i, PAIR * (f % 2), m_hi[:, 0], m_lo[:, 0], y_c, f)
                        mm.then_inc(s["h_ps"], 1)

                def contract(g, h_hi=h_hi, h_lo=h_lo):
                    it = blk * GROUPS + g
                    pe.wait_ge(s["hh_done"], it + 1)
                    pe.wait_ge(s["hl_done"], START + it + 1)
                    for j in range(2):
                        pe.wait_ge(s["xc_done"], START + 2 * it + j - 1)
                        mm = rows(6 + j, h_hi, h_lo, j, m_hi[:, 1], m_lo[:, 1], stk_c[2][0:64, :])
                        mm.then_inc(s["m2_ps"], 1)

                def mlp(g, first, last):
                    n = GROUPS * (2 * blk + 1) + g + 1
                    if last:
                        pe.wait_ge(s["stk_a_in"], 16 * (blk + 2))
                        modulate(n, stk_a[:, 0, :], stk_a[:, 1, :])
                    else:
                        modulate(n, stk_c[0][:], stk_c[1][:])
                    hidden(g)
                    turn_rows(n)
                    if not first:
                        contract(g - 1)

                mlp(0, True, False)
                pe.wait_ge(s["xb_done"], START + 2 * GROUPS * (blk + 1))
                pe.wait_ge(s["m_hi1_done"], blk + 1)
                pe.wait_ge(s["m_lo1_done"], blk + 1)
                wait_apart(pe, s["stk_d_in"], 16 * (blk + 1))
                with pe.Fori(1, GROUPS - 1) as g:
                    mlp(g, False, False)
                mlp(GROUPS - 1, False, True)
                contract(GROUPS - 1, *h_last)

        @block.vector
        def _(dve):
            start_counts(dve, [s[name] for name in by_dve])
            dve.memset(ones_f[:], 1.0).then_inc(s["const_ready"], 1)
            dve.memset(zero10[:], 0.0).then_inc(s["const_ready"], 1)
            dve.memset(minus_half[:], -0.5).then_inc(s["const_ready"], 1)
            dve.memset(zeros[:], 0.0).then_inc(s["zero_ready"], 1)
            dve.wait_ge(s["edges_in"], 32)
            for e in range(2):
                dve.tensor_copy(edge_f[:, e], edge_int[:, e]).then_inc(s["edge_float"], 1)
            dve.wait_ge(s["edge_float"], 2)
            dve.tensor_reduce(step_stats[:, 0:1], edge_f[:, 1, :], AX_X, ALU.min).then_inc(s["step_stat"], 1)
            dve.tensor_reduce(step_stats[:, 1:2], edge_f[:, 1, :], AX_X, ALU.max).then_inc(s["step_stat"], 1)
            dve.wait_ge(s["step_stat"], 2)
            dve.wait_ge(s["const_ready"], 3)
            for c in range(2):
                dve.tensor_scalar(step_wide[:, c, :], zero10[:], step_stats[:, c:c + 1], None, ALU.add).then_inc(s["step_wide_ready"], 1)
            dve.wait_ge(s["consts_in"], 32)
            counts = {"reduced": 0, "win_step": 0, "scan_step": 0}

            def then(name, instruction):
                counts[name] += 1
                instruction.then_inc(s[name], 1)
                dve.wait_ge(s[name], counts[name])

            dve.wait_ge(s["edge_ps"], 1)
            for e, ends in enumerate((src_t, dst_t)):
                dve.tensor_copy(ends[:], bank(3 + e, HALF, PARTS * STEPS).rearrange("p (h n) -> p h n", h=PARTS)).then_inc(s["edge_t_ready"], 1)
            dve.wait_ge(s["bound_ps"], 1)
            least, most = bank(6, TILES, STEPS), bank(6, TILES, STEPS, STEPS)
            then("scan_step", dve.tensor_scalar(win_a[:], least, win_hi, None, ALU.is_le))
            then("win_step", dve.scalar_tensor_tensor(out=win_rel[:], in0=most, scalar=win_lo, in1=win_a[:], op0=ALU.is_ge, op1=ALU.mult))
            then("scan_step", dve.scalar_tensor_tensor(out=win_first[:], in0=win_rel[:], scalar=-1000.0, in1=arange_p, op0=ALU.mult, op1=ALU.add))
            then("scan_step", dve.scalar_tensor_tensor(out=win_last[:], in0=arange_p, scalar=-999.0, in1=win_rel[:], op0=ALU.add, op1=ALU.mult))
            then("win_step", dve.tensor_reduce(win[:, 0:1], win_first[:], AX_X, ALU.min))
            then("win_step", dve.tensor_reduce(win[:, 1:2], win_last[:], AX_X, ALU.max))
            then("win_step", dve.tensor_scalar(win[:, 4:5], win[:, 0:1], float(STEPS - 1), None, ALU.min))
            then("win_step", dve.tensor_scalar(win[:, 2:3], win[:, 4:5], 1.0, None, ALU.add))
            then("win_step", dve.tensor_tensor(win[:, 3:4], win[:, 1:2], win[:, 2:3], ALU.max))
            then("win_step", dve.tensor_tensor(win[:, 5:6], win[:, 3:4], win[:, 4:5], ALU.subtract))
            dve.wait_ge(s["nv_in"], 16)
            for t in range(TILES):
                mm = dve.tensor_scalar(phase[:, t, :], freqs, nv[:, t:t + 1], None, ALU.mult)
            mm.then_inc(s["phase_done"], 1)
            dve.wait_ge(s["phase_done"], 1)
            for shift in range(2):
                part = emb[:, :, FREQS * shift:FREQS * shift + FREQS]
                then("reduced", dve.tensor_scalar(turns[:], phase[:], 1.0 / TWO_PI, 0.25 * shift, ALU.mult, ALU.add))
                then("reduced", dve.tensor_scalar(turns[:], turns[:], ROUND, None, ALU.add))
                then("reduced", dve.tensor_scalar(turns[:], turns[:], -ROUND, None, ALU.add))
                then("reduced", dve.scalar_tensor_tensor(out=part, in0=turns[:], scalar=-PI_HI, in1=phase[:], op0=ALU.mult, op1=ALU.add))
                then("reduced", dve.scalar_tensor_tensor(out=part, in0=turns[:], scalar=-PI_MID, in1=part, op0=ALU.mult, op1=ALU.add))
                then("reduced", dve.scalar_tensor_tensor(out=part, in0=turns[:], scalar=-PI_LO, in1=part, op0=ALU.mult, op1=ALU.add))
                if shift:
                    then("reduced", dve.tensor_scalar(part, part, TWO_PI / 4, None, ALU.add))
                then("reduced", dve.tensor_scalar(part, part, SIN_MAX, -SIN_MAX, ALU.min, ALU.max))
            dve.tensor_copy(ident[:], idn).then_inc(s["const_ready"], 1)
            dve.tensor_scalar(ones_stack[:], ones_f[0:64, 0:TILE], 1.0, None, ALU.mult).then_inc(s["const_ready"], 1)
            dve.wait_ge(s["w1_in"], 80)
            dve.tensor_scalar(bq_scaled[:], bcol[:, 0], QSCALE, None, ALU.mult).then_inc(s["bq_ready"], 1)
            dve.wait_ge(s["win_row_in"], 16)
            then("scan_step", dve.tensor_copy(win_scan[:, 2, :], win_row[:, :, 1]))
            then("scan_step", dve.tensor_tensor_scan(win_scan[:, 0, :], ones_f[0:1, 0:TILES], win_scan[:, 2, :], 0.0, ALU.mult, ALU.add))
            then("scan_step", dve.tensor_tensor(win_scan[:, 1, :], win_scan[:, 0, :], win_scan[:, 2, :], ALU.subtract))
            dve.tensor_copy(win_int[:, 0, :], win_row[:, :, 0]).then_inc(s["win_ready"], 1)
            dve.tensor_copy(win_int[:, 1, :], win_row[:, :, 1]).then_inc(s["win_ready"], 1)
            dve.tensor_copy(win_int[:, 2, :], win_scan[:, 1, :]).then_inc(s["win_ready"], 1)
            dve.wait_ge(s["win_ready"], 3)
            dve.wait_ge(s["edge_t_ready"], 2)
            def window(t):
                first = dve.value_load(win_int[0:1, 0, bass.ds(t, 1)], min_val=0, max_val=STEPS - 1)
                length = dve.value_load(win_int[0:1, 1, bass.ds(t, 1)], min_val=1, max_val=STEPS)
                base = dve.value_load(win_int[0:1, 2, bass.ds(t, 1)], min_val=0, max_val=STEPS * TILES)
                with dve.Fori(0, length) as k:
                    step = nc.s_assert_within(first + k, 0, STEPS - 1, skip_runtime_bounds_check_because="a window ends at the last step")
                    for part in range(PARTS):
                        wait_apart(dve, onehot_used[part], START + base + k)
                        dve.tensor_scalar(onehot_dst[:, part, :], iota[:, bass.ds(t * TILE, TILE)],
                                          dst_t[:, part, bass.ds(step, 1)], None, ALU.is_equal)
                        dve.tensor_scalar(onehot_src[:, part, :], iota[:],
                                          src_t[:, part, bass.ds(step, 1)], None, ALU.is_equal).then_inc(onehot_ready[part], 1)

            with dve.Fori(0, GROUPS) as t:
                window(t)
                wait_apart(dve, s["e1_ready"], 1)
                dve.reciprocal(gate_r[:, bass.ds(t * PAIR, PAIR)], gate_e[:, bass.ds(t * PAIR, PAIR)]).then_inc(s["r_ready"], 1)
            def statistics(n, g):
                for j in range(2):
                    dve.bn_stats(stats[:, j, :], tile_of(x_sb, 2 * g + j)).then_inc(s["stat_done"], 1)
                for j in range(2):
                    wait_apart(dve, s["stat_done"], 2 * n + j + 1)
                    dve.bn_aggr(mean_var[:, j, :], stats[:, j, :]).then_inc(s["mv_done"], 1)

            def scaled_rows(n, g):
                dve.wait_ge(s["mv_done"], 2 * n + 2)
                dve.wait_ge(s["yt_ps"], START + 2 * n)
                for j in range(2):
                    dve.wait_ge(s["mod_ps"], START + 2 * n + j + 1)
                    dve.scalar_tensor_tensor(out=y_sb[:, j, :], in0=tile_of(x_sb, 2 * g + j), scalar=mean_var[:, j, 0:1],
                                             in1=bank(2 * j, TILE), op0=ALU.subtract, op1=ALU.mult).then_inc(s["z_done"], 1)

            def shifted_rows(n):
                for j in range(2):
                    dve.wait_ge(s["z_done"], 2 * n + j + 1)
                    if j == 0:
                        dve.wait_ge(s["rstd_done"], n + 1)
                    dve.scalar_tensor_tensor(out=y_sb[:, j, :], in0=y_sb[:, j, :], scalar=rstd[:, j:j + 1],
                                             in1=bank(2 * j + 1, TILE), op0=ALU.mult, op1=ALU.add).then_inc(s["y_done"], 1)

            def modulated(n, g):
                scaled_rows(n, g)
                shifted_rows(n)

            def low_rows(n, y, j):
                dve.wait_ge(s["yh_done"], 2 * n + j + 1)
                dve.tensor_tensor(y[1][:, :, TILE * j:TILE * j + TILE], tiles_of(2 * j),
                                  y[0][:, :, TILE * j:TILE * j + TILE].bitcast(F32), ALU.subtract).then_inc(s["yl_done"], 1)

            dve.wait_ge(s["x_in"], 16)
            statistics(0, 0)
            with dve.Fori(GROUPS, TILES) as t:
                window(t)
            dve.wait_ge(s["stack_out"], 16 * (2 * CUT + 1))
            modulated(0, 0)
            for j in range(2):
                low_rows(0, Y[0], j)
            dve.wait_ge(s["lnc_out"], 16 * (TILES + 1))
            statistics(1, 1)

            with dve.Fori(0, BLOCKS) as blk:
                it0 = blk * GROUPS
                def low_keys(g, first_bank=6):
                    for i in range(2):
                        dve.wait_ge(s["kh_done"], 2 * (it0 + g) + i + 1)
                        for f in (2 * i, 2 * i + 1):
                            mm = dve.scalar_tensor_tensor(out=k_lo[:, f, bass.ds(g * PAIR, PAIR)], in0=bank(first_bank + i, 128, PAIR, PAIR * (f % 2)),
                                                          scalar=bcol[:, 1, bass.ds(blk, 1), f], in1=k_hi[:, f, bass.ds(g * PAIR, PAIR)].bitcast(F32),
                                                          op0=ALU.add, op1=ALU.subtract)
                        mm.then_inc(s["kl_done"], 1)

                def low_values(g, v_bank, j):
                    dve.wait_ge(s["vh_done"], 2 * (it0 + g) + j + 1)
                    dve.tensor_tensor(tile_of(v_lo, 2 * g + j), bank(v_bank, TILE), tile_of(v_hi, 2 * g + j).bitcast(F32),
                                      ALU.subtract).then_inc(s["vl_done"], 1)

                def high_queries(g, h):
                    dve.tensor_copy(q_hi[:, h, :], q_raw[:, h, bass.ds(g * PAIR, PAIR)]).then_inc(s["qh_done"], 1)

                def project(g, y, v_bank, last):
                    n = 2 * GROUPS * blk + g + 1
                    modulated(n, g + 1)
                    low_keys(g)
                    for j in range(2):
                        low_rows(n, y, j)
                    if not last:
                        statistics(n + 1, g + 2)
                    for j in range(2):
                        low_values(g, v_bank + j, j)

                wait_apart(dve, s["xc_done"], START + 2 * it0)
                with dve.Fori(0, GROUPS // 2 - 1) as i:
                    project(2 * i, Y[1], 4, False)
                    project(2 * i + 1, Y[0], 6, False)
                project(GROUPS - 3, Y[1], 4, False)
                project(GROUPS - 2, Y[0], 6, True)
                dve.wait_ge(s["q_done"], 2 * it0 + 2)
                for h in range(HEADS):
                    high_queries(0, h)
                low_keys(GROUPS - 1, 4)

                def masked_max(it, h, j):
                    n = 2 * h + j
                    if h == 0:
                        dve.wait_ge(lnc_in[j], 16 * (it + 1))
                    wait_apart(dve, s["s_ps"], START + 8 * it + n + 1)
                    dve.tensor_tensor_reduce(probs[n % PSLOTS][:], ps[0:TILE, NODES * j:NODES * j + NODES], lnc_sb[j][:],
                                             1.0, -BIG / 10, ALU.add, ALU.max, row_max[:, n:n + 1]).then_inc(s["ttr_done"], 1)
                    dve.wait_ge(s["ttr_done"], START + 8 * it + n + 1)
                    dve.tensor_scalar(neg_max[:, n:n + 1], row_max[:, n:n + 1], -1.0, None, ALU.mult).then_inc(s["negm_done"], 1)

                def low_probs(it, h, dp):
                    n = 5 * h + dp
                    dve.wait_ge(s["pth_done"], 5 * HEADS * it + n + 1)
                    dve.tensor_tensor(pt[n % TSLOTS][:, 1], bank(T_BANK + n % 2, TILE, 2 * PAIR).rearrange("p (e n) -> p e n", e=2),
                                      pt[n % TSLOTS][:, 0].bitcast(F32), ALU.subtract).then_inc(s["ptl_done"], 1)

                def normalise(it, h):
                    dve.wait_ge(s["bc_done"], HEADS * it + h + 1)
                    dve.wait_ge(s["ol_done"], START + HEADS * it + h)
                    dve.tensor_tensor(o_f[:], bank(O_BANK, 128, PAIR), rbc[:], ALU.mult).then_inc(s["of_done"], 1)

                def add_output(g, out_bank, j):
                    dve.wait_ge(s["wo_ps"], START + 2 * (it0 + g) + j + 1)
                    dve.tensor_tensor(tile_of(x_sb, 2 * g + j), bank(out_bank, TILE), tile_of(x_sb, 2 * g + j),
                                      ALU.add).then_inc(s["xb_done"], 1)

                def attend(g, first, last):
                    it = blk * GROUPS + g
                    for h in range(HEADS):
                        before = (it, h - 1) if h else None if first else (it - 1, HEADS - 1)
                        nxt = (it, h + 1) if h + 1 < HEADS else None if last else (it + 1, 0)
                        if nxt:
                            masked_max(*nxt, 0)
                        low_probs(it, h, 0)
                        dve.wait_ge(s["exp_done"], 8 * it + 2 * h + 2)
                        dve.tensor_scalar(den_safe[:, 2 * h:2 * h + 2], den[:, 2 * h:2 * h + 2], 1e-30, None, ALU.max).then_inc(s["densafe_done"], 1)
                        dve.wait_ge(s["densafe_done"], HEADS * it + h + 1)
                        dve.reciprocal(rden[:, 2 * h:2 * h + 2], den_safe[:, 2 * h:2 * h + 2]).then_inc(s["rden_done"], 1)
                        if before:
                            normalise(*before)
                        low_probs(it, h, 1)
                        low_probs(it, h, 2)
                        if nxt:
                            masked_max(*nxt, 1)
                        elif last:
                            scaled_rows(GROUPS * (2 * blk + 1), 0)
                        low_probs(it, h, 3)
                        if h == 0 and not first:
                            add_output(g - 1, T_BANK, 0)
                        low_probs(it, h, 4)
                        if h == 0 and not first:
                            add_output(g - 1, T_BANK + 1, 1)
                        if not last:
                            high_queries(g + 1, h)
                        elif h == HEADS - 2:
                            dve.wait_ge(s["xb_done"], START + 2 * it0 + 2)
                            statistics(GROUPS * (2 * blk + 1), 0)
                    if last:
                        shifted_rows(GROUPS * (2 * blk + 1))
                        normalise(it, HEADS - 1)

                for j in range(2):
                    masked_max(it0, 0, j)
                for j in range(2):
                    low_values(GROUPS - 1, 5 + j, j)
                attend(0, True, False)
                with dve.Fori(1, GROUPS - 1) as g:
                    attend(g, False, False)
                attend(GROUPS - 1, False, True)
                for j in range(2):
                    low_rows(GROUPS * (2 * blk + 1), y_c, j)
                dve.wait_ge(s["xb_done"], START + 2 * it0 + 4)
                statistics(GROUPS * (2 * blk + 1) + 1, 1)
                dve.wait_ge(stage_in[0], 16 * (NEXT // 2 + MATS // 2 * blk + 1))
                dve.tensor_copy(m_hi[:, 0], stage[0][:]).then_inc(s["m_hi0_done"], 1)
                dve.wait_ge(s["m_hi0_done"], blk + 1)
                dve.tensor_tensor(m_lo[:, 0], stage[0][:], m_hi[:, 0].bitcast(F32), ALU.subtract).then_inc(s["m_lo0_done"], 1)
                for j in range(2):
                    add_output(GROUPS - 1, 6 + j, j)

                dve.wait_ge(s["xb_done"], START + 2 * GROUPS * (blk + 1))

                def residual(g):
                    it = blk * GROUPS + g
                    for j in range(2):
                        dve.wait_ge(s["m2_ps"], START + 2 * it + j + 1)
                        dve.tensor_tensor(tile_of(x_sb, 2 * g + j), bank(6 + j, TILE), tile_of(x_sb, 2 * g + j),
                                          ALU.add).then_inc(s["xc_done"], 1)

                n1 = GROUPS * (2 * blk + 1)

                def split_hidden(g, h_hi=h_hi, h_lo=h_lo):
                    it = blk * GROUPS + g
                    dve.wait_ge(s["hraw_done"], START + 2 * it + 2)
                    dve.tensor_copy(h_hi[:], h_raw[:]).then_inc(s["hh_done"], 1)
                    dve.wait_ge(s["hh_done"], it + 1)
                    dve.tensor_tensor(h_lo[:], h_raw[:], h_hi[:].bitcast(F32), ALU.subtract).then_inc(s["hl_done"], 1)

                def mlp(g):
                    modulated(n1 + g + 1, g + 1)
                    for j in range(2):
                        low_rows(n1 + g + 1, y_c, j)
                    statistics(n1 + g + 2, g + 2)
                    residual(g - 1)
                    split_hidden(g)

                modulated(n1 + 1, 1)
                for j in range(2):
                    low_rows(n1 + 1, y_c, j)
                statistics(n1 + 2, 2)
                split_hidden(0)
                with dve.Fori(1, GROUPS - 2) as g:
                    mlp(g)
                modulated(n1 + GROUPS - 1, GROUPS - 1)
                for j in range(2):
                    low_rows(n1 + GROUPS - 1, y_c, j)
                dve.wait_ge(s["xc_done"], START + 2 * it0 + 2)
                statistics(n1 + GROUPS, 0)
                residual(GROUPS - 3)
                split_hidden(GROUPS - 2)
                modulated(n1 + GROUPS, 0)
                for j in range(2):
                    low_rows(n1 + GROUPS, Y[0], j)
                split_hidden(GROUPS - 1, *h_last)
                dve.wait_ge(s["xc_done"], START + 2 * it0 + 4)
                statistics(n1 + GROUPS + 1, 1)
                residual(GROUPS - 2)
                residual(GROUPS - 1)

            dve.wait_ge(s["x0_in"], 16)
            dve.wait_ge(s["xc_done"], START + 2 * GROUPS * BLOCKS)
            late = [t for t in range(TILES) if t not in EARLY]
            for t in late:
                dve.tensor_tensor(x_sb[:, t, :], x_sb[:, t, :], x0_sb[:, t, :], ALU.add).then_inc(s["f_sum"], 1)
            for i, t in enumerate(late + list(EARLY)):
                if t in EARLY:
                    dve.wait_ge(s["f_early"], t - EARLY[0] + 1)
                else:
                    dve.wait_ge(s["f_sum"], i + 1)
                dve.bn_stats(f_stats[:, t, :], x_sb[:, t, :]).then_inc(s["f_stat"], 1)
            dve.wait_ge(s["f_stat"], TILES)
            for t in range(TILES):
                dve.bn_aggr(f_mean_var[:, t, :], f_stats[:, t, :]).then_inc(s["f_mv"], 1)
            dve.wait_ge(s["f_rstd"], 1)
            for t in range(TILES):
                dve.tensor_scalar(x_sb[:, t, :], x_sb[:, t, :], f_mean_var[:, t, 0:1], f_rstd[:, t:t + 1],
                                  ALU.subtract, ALU.mult).then_inc(s["f_out"], 1)

        @block.scalar
        def _(act):
            start_counts(act, [s[name] for name in by_act])
            for shift in range(2):
                act.wait_ge(s["reduced"], (7, 15)[shift])
                part = emb[:, :, FREQS * shift:FREQS * shift + FREQS]
                act.activation(part, part, ACT.Sin).then_inc(s["emb_ready"], 1)
            act.wait_ge(s["emb_ps"], 1)
            for i, n in enumerate((4, 4, 2)):
                act.activation(emb_t[:, 4 * TILE * i:4 * TILE * i + n * TILE], bank(i, 2 * FREQS, n * TILE),
                               ACT.Copy).then_inc(s["emb_t_ready"], 1)
            act.wait_ge(s["z_ps"], 1)
            act.wait_ge(s["w1_in"], 80)
            act.activation(gate_z[:], ps[0:CONDS, 3 * BANK:3 * BANK + NODES], ACT.Identity, bias=small[0:CONDS, 0:1]).then_inc(s["z_ready"], 1)
            act.wait_ge(s["z_ready"], 1)
            act.activation(gate_e[:], gate_z[:], ACT.Exp, scale=-1.0).then_inc(s["e_ready"], 1)

            def split_hi(turn, stage_n, matrix):
                act.wait_ge(stage_in[stage_n], 16 * (turn + 1))
                act.activation(matrix, stage[stage_n][:], ACT.Copy).then_inc(s["w_hi_done"], 1)

            def copy_counts(t):
                act.wait_ge(s["ct_ps"], t + 1)
                act.activation(ct_sb[:], ps[0:TILE, 0:NODES], ACT.Copy).then_inc(s["ct_copied"], 1)

            def log_counts(t):
                act.wait_ge(s["cn_ps"], t + 1)
                act.wait_ge(s["lnc_ready"], START + t)
                for i, n in enumerate((4, 4, 2)):
                    window = bank(3 + i, TILE, n * TILE).rearrange("p (a b) -> p a b", a=n)
                    mm = act.activation(ln_c[:, 4 * i:4 * i + n, :], window, ACT.Ln, bias=float(2.0 ** -60))
                mm.then_inc(s["ln_ready"], 1)
                for i, n in enumerate((4, 4, 2)):
                    window = bank(3 + i, TILE, n * TILE).rearrange("p (a b) -> p a b", a=n)
                    mm = act.activation(no_edge[:, 4 * i:4 * i + n, :], window, ACT.Relu, bias=BIG, scale=-BIG)
                mm.then_inc(s["noedge_ready"], 1)

            def high_stacks(t):
                act.wait_ge(s["stack_in"], 48 * (t + 1))
                wait_apart(act, s["stack_out"], 16 * (2 * t + 1))
                act.activation(stack_raw[:], stack_raw[:], ACT.Identity, bias=cst[0:STACK, bass.ds(260 + t, 1)]).then_inc(s["stack_hi"], 1)
                wait_apart(act, s["stack_hi"], 2 * t + 1)
                act.activation(stack_r[:], stack_raw[:], ACT.Copy).then_inc(s["stack_hi"], 1)

            for n in range(2):
                split_hi(0, n, w_hi[:, n])
            copy_counts(0)
            for n in range(2, NEXT):
                split_hi(1, n % 2, w_hi[:, n])
            log_counts(0)
            high_stacks(0)
            with act.Fori(1, CUT - 1) as t:
                copy_counts(t)
                log_counts(t)
                high_stacks(t)
            copy_counts(CUT - 1)
            act.wait_ge(s["c_ps"], 1)
            act.activation(cond_f[:], ps[0:STACK, 3 * BANK:3 * BANK + NODES], ACT.Identity, bias=small[0:STACK, 1:2]).then_inc(s["c_ready"], 1)
            act.wait_ge(s["c_ready"], 1)
            act.activation(cond_stack[:], cond_f[:], ACT.Copy).then_inc(s["cond_ready"], 1)
            log_counts(CUT - 1)
            high_stacks(CUT - 1)
            with act.Fori(CUT, TILES) as t:
                copy_counts(t)
                log_counts(t)

            act.wait_ge(s["stack_out"], 16 * (2 * CUT + 1))
            act.wait_ge(s["bq_ready"], 1)

            def high_rows(n, y, j):
                act.wait_ge(s["yt_ps"], START + 2 * n + j + 1)
                act.activation(y[0][:, :, TILE * j:TILE * j + TILE], tiles_of(2 * j), ACT.Copy).then_inc(s["yh_done"], 1)

            for j in range(2):
                high_rows(0, Y[0], j)
            act.wait_ge(s["lnc_out"], 16 * (TILES + 1))

            with act.Fori(0, BLOCKS) as blk:
                it0 = blk * GROUPS
                def copy_queries(g, first_bank=4):
                    for i in range(2):
                        wait_apart(act, s["q_ps"], 2 * (it0 + g) + i + 1)
                        for f in (2 * i, 2 * i + 1):
                            mm = act.activation(q_raw[:, f, bass.ds(g * PAIR, PAIR)], bank(first_bank + i, 128, PAIR, PAIR * (f % 2)), ACT.Identity,
                                                bias=bq_scaled[:, bass.ds(blk, 1), f], scale=QSCALE)
                        mm.then_inc(s["q_done"], 1)

                def high_keys(g, first_bank=6):
                    for i in range(2):
                        wait_apart(act, s["k_ps"], 2 * (it0 + g) + i + 1)
                        for f in (2 * i, 2 * i + 1):
                            mm = act.activation(k_hi[:, f, bass.ds(g * PAIR, PAIR)], bank(first_bank + i, 128, PAIR, PAIR * (f % 2)), ACT.Identity,
                                                bias=bcol[:, 1, bass.ds(blk, 1), f])
                        mm.then_inc(s["kh_done"], 1)

                def high_values(g, v_bank, j):
                    act.activation(tile_of(v_hi, 2 * g + j), bank(v_bank, TILE), ACT.Copy).then_inc(s["vh_done"], 1)

                def rows_and_values(g, y, v_bank):
                    for j in range(2):
                        high_rows(2 * GROUPS * blk + g + 1, y, j)
                    for j in range(2):
                        wait_apart(act, s["v_ps"], START + 2 * (it0 + g) + j + 1)
                        high_values(g, v_bank + j, j)

                with act.Fori(0, GROUPS // 2) as i:
                    copy_queries(2 * i)
                    high_keys(2 * i)
                    rows_and_values(2 * i, Y[1], 4)
                    high_keys(2 * i + 1)
                    copy_queries(2 * i + 1)
                    rows_and_values(2 * i + 1, Y[0], 6)

                def exponent(it, h, j):
                    n = 2 * h + j
                    act.wait_ge(s["negm_done"], 8 * it + n + 1)
                    act.activation(probs[n % PSLOTS][:], probs[n % PSLOTS][:], ACT.Exp, bias=neg_max[:, n:n + 1],
                                   accum_out=den[:, n:n + 1]).then_inc(s["exp_done"], 1)

                def high_probs(it, h, dp):
                    n = 5 * h + dp
                    act.wait_ge(s["tp_ps"], 5 * HEADS * it + n + 1)
                    act.wait_ge(s["pv_done"], START + 5 * HEADS * it + n - 3)
                    act.activation(pt[n % TSLOTS][:, 0], bank(T_BANK + n % 2, TILE, 2 * PAIR).rearrange("p (e n) -> p e n", e=2),
                                   ACT.Copy).then_inc(s["pth_done"], 1)

                def copy_spread(it, h):
                    act.wait_ge(s["bc_ps"], START + HEADS * it + h + 1)
                    act.wait_ge(s["of_done"], START + HEADS * it + h)
                    act.activation(rbc[:], bank(O_BANK, 128, PAIR, PAIR), ACT.Copy).then_inc(s["bc_done"], 1)

                def high_output(it, h):
                    act.wait_ge(s["of_done"], START + HEADS * it + h + 1)
                    act.wait_ge(s["wo_ps"], START + 2 * it)
                    act.activation(o_hi[:, h, :], o_f[:], ACT.Copy).then_inc(s["oh_done"], 1)

                def attend(g, first, last):
                    it = blk * GROUPS + g
                    for h in range(HEADS):
                        before = (it, h - 1) if h else None if first else (it - 1, HEADS - 1)
                        nxt = (it, h + 1) if h + 1 < HEADS else None if last else (it + 1, 0)
                        high_probs(it, h, 0)
                        if before:
                            copy_spread(*before)
                        high_probs(it, h, 1)
                        if before:
                            high_output(*before)
                        high_probs(it, h, 2)
                        if nxt:
                            exponent(*nxt, 0)
                        else:
                            act.wait_ge(stage_in[1], 16 * (NEXT // 2 + MATS // 2 * blk + 1))
                            act.activation(m_hi[:, 1], stage[1][:], ACT.Copy).then_inc(s["m_hi1_done"], 1)
                        high_probs(it, h, 3)
                        high_probs(it, h, 4)
                        if nxt:
                            exponent(*nxt, 1)

                high_keys(GROUPS - 1, 4)
                copy_queries(GROUPS - 1, 6)
                for j in range(2):
                    exponent(it0, 0, j)
                for j in range(2):
                    act.wait_ge(s["v_ps"], START + 2 * (it0 + GROUPS - 1) + j + 1)
                    high_values(GROUPS - 1, 5 + j, j)
                attend(0, True, False)
                with act.Fori(1, GROUPS - 1) as g:
                    attend(g, False, False)
                attend(GROUPS - 1, False, True)
                n1 = GROUPS * (2 * blk + 1)
                copy_spread(it0 + GROUPS - 1, HEADS - 1)
                high_rows(n1, y_c, 0)
                high_output(it0 + GROUPS - 1, HEADS - 1)
                high_rows(n1, y_c, 1)

                for g in range(GROUPS):
                    it = blk * GROUPS + g
                    act.wait_ge(s["hl_done"], START + it)
                    for i in range(2):
                        wait_apart(act, s["h_ps"], START + 2 * it + i + 1)
                        for f in (2 * i, 2 * i + 1):
                            mm = act.activation(h_raw[:, f, :], bank(4 + i, 128, PAIR, PAIR * (f % 2)), ACT.Relu,
                                                bias=bcol[:, 2, bass.ds(blk, 1), f])
                        mm.then_inc(s["hraw_done"], 1)
                    for j in range(2):
                        high_rows(n1 + g + 1, Y[0] if g == GROUPS - 1 else y_c, j)
                    if g < NEXT:
                        split_hi(NEXT // 2 + MATS // 2 * blk + 1 + g // 2, g % 2, w_hi[:, g])

        @block.gpsimd
        def _(pool):
            start_counts(pool, [s[name] for name in by_pool])

            def split_lo(count, stage_n, low, high):
                pool.wait_ge(s["w_hi_done"], count)
                pool.tensor_tensor(low, stage[stage_n][:], high.bitcast(F32), ALU.subtract).then_inc(s["w_lo_done"], 1)

            pool.wait_ge(s["e_ready"], 1)
            pool.tensor_scalar(gate_e[:], gate_e[:], 1.0, None, ALU.add).then_inc(s["e1_ready"], 1)

            for n in range(NEXT):
                split_lo(n + 1, n % 2, w_lo[:, n], w_hi[:, n])

            def log_counts(t):
                pool.wait_ge(s["ln_ready"], t + 1)
                pool.wait_ge(s["noedge_ready"], START + t + 1)
                pool.wait_ge(s["lnc_out"], 16 * (t + 1))
                pool.tensor_tensor(lnc_w[:], ln_c[:], no_edge[:], ALU.subtract).then_inc(s["lnc_ready"], 1)

            def split_stacks(t):
                wait_apart(pool, s["lnc_ready"], START + t + 1)
                pool.wait_ge(s["stack_hi"], 2 * t + 2)
                pool.tensor_tensor(stack_r[32:64], stack_raw[32:64], stack_r[32:64].bitcast(F32), ALU.subtract).then_inc(s["stack_split"], 1)
                pool.wait_ge(s["stack_split"], t + 1)

            with pool.Fori(0, GROUPS) as t:
                log_counts(t)
                split_stacks(t)
            pool.wait_ge(s["r_ready"], GROUPS)
            pool.tensor_tensor(gate_r[:], gate_r[:], gate_z[:], ALU.mult).then_inc(s["s_ready"], 1)
            with pool.Fori(GROUPS, CUT) as t:
                log_counts(t)
                split_stacks(t)
            pool.wait_ge(s["cond_ready"], 1)
            pool.tensor_tensor(cond_stack[64:96], cond_f[64:96], cond_stack[64:96].bitcast(F32), ALU.subtract).then_inc(s["cond_ready"], 1)
            pool.wait_ge(s["cond_ready"], 2)
            pool.wait_ge(s["const_ready"], 5)

            def condition(n, g):
                wait_apart(pool, s["mod_ps"], START + 2 * n)
                pool.tensor_copy(cond_group[:], cond_stack[:, bass.ds(g * PAIR, PAIR)].bitcast(F32)).then_inc(s["cg_ready"], 1)

            def deviation(n):
                wait_apart(pool, s["mv_done"], 2 * n + 2)
                pool.tensor_scalar(var_eps[:], mean_var[:, :, 1], EPS, None, ALU.add).then_inc(s["vareps_done"], 1)
                pool.wait_ge(s["vareps_done"], n + 1)
                pool.wait_ge(s["y_done"], START + 2 * n)
                pool.tensor_tensor(rstd[:], var_eps[:], minus_half[:, 0:2], ALU.pow).then_inc(s["rstd_done"], 1)

            condition(0, 0)
            deviation(0)
            with pool.Fori(CUT, TILES) as t:
                log_counts(t)
            condition(1, 1)

            with pool.Fori(0, BLOCKS) as blk:
                it0 = blk * GROUPS
                n0 = 2 * GROUPS * blk
                n1 = n0 + GROUPS
                with pool.Fori(0, GROUPS - 2) as g:
                    deviation(n0 + g + 1)
                    condition(n0 + g + 2, g + 2)
                deviation(n1 - 1)
                condition(n1, 0)

                def low_queries(g, h):
                    pool.wait_ge(s["qh_done"], HEADS * (it0 + g) + h + 1)
                    pool.tensor_tensor(q_lo[:, h, :], q_raw[:, h, bass.ds(g * PAIR, PAIR)], q_hi[:, h, :].bitcast(F32), ALU.subtract).then_inc(s["ql_done"], 1)

                def low_output(it, h):
                    pool.wait_ge(s["oh_done"], HEADS * it + h + 1)
                    pool.wait_ge(s["wo_ps"], START + 2 * it)
                    pool.tensor_tensor(o_lo[:, h, :], o_f[:], o_hi[:, h, :].bitcast(F32), ALU.subtract).then_inc(s["ol_done"], 1)

                def attend(g, first, last):
                    it = blk * GROUPS + g
                    for h in range(HEADS):
                        before = (it, h - 1) if h else None if first else (it - 1, HEADS - 1)
                        pool.wait_ge(s["bc_ps"], START + HEADS * it + h)
                        wait_apart(pool, s["rden_done"], START + HEADS * it + h + 1)
                        for j in range(2):
                            mm = pool.tensor_scalar(diag[:, j, :], ident[0:TILE, 0:TILE], rden[:, 2 * h + j:2 * h + j + 1], None, ALU.mult)
                        mm.then_inc(s["diag_done"], 1)
                        if h == HEADS - 1 and last:
                            deviation(n1)
                        if before:
                            low_output(*before)
                        if not last:
                            low_queries(g + 1, h)

                for h in range(HEADS):
                    low_queries(0, h)
                attend(0, True, False)
                with pool.Fori(1, GROUPS - 1) as g:
                    attend(g, False, False)
                attend(GROUPS - 1, False, True)
                low_output(it0 + GROUPS - 1, HEADS - 1)
                condition(n1 + 1, 1)
                pool.wait_ge(s["m_hi1_done"], blk + 1)
                pool.tensor_tensor(m_lo[:, 1], stage[1][:], m_hi[:, 1].bitcast(F32), ALU.subtract).then_inc(s["m_lo1_done"], 1)

                for g in range(GROUPS):
                    deviation(n1 + g + 1)
                    condition(n1 + g + 2, (g + 2) % GROUPS)
                    if g < NEXT:
                        split_lo(NEXT * (blk + 1) + g + 1, g % 2, w_lo[:, g], w_hi[:, g])
            pool.wait_ge(s["x0_in"], 16)
            pool.wait_ge(s["xc_done"], START + 2 * GROUPS * (BLOCKS - 1) + EARLY[-1] + 1)
            for t in EARLY:
                pool.tensor_tensor(x_sb[:, t, :], x_sb[:, t, :], x0_sb[:, t, :], ALU.add).then_inc(s["f_early"], 1)
            pool.wait_ge(s["f_mv"], TILES)
            pool.tensor_scalar(f_var[:], f_mean_var[:, :, 1], EPS, None, ALU.add).then_inc(s["f_var"], 1)
            pool.wait_ge(s["f_var"], 1)
            pool.tensor_tensor(f_rstd[:], f_var[:], minus_half[:], ALU.pow).then_inc(s["f_rstd"], 1)


def kernel(**inputs):
    import numpy as np
    import concourse.bacc as bacc
    from concourse.bass_utils import run_bass_kernel_spmd

    a = {k.replace("L0_gnn_", ""): np.ascontiguousarray(v) for k, v in inputs.items()}
    f32 = np.float32

    def chunked(w):
        return w.reshape(KC, 128, DIM).transpose(1, 0, 2).reshape(128, KC * DIM)

    mats = [chunked(a[name][b]) for b in range(BLOCKS) for name in ("wq", "wk", "wv", "wo", "m_w1", "m_w2")]
    mats += mats[:NEXT]
    stacks = np.zeros((7, BLOCKS, 32, DIM), f32)
    for kind, (w, b) in enumerate((("s1_w", "s1_b"), ("b1_w", "b1_b"), (None, "bv"), (None, "bo"),
                                   ("s2_w", "s2_b"), ("b2_w", "b2_b"), (None, "m_b2"))):
        if w:
            stacks[kind, :, 0:CONDS] = a[w]
        stacks[kind, :, CONDS] = a[b]
    bias_cols = np.stack([a[n].reshape(BLOCKS, KC, 128) for n in ("bq", "bk", "m_b1")]).transpose(3, 0, 1, 2).reshape(128, -1)
    w2 = np.zeros((CONDS, STACK), f32)
    b2 = np.zeros((STACK, 1), f32)
    for i in range(3):
        w2[:, 32 * i:32 * i + CONDS] = a["f_w2"]
        b2[32 * i:32 * i + CONDS, 0] = a["f_b2"]
    b2[CONDS] = b2[32 + CONDS] = 1.0
    consts = np.zeros((128, 512), f32)
    consts[0:TILES, 128] = TILE * np.arange(TILES)
    consts[0:TILES, 129] = TILE * np.arange(TILES) + TILE - 1
    consts[:, 130:130 + FREQS] = np.arange(1, FREQS + 1, dtype=f32) * f32(2.0 * np.pi / 16)
    for kind in (0, 4):
        consts[[CONDS, 32 + CONDS, 64 + CONDS], 260 + kind] = 1.0
    consts[:, 164:164 + STEPS] = 1000.0 + np.arange(STEPS)
    consts[:, 384:512] = np.eye(128)
    arrays = {
        "x": a["x"], "src": a["src"], "dst": a["dst"], "node_vec": np.ascontiguousarray(a["node_vec1"].reshape(TILES, TILE).T),
        "weights": np.ascontiguousarray(np.stack(mats)), "stacks": stacks, "bias_cols": np.ascontiguousarray(bias_cols),
        "f_w1": a["f_w1"], "f_b1": a["f_b1"].reshape(CONDS, 1), "f_w2": w2, "f_b2": b2,
        "consts": consts, "iota_row": np.tile(np.arange(NODES, dtype=np.float16), (HALF, 1)),
    }
    arrays = {f"in_{k}": v for k, v in arrays.items()}
    nc = bacc.Bacc("TRN2", target_bir_lowering=False, num_devices=1, dynamic_dma_scratch_size=1024)
    args = [nc.dram_tensor(k, v.shape, mybir.dt.from_np(v.dtype), kind="ExternalInput").ap() for k, v in arrays.items()]
    args.append(nc.dram_tensor("out", (NODES, DIM), F32, kind="ExternalOutput").ap())
    gnn_kernel(nc, *args)
    r = run_bass_kernel_spmd(nc, [arrays], core_ids=[0])
    return r.results[0]["out"]
```
